# Optimizing a Trainium2 kernel written in Bass

```python
import numpy as np
import jax
import jax.numpy as jnp

def _softmax(x, axis=-1):
    return jax.nn.softmax(x, axis=axis)

def _gelu(x):
    return jax.nn.gelu(x, approximate=True)

def _silu(x):
    return jax.nn.silu(x)

def _sigmoid(x):
    return jax.nn.sigmoid(x)

def _layernorm(x, axis=-1, eps=1e-05):
    m = jnp.mean(x, axis=axis, keepdims=True)
    v = jnp.var(x, axis=axis, keepdims=True)
    return (x - m) / jnp.sqrt(v + eps)

def _scatter_add(tgt, idx, src, axis=0):
    return tgt.at[idx].add(src)

def _segment_sum(src, seg, n):
    return jax.ops.segment_sum(src, seg, n)
kernel_name = 'mk_gnn_ffn_d1_gnn_r8_1b2186'

def setup_inputs(seed: int=0):
    np.random.seed(seed)
    _w = jnp.asarray

    def _rec_inputs():
        import jax
        import jax.numpy as jnp
        _gk = jax.random.key(seed)
        x = -0.0002117 + 1 * jax.random.normal(jax.random.fold_in(_gk, 1), (6250, 256), jnp.float32)
        src = jax.random.randint(jax.random.fold_in(_gk, 2), (100000,), 0, 6250, jnp.int32)
        dst = jax.random.randint(jax.random.fold_in(_gk, 3), (100000,), 0, 6250, jnp.int32)
        _o = jnp.argsort(dst, stable=True)
        src = src[_o]
        dst = dst[_o]
        return (x, src, dst)
    x, src, dst = _rec_inputs()

    def _L0_gnn_setup():
        import jax, jax.numpy as jnp
        import numpy as np
        NEG = -1000.0
        SLOPE = 0.01
        N_NODES, N_EDGES, D_IN, D_OUT, N_HEADS = (12500, 200000, 256, 64, 4)
        key = jax.random.key(seed)
        k0, k1, k2, k3, k4 = jax.random.split(key, 5)
        h = jax.random.normal(k0, (N_NODES, D_IN), jnp.float32)
        src = jax.random.randint(k1, (N_EDGES,), 0, N_NODES)
        dst = jax.random.randint(k2, (N_EDGES,), 0, N_NODES)
        W = jax.random.normal(k3, (N_HEADS, D_IN, D_OUT), jnp.float32) / np.sqrt(D_IN)
        att = jax.random.normal(k4, (N_HEADS, 2 * D_OUT), jnp.float32) / np.sqrt(2.0 * D_OUT)
        return {'h': h, 'W': W, 'att': att, 'src': src, 'dst': dst}
    _L0_gnn_all = _L0_gnn_setup()
    _L0_gnn_in = {k: v for k, v in _L0_gnn_all.items() if k in ('W', 'att')}
    del _L0_gnn_all

    def _L0_ffn_setup():
        import jax, jax.numpy as jnp
        import numpy as np
        E = 8
        K = 2
        D = 256
        H = 512
        DOUT = 256
        EPS = 1e-05
        key = jax.random.key(seed)
        ks = jax.random.split(key, 9)
        s = 0.02
        return {'x': jax.random.normal(ks[0], (4, 1024, D), jnp.float32), 'gamma': 1.0 + 0.05 * jax.random.normal(ks[1], (D,), jnp.float32), 'beta': 0.05 * jax.random.normal(ks[2], (D,), jnp.float32), 'Wr': 0.01 * jax.random.normal(ks[3], (D, E), jnp.float32), 'br': jnp.zeros((E,), jnp.float32), 'W1': s * jax.random.normal(ks[4], (E, D, H), jnp.float32), 'b1': s * jax.random.normal(ks[5], (E, H), jnp.float32), 'W2': s * jax.random.normal(ks[6], (E, H, DOUT), jnp.float32), 'b2': s * jax.random.normal(ks[7], (E, DOUT), jnp.float32)}
    _L0_ffn_all = _L0_ffn_setup()
    _L0_ffn_in = {k: v for k, v in _L0_ffn_all.items() if k in ('gamma', 'beta', 'Wr', 'br', 'W1', 'b1', 'W2', 'b2')}
    del _L0_ffn_all
    return {'x': x, 'src': src, 'dst': dst, 'L0_gnn_W': _L0_gnn_in['W'], 'L0_gnn_att': _L0_gnn_in['att'], 'L0_ffn_gamma': _L0_ffn_in['gamma'], 'L0_ffn_beta': _L0_ffn_in['beta'], 'L0_ffn_Wr': _L0_ffn_in['Wr'], 'L0_ffn_br': _L0_ffn_in['br'], 'L0_ffn_W1': _L0_ffn_in['W1'], 'L0_ffn_b1': _L0_ffn_in['b1'], 'L0_ffn_W2': _L0_ffn_in['W2'], 'L0_ffn_b2': _L0_ffn_in['b2']}

def reference(x, src, dst, L0_gnn_W, L0_gnn_att, L0_ffn_gamma, L0_ffn_beta, L0_ffn_Wr, L0_ffn_br, L0_ffn_W1, L0_ffn_b1, L0_ffn_W2, L0_ffn_b2):
    import jax
    import jax.numpy as jnp

    def _L0_gnn_ref(h, W, att, src, dst):
        import jax, jax.numpy as jnp
        import numpy as np
        NEG = -1000.0
        SLOPE = 0.01
        N_NODES, N_EDGES, D_IN, D_OUT, N_HEADS = (12500, 200000, 256, 64, 4)
        N = h.shape[0]
        H, _, F = W.shape
        z = jnp.einsum('nd,hdf->nhf', h, W)
        a_src, a_dst = (att[:, :F], att[:, F:])
        es = jnp.einsum('nhf,hf->nh', z, a_src)
        ed = jnp.einsum('nhf,hf->nh', z, a_dst)
        e = jax.nn.leaky_relu(es[src] + ed[dst], SLOPE)
        e = jnp.where(e == 0.0, NEG, e)
        m = jax.ops.segment_max(e, dst, num_segments=N)
        m = jnp.where(jnp.isfinite(m), m, 0.0)
        ex = jnp.exp(e - m[dst])
        denom = jax.ops.segment_sum(ex, dst, num_segments=N)
        safe = jnp.where(denom[dst] > 0.0, denom[dst], 1.0)
        alpha = ex / safe
        out = jax.ops.segment_sum(alpha[:, :, None] * z[src], dst, num_segments=N)
        return out.reshape(N, H * F)

    def _L0_ffn_ref(x, gamma, beta, Wr, br, W1, b1, W2, b2):
        import jax, jax.numpy as jnp
        import numpy as np
        E = 8
        K = 2
        D = 256
        H = 512
        DOUT = 256
        EPS = 1e-05
        mu = jnp.mean(x, axis=-1, keepdims=True)
        var = jnp.mean(jnp.square(x - mu), axis=-1, keepdims=True)
        xn = (x - mu) * jax.lax.rsqrt(var + EPS) * gamma + beta
        logits = jnp.einsum('bsd,de->bse', xn, Wr) + br
        top_vals, top_idx = jax.lax.top_k(logits, K)
        w = jax.nn.softmax(top_vals, axis=-1)
        w_full = jnp.einsum('bsk,bske->bse', w, jax.nn.one_hot(top_idx, E, dtype=w.dtype))
        y = jnp.zeros(x.shape[:-1] + (DOUT,), x.dtype)
        for e in range(E):
            h = jax.nn.gelu(jnp.einsum('bsd,dh->bsh', xn, W1[e]) + b1[e], approximate=False)
            y_e = jnp.einsum('bsh,hd->bsd', h, W2[e]) + b2[e]
            y = y + y_e * w_full[..., e, None]
        return y
    x = x + _L0_gnn_ref(_layernorm(x, axis=-1), L0_gnn_W, L0_gnn_att, src, dst)
    x = x + _L0_ffn_ref(_layernorm(x, axis=-1)[None], L0_ffn_gamma, L0_ffn_beta, L0_ffn_Wr, L0_ffn_br, L0_ffn_W1, L0_ffn_b1, L0_ffn_W2, L0_ffn_b2)[0]
    return x

_drawn_inputs = setup_inputs


def setup_inputs(seed=0):
    import zlib

    import numpy as np

    out = dict(_drawn_inputs(seed))
    spreads = {'L0_ffn_br': (0.0, 0.1)}
    factors = {'L0_ffn_gamma': 6.339, 'L0_ffn_beta': 5.221, 'L0_ffn_b1': 8.0, 'L0_ffn_b2': 4.402}
    for name, (base, spread) in spreads.items():
        noise = np.random.default_rng([zlib.crc32(name.encode()), seed]).standard_normal(out[name].shape)
        drawn = base * np.exp(spread * noise) if base else spread * noise
        out[name] = jnp.asarray(drawn.astype(out[name].dtype))
    for name, factor in factors.items():
        out[name] = (out[name] * factor).astype(out[name].dtype)
    return out
```

```python
from contextlib import ExitStack

import concourse.bass as bass
from concourse import mybir

P = 128
F32 = mybir.dt.float32
I32 = mybir.dt.int32
ALU = mybir.AluOpType
ACT = mybir.ActivationFunctionType
AX_X = mybir.AxisListType.X
DVE_ONLY = (mybir.EngineType.DVE,)
PE_ONLY = (mybir.EngineType.PE,)
WHY_IN_RANGE = "the table is clamped on the chip to the buffer's range"

N_NODES, N_EDGES = 6250, 100000
D = 256
HEADS, HD = 4, 64
HB = HD + 1
ROW = HEADS * HB + HEADS
E, TOPK, HID = 8, 2, 512

NT = -(-N_NODES // P) + 1
NP = NT * P
PAD_ROW = (NT - 1) * P
ET = -(-N_EDGES // P)
PAD_DST = 8191
SB = 32
NB = -(-(ET + NT - 2) // SB)
NB += NB % 2
STEPS = NB * SB
SJ = -(-(STEPS + 1) // P)
SP = SJ * P
ST_ = TOPK * N_NODES // P + E + 1
ST_ += ST_ % 2
SLOTS = ST_ * P
BIG = 1e30
EPS = 1e-5
SLOPE, NEG = 0.01, -1000.0


class Chain:

    def __init__(self, eng, sem, base=0):
        self.eng, self.sem, self.base, self.n = eng, sem, base, 0

    def __call__(self, ins):
        self.n += 1
        ins.then_inc(self.sem, 1)
        self.eng.wait_ge(self.sem, self.base + self.n)


class Mem:

    def __init__(self, nc, ctx):
        self.nc, self.ctx = nc, ctx

    def sb(self, name, shape, dt=F32):
        return self.ctx.enter_context(self.nc.sbuf_tensor(name, shape, dt))

    def ps(self, name, shape):
        return self.ctx.enter_context(self.nc.psum_tensor(name, shape, F32))

    def sem(self, name):
        return self.ctx.enter_context(self.nc.semaphore(name))

    def sems(self, name, n):
        return [self.sem(f"{name}{i}") for i in range(n)]


def constants_phase(nc, K):
    with ExitStack() as ctx:
        m = Mem(nc, ctx)
        made = m.sem("const_made")
        block = ctx.enter_context(nc.Block())

        @block.gpsimd
        def _(pool):
            link = Chain(pool, made)
            link(nc.gpsimd.memset(K["ident"][:], 0.0))
            link(nc.gpsimd.affine_select(out=K["ident"][:], in_=K["ident"][:], compare_op=ALU.not_equal, fill=1.0,
                                         base=0, pattern=[[-1, P]], channel_multiplier=1))
            link(nc.gpsimd.iota(K["iota_row"][:], pattern=[[1, P]], base=0, channel_multiplier=0,
                                allow_small_or_imprecise_dtypes=True))
            link(nc.gpsimd.iota(K["iota_col"][:], pattern=[[0, 1]], base=0, channel_multiplier=1,
                                allow_small_or_imprecise_dtypes=True))
            link(nc.gpsimd.memset(K["ones"][:], 1.0))
            link(nc.gpsimd.memset(K["eps"][:], EPS))


def step_table_phase(nc, K, dram, src, dst):
    CH = ET // 2
    with ExitStack() as ctx:
        m = Mem(nc, ctx)
        ends = m.sb("tile_ends", [1, 2, ET], I32)
        tiles = m.sb("tile_ends_node_tile", [1, 2, ET])
        row = m.sb("cum_and_shift", [1, 2, ET])
        cb = m.sb("cum_and_shift_all", [P, 2, ET])
        one_row = m.sb("one_row", [1, ET])
        junk = m.sb("junk", [P, ET])
        iota_e = m.sb("iota_e", [P, ET])
        s_col = m.sb("s_col", [P, SJ])
        e_col, d_col, n_col = m.sb("e_col", [P, SJ]), m.sb("d_col", [P, SJ]), m.sb("n_col", [P, SJ])
        e_int, n_int = m.sb("e_int", [P, SJ], I32), m.sb("n_int", [P, SJ], I32)
        base_col = m.sb("node_base_col", [P, SJ])
        idx = m.sb("step_rows_idx", [P, 3, SJ], I32)
        rows = m.sb("step_dst", [P, 3, SJ, P], I32)
        srow = m.sb("step_src", [P, SJ, P], I32)
        same = m.sb("same_flags", [P, 2, SJ, P])
        locf, srcf = m.sb("loc_rows", [P, SJ, P]), m.sb("src_rows", [P, SJ, P])
        last_tile = m.sb("last_tile", [1, 1], I32)
        pb = m.ps("bcast_ps", [P, 4, 512])
        pt = m.ps("turn_ps", [P, 2, 512])

        in_s, row_done, bc_done, pool_c = m.sem("ends_in"), m.sem("row_done"), m.sem("bcast_done"), m.sem("pool_tbl")
        dch, e_done, tbl_out = m.sem("dve_tbl"), m.sem("e_done"), m.sem("tbl_out")
        idx_in, rows_in, flags_done, flags_out = (m.sem("idx_in"), m.sem("rows_in"), m.sem("flags_done"),
                                                  m.sem("flags_out"))
        turned, copied, rep_in = m.sem("turned"), m.sem("turn_copied"), m.sem("flags_rep_in")
        ctx.enter_context(nc.allow_non_contiguous_dma(reason="one word for an edge tile or a step, once"))
        block = ctx.enter_context(nc.Block())
        e_dram, n_dram, flag_dram = dram["step_edge_tile"], dram["step_node_tile"], dram["flags"]

        @block.sync
        def _(sp):
            for j, col in ((0, 0), (1, P - 1)):
                sp.dma_start(ends[0:1, j, :], dst[:, col:col + 1].rearrange("e o -> o e")).then_inc(in_s, 16)
            sp.wait_ge(in_s, 32)
            lp = (N_EDGES - 1) % P
            sp.dma_start(ends[0:1, 1, ET - 1:ET], dst[ET - 1:ET, lp:lp + 1]).then_inc(in_s, 16)
            sp.wait_ge(e_done, 1)
            sp.dma_start(e_dram[1:1 + SP].rearrange("(j p) -> p j", p=P), e_int[:]).then_inc(tbl_out, 16)
            for at in (0, SP + 1):
                sp.dma_start(e_dram[at:at + 1].rearrange("(a b) -> a b", b=1), last_tile[:]).then_inc(tbl_out, 16)
            sp.dma_start(n_dram[0:SP].rearrange("(j p) -> p j", p=P), n_int[:]).then_inc(tbl_out, 16)
            sp.wait_ge(tbl_out, 64)
            for o in range(2):
                sp.dma_start(idx[:, o * 2, :], e_dram[2 * o:2 * o + SP].rearrange("(j p) -> p j", p=P)
                             ).then_inc(idx_in, 16)
            sp.dma_start(K["step_node"][:], n_dram[0:STEPS + SB].rearrange("(a s) -> a s", a=1)).then_inc(idx_in, 16)
            sp.wait_ge(flags_done, 1)
            for o in range(2):
                sp.dma_start(flag_dram[o].rearrange("(j p) i -> p j i", p=P), same[:, o]).then_inc(flags_out, 16)
            sp.wait_ge(flags_out, 32)
            for o, name in enumerate(("reset_fwd", "reset_bwd")):
                for h in range(HEADS):
                    sp.dma_start(K[name][h * SB:(h + 1) * SB],
                                 flag_dram[o, 0:STEPS].rearrange("(b k) i -> k b i", k=SB)).then_inc(rep_in, 16)
            sp.wait_ge(rep_in, 16 * 2 * HEADS)
            sp.wait_ge(idx_in, 48)

        @block.gpsimd
        def _(pool):
            nc.gpsimd.iota(iota_e[:], pattern=[[1, ET]], base=0, channel_multiplier=0,
                           allow_small_or_imprecise_dtypes=True).then_inc(pool_c, 1)
            nc.gpsimd.iota(s_col[:], pattern=[[P, SJ]], base=0, channel_multiplier=1,
                           allow_small_or_imprecise_dtypes=True).then_inc(pool_c, 1)
            nc.gpsimd.memset(last_tile[:], ET - 1).then_inc(pool_c, 1)
            pool.wait_ge(idx_in, 48)
            pool.wait_ge(e_done, 1)
            for j in range(SJ):
                for o in (0, 2):
                    nc.gpsimd.indirect_dma_start(
                        out=rows[:, o, j, :], out_offset=None, in_=dst,
                        in_offset=bass.IndirectOffsetOnAxis(ap=idx[:, o, j:j + 1], axis=0)).then_inc(rows_in, 16)
                for out, table in ((rows[:, 1, j, :], dst), (srow[:, j, :], src)):
                    nc.gpsimd.indirect_dma_start(
                        out=out, out_offset=None, in_=table,
                        in_offset=bass.IndirectOffsetOnAxis(ap=e_int[:, j:j + 1], axis=0)).then_inc(rows_in, 16)

        @block.tensor
        def _(pe):
            pe.wait_ge(row_done, 1)
            for a in range(2):
                for c in range(2):
                    mm = nc.tensor.matmul(pb[:, 2 * a + c, 0:CH], K["ones"][0:1, :], row[0:1, a, c * CH:(c + 1) * CH],
                                          start=True, stop=True)
            mm.then_inc(bc_done, 1)
            pe.wait_ge(flags_done, 1)
            for n in range(2 * SJ):
                if n >= 2:
                    pe.wait_ge(copied, n - 1)
                source = (locf, srcf)[n % 2]
                nc.tensor.transpose(pt[:, n % 2, 0:P], source[:, n // 2, :], K["ident"][:]).then_inc(turned, 1)

        @block.vector
        def _(dve):
            v = nc.vector
            link = Chain(dve, dch)
            dve.wait_ge(in_s, 48)
            link(v.tensor_scalar(ends[:], ends[:], 7, None, ALU.arith_shift_right))
            link(v.tensor_copy(tiles[:], ends[:]))
            link(v.memset(one_row[:], 1.0))
            link(v.tensor_tensor(row[0:1, 1, :], tiles[0:1, 1, :], tiles[0:1, 0, :], ALU.subtract))
            link(v.tensor_scalar(row[0:1, 1, :], row[0:1, 1, :], 1.0, None, ALU.add))
            link(v.tensor_tensor_scan(row[0:1, 0, :], one_row[:], row[0:1, 1, :], 0.0, ALU.mult, ALU.add))
            link(v.tensor_tensor(row[0:1, 1, :], row[0:1, 0, :], row[0:1, 1, :], ALU.subtract))
            v.tensor_tensor(row[0:1, 1, :], row[0:1, 1, :], tiles[0:1, 0, :], ALU.subtract).then_inc(row_done, 1)
            dve.wait_ge(bc_done, 1)
            for a in range(2):
                link(v.tensor_copy(cb[:, a].rearrange("p (c x) -> p c x", c=2), pb[:, 2 * a:2 * a + 2, 0:CH]))
            dve.wait_ge(pool_c, 3)
            for j in range(SJ):
                link(v.tensor_scalar(junk[:], cb[:, 0], s_col[:, j:j + 1], 0.0, ALU.is_le, ALU.add,
                                     accum_out=e_col[:, j:j + 1]))
            link(v.tensor_scalar(e_col[:], e_col[:], float(ET - 1), None, ALU.min))
            for j in range(SJ):
                link(v.scalar_tensor_tensor(out=junk[:], in0=iota_e[:], scalar=e_col[:, j:j + 1], in1=cb[:, 1],
                                            op0=ALU.is_equal, op1=ALU.mult, accum_out=d_col[:, j:j + 1]))
            link(v.tensor_tensor(n_col[:], s_col[:], d_col[:], ALU.subtract))
            link(v.tensor_scalar(n_col[:], n_col[:], float(NT - 1), 0.0, ALU.min, ALU.max))
            link(v.tensor_scalar(base_col[:], n_col[:], float(P), None, ALU.mult))
            link(v.tensor_copy(e_int[:], e_col[:]))
            v.tensor_copy(n_int[:], n_col[:]).then_inc(e_done, 1)
            dve.wait_ge(e_done, 1)
            dve.wait_ge(rows_in, 16 * 4 * SJ)
            cur = rows[:, 1]
            link(v.tensor_tensor(same[:, 0, :, 1:P], cur[:, :, 1:P], cur[:, :, 0:P - 1], ALU.is_equal))
            link(v.tensor_tensor(same[:, 0, :, 0:1], cur[:, :, 0:1], rows[:, 0, :, P - 1:P], ALU.is_equal))
            link(v.tensor_tensor(same[:, 1, :, P - 1:0:-1], cur[:, :, 1:P], cur[:, :, 0:P - 1], ALU.is_equal))
            link(v.tensor_tensor(same[:, 1, :, 0:1], cur[:, :, P - 1:P], rows[:, 2, :, 0:1], ALU.is_equal))
            link(v.tensor_scalar(same[:], same[:], 1.0, BIG, ALU.subtract, ALU.mult))
            for j in range(SJ):
                link(v.tensor_scalar(locf[:, j, :], cur[:, j, :], base_col[:, j:j + 1], None, ALU.subtract))
            v.tensor_copy(srcf[:], srow[:]).then_inc(flags_done, 1)
            for n in range(2 * SJ):
                dve.wait_ge(turned, n + 1)
                out = (K["loc_dst"], K["src_idx"])[n % 2]
                v.tensor_copy(out[:, (n // 2) * P:(n // 2 + 1) * P], pt[:, n % 2, 0:P]).then_inc(copied, 1)


def chain_table_phase(nc, K):
    with ExitStack() as ctx:
        m = Mem(nc, ctx)
        first = m.sb("first_loc", [1, NB])
        pf = m.ps("first_ps", [P, 512])
        dch, first_done, f_bc = m.sem("dve_ch"), m.sem("first_done"), m.sem("first_bcast")
        block = ctx.enter_context(nc.Block())

        @block.tensor
        def _(pe):
            pe.wait_ge(first_done, 1)
            nc.tensor.matmul(pf[:, 0:NB], K["ones"][0:1, :], first[:], start=True, stop=True).then_inc(f_bc, 1)

        @block.vector
        def _(dve):
            v = nc.vector
            link = Chain(dve, dch)
            v.tensor_copy(first[:], K["loc_dst"][0:1, 0:STEPS].rearrange("a (b k) -> a b k", k=SB)[:, :, 0]
                          ).then_inc(first_done, 1)
            for o, name in enumerate(("reset_fwd", "reset_bwd")):
                link(v.tensor_reduce(K["whole"][:, o, :], K[name][:], AX_X, ALU.min))
            link(v.tensor_scalar(K["goes_on"][:], K["reset_fwd"][0:1, :, 0], 0.0, None, ALU.is_equal))
            dve.wait_ge(f_bc, 1)
            link(v.tensor_scalar(K["first_node"][:], pf[:, 0:NB], K["iota_col"][:, 0:1], None, ALU.is_equal))


def mean_and_rstd(nc, dve, link, stats, mean, rstd, tmp, var_ready, std_ready, n):
    v = nc.vector
    half = stats.rearrange("p t (o c) -> p t o c", o=2)
    me, mo = half[:, :, 0, 1], half[:, :, 1, 1]
    link(v.tensor_tensor(mean, me, mo, ALU.add))
    link(v.tensor_scalar(mean, mean, 0.5, None, ALU.mult))
    link(v.tensor_tensor(tmp, me, mo, ALU.subtract))
    link(v.tensor_tensor(tmp, tmp, tmp, ALU.mult))
    link(v.tensor_scalar(tmp, tmp, D / 4.0, None, ALU.mult))
    link(v.tensor_tensor(tmp, tmp, half[:, :, 0, 2], ALU.add))
    link(v.tensor_tensor(tmp, tmp, half[:, :, 1, 2], ALU.add))
    v.tensor_scalar(rstd, tmp, 1.0 / D, None, ALU.mult).then_inc(var_ready, 1)
    dve.wait_ge(std_ready, n)
    link(v.reciprocal(rstd, rstd))


def node_phase(nc, K, dram, x, W, att):
    ZC = HEADS * HD
    CHUNKS = 5
    TC = NT // CHUNKS
    with ExitStack() as ctx:
        m = Mem(nc, ctx)
        xr = m.sb("x_all", [P, NT, D])
        stats = m.sb("stats", [P, NT, 6])
        mean, rstd, tmp = m.sb("mean", [P, NT]), m.sb("rstd", [P, NT]), m.sb("ln_tmp", [P, NT])
        w_all = m.sb("w_all", [P, 2, ZC + 2 * HEADS])
        w_in = m.sb("w_in", [P, 2, HEADS, HD])
        att_in, prod = m.sb("att_in", [1, HEADS * 2 * HD]), m.sb("att_prod", [P, 2, 2, HEADS, HD])
        xn, xT = m.sb("xn", [P, 2, D]), m.sb("xT", [P, 2, 2, P])
        zrow = m.sb("zrow", [P, 2, ROW])
        t_ps, z_ps, a_ps = m.ps("t_ps", [P, 2, 512]), m.ps("z_ps", [P, 2, 512]), m.ps("a_ps", [P, 512])

        x_in, w_s, z_out = m.sems("x_in", CHUNKS), m.sem("w_in_s"), m.sems("z_out", 2)
        dch, zch, att_bc, w_ready = m.sem("dve_n"), m.sem("dve_z"), m.sem("att_bc"), m.sem("w_ready")
        stats_done, var_ready, std_ready = m.sem("stats_done"), m.sem("var_ready"), m.sem("std_ready")
        xn_free, xn_done, xt_done, xt_copied = m.sem("xn_free"), m.sem("xn_done"), m.sem("xt_done"), m.sem("xt_cp")
        z_done, z_copied, z_free = m.sem("z_done"), m.sem("z_copied"), m.sem("z_free")
        block = ctx.enter_context(nc.Block())

        @block.sync
        def _(sp):
            for c in range(CHUNKS):
                sp.dma_start(xr[:, c * TC:(c + 1) * TC, :],
                             x[c * TC * P:(c + 1) * TC * P, :].rearrange("(t p) d -> p t d", p=P)
                             ).then_inc(x_in[c], 16)
                if c == 0:
                    for h in range(HEADS):
                        sp.dma_start(w_in[:, :, h, :], W[h].rearrange("(k p) f -> p k f", p=P)).then_inc(w_s, 16)
                    sp.dma_start(att_in[:], att.rearrange("(a h) c -> a (h c)", a=1)).then_inc(w_s, 16)
            with sp.Fori(0, NT // 2) as i:
                for u in range(2):
                    sp.wait_ge(z_copied, i * 2 + (u + 1))
                    sp.dma_start(dram["z_table"][bass.ds((i * 2 + u) * P, P), :], zrow[:, u, :]
                                 ).then_inc(z_out[u], 16)
            for u in range(2):
                sp.wait_ge(z_out[u], 16 * (NT // 2))

        @block.tensor
        def _(pe):
            pe.sem_inc(xn_free, 2)
            pe.wait_ge(w_s, 16 * (HEADS + 1))
            pe.wait_ge(K["setup"], 1)
            nc.tensor.matmul(a_ps[:], K["ones"][0:1, :], att_in[:], start=True, stop=True).then_inc(att_bc, 1)
            pe.wait_ge(w_ready, 1)
            with pe.Fori(0, NT // 2) as i:
                for u in range(2):
                    pe.wait_ge(xn_done, i * 2 + (u + 1))
                    for k in range(2):
                        mm = nc.tensor.transpose(t_ps[:, u, k * P:(k + 1) * P], xn[:, u, k * P:(k + 1) * P],
                                                 K["ident"][:])
                    mm.then_inc(xt_done, 1)
                    pe.wait_ge(xt_copied, i * 2 + (u + 1))
                    pe.wait_ge(z_free, i * 2 + (u + 1))
                    for k in range(2):
                        mm = nc.tensor.matmul(z_ps[:, u, 0:ZC + 2 * HEADS], xT[:, u, k, :], w_all[:, k, :],
                                              start=(k == 0), stop=(k == 1))
                    mm.then_inc(z_done, 1)

        @block.scalar
        def _(act):
            act.wait_ge(var_ready, 1)
            nc.scalar.activation(rstd[:], rstd[:], ACT.Sqrt, bias=K["eps"][:, 0:1]).then_inc(std_ready, 1)
            with act.Fori(0, NT // 2) as i:
                for u in range(2):
                    act.wait_ge(xt_done, i * 2 + (u + 1))
                    act.wait_ge(z_free, i * 2 + (u + 1))
                    nc.scalar.copy(xT[:, u].rearrange("p k n -> p (k n)"), t_ps[:, u, 0:2 * P]).then_inc(xt_copied, 1)

        @block.vector
        def _(dve):
            v = nc.vector
            link = Chain(dve, dch)
            dve.sem_inc(z_free, 2)
            link(v.memset(zrow[:], 1.0))
            link(v.memset(K["acc"][:], 0.0))
            dve.sem_inc(K["setup"], 1)
            dve.wait_ge(att_bc, 1)
            a4 = a_ps[:].rearrange("p (h o f) -> p o h f", h=HEADS, o=2)
            for k in range(2):
                link(v.tensor_copy(w_all[:, k, 0:ZC].rearrange("p (h f) -> p h f", h=HEADS), w_in[:, k]))
                for o in range(2):
                    link(v.tensor_tensor(prod[:, k, o], w_in[:, k], a4[:, o], ALU.mult))
                    link(v.tensor_reduce(w_all[:, k, ZC + o * HEADS:ZC + (o + 1) * HEADS], prod[:, k, o], AX_X,
                                         ALU.add))
            dve.sem_inc(w_ready, 1)
            for c in range(CHUNKS):
                dve.wait_ge(x_in[c], 16)
                with dve.Fori(c * TC, (c + 1) * TC) as t:
                    v.bn_stats(stats[:, bass.ds(t, 1), :].rearrange("p a c -> p (a c)"),
                               xr[:, bass.ds(t, 1), :].rearrange("p a c -> p (a c)")).then_inc(stats_done, 1)
            dve.wait_ge(stats_done, NT)
            mean_and_rstd(nc, dve, link, stats[:], mean[:], rstd[:], tmp[:], var_ready, std_ready, 1)

            def normalise(t, u, count):
                dve.wait_ge(xt_done, count) if count is not None else None
                v.tensor_scalar(xn[:, u], xr[:, bass.ds(t, 1), :].rearrange("p a c -> p (a c)"),
                                mean[:, bass.ds(t, 1)], rstd[:, bass.ds(t, 1)],
                                ALU.subtract, ALU.mult).then_inc(xn_done, 1)

            v.tensor_scalar(xn[:, 0], xr[:, 0, :], mean[:, 0:1], rstd[:, 0:1], ALU.subtract, ALU.mult
                            ).then_inc(xn_done, 1)
            v.tensor_scalar(xn[:, 1], xr[:, 1, :], mean[:, 1:2], rstd[:, 1:2], ALU.subtract, ALU.mult
                            ).then_inc(xn_done, 1)

            def take_rows(t, u, i):
                dve.wait_ge(z_done, t + 1)
                dve.wait_ge(z_out[u], i * 16)
                v.tensor_copy(zrow[:, u, 0:HEADS * HB].rearrange("p (h f) -> p h f", h=HEADS)[:, :, 0:HD],
                              z_ps[:, u, 0:ZC].rearrange("p (h f) -> p h f", h=HEADS)).then_inc(zch, 1)
                v.tensor_copy(zrow[:, u, HEADS * HB:], z_ps[:, u, ZC:ZC + HEADS]).then_inc(zch, 1)
                v.tensor_copy(K["ed"][:, bass.ds(t, 1), :].rearrange("p a h -> p (a h)"),
                              z_ps[:, u, ZC + HEADS:ZC + 2 * HEADS]).then_inc(z_free, 1)
                dve.wait_ge(zch, t * 2 + 2)
                dve.sem_inc(z_copied, 1)

            with dve.Fori(0, NT // 2 - 1) as i:
                for u in range(2):
                    take_rows(i * 2 + u, u, i)
                    normalise(i * 2 + (u + 2), u, i * 2 + (u + 1))
            for u in range(2):
                take_rows(NT - 2 + u, u, NT // 2 - 1)
            dve.wait_ge(z_free, NT + 2)


def lasting(nc, ctx):
    m = Mem(nc, ctx)
    return {
        "ident": m.sb("ident", [P, P]), "iota_row": m.sb("iota_row", [P, P]), "iota_col": m.sb("iota_col", [P, 1]),
        "ones": m.sb("ones", [P, P]), "eps": m.sb("eps", [P, 1]), "setup": m.sem("setup"),
        "acc": m.sb("acc", [P, NT, HEADS * HB]),
    }


def graph_tables(nc, ctx):
    m = Mem(nc, ctx)
    return {
        "step_node": m.sb("step_node", [1, STEPS + SB], I32),
        "loc_dst": m.sb("loc_dst", [P, SP]),
        "src_idx": m.sb("src_idx", [P, SP], I32),
        "reset_fwd": m.sb("reset_fwd", [P, NB, P]),
        "reset_bwd": m.sb("reset_bwd", [P, NB, P]),
        "whole": m.sb("whole", [P, 2, NB]),
        "goes_on": m.sb("goes_on", [1, NB]), "first_node": m.sb("first_node", [P, NB]),
        "ed": m.sb("ed", [P, NT, HEADS]),
    }


def expert_buffers(nc, ctx):
    m = Mem(nc, ctx)
    return {
        "w1": m.sb("w1_all", [P, 2, E * HID]), "w2": m.sb("w2_all", [P, 4, E * D]),
        "b1": m.sb("b1_all", [P, E * HID]), "b2": m.sb("b2_all", [P, E * D]), "weights_in": m.sem("weights_in"),
        "tile_expert": m.sb("tile_expert", [1, ST_ + 2], I32), "slot_w": m.sb("slot_w", [ST_ + 2, P]),
        "xn_now": m.sb("xn_now", [P, 2, D]),
    }


def edge_phase(nc, K, dram):
    G4 = SB // 4
    S8 = SB // 8
    HK = HEADS * (SB + 1)
    with ExitStack() as ctx:
        m = Mem(nc, ctx)
        rows = m.sb("edge_rows", [P, 2, SB, ROW])
        onehot = m.sb("onehot", [P, 2, SB, P])
        onehot_t = m.sb("onehot_t", [P, 2, 4, P])
        idx = m.sb("edge_idx", [P, 2, SB], I32)
        sc, sc2 = m.sb("scores", [P, HEADS, SB]), m.sb("scores2", [P, HEADS, SB])
        fwd, bwd, top = m.sb("fwd", [P, P]), m.sb("bwd", [P, P]), m.sb("top", [P, P])
        ends = m.sb("chain_in", [1, 2, 2, HK])
        chain = m.sb("chain_max", [1, 2, HK])
        enter = m.sb("chain_enter", [1, 2, P])
        init = m.sb("chain_init", [P, 2])
        mx4, dl4, g4 = m.sb("mx4", [1, HEADS]), m.sb("dl4", [1, HEADS]), m.sb("g4", [1, HEADS])
        node_scale = m.sb("node_scale", [P, HEADS])
        whole_now = m.sb("whole_now", [P, 2])
        wt = m.sb("weights", [P, 2, HEADS, SB])
        y = m.sb("weighted", [P, 2, HEADS * HB])
        t_ps, ed_ps, e_ps = m.ps("oh_ps", [P, 2, 512]), m.ps("ed_ps", [P, 512]), m.ps("e_ps", [P, 512])
        small, out_ps = m.ps("small_ps", [P, 512]), m.ps("out_ps", [P, 2, 512])

        gath, rows_free, idx_c = m.sems("gathered", 2), m.sem("rows_free"), m.sem("idx_copied")
        issuing = m.sem("edge_gathers_issuing")
        oh_built, oh_free, oht_ps, oht_sb, oht_free = (m.sem("oh_built"), m.sem("oh_free"), m.sem("oht_ps"),
                                                       m.sem("oht_sb"), m.sem("oht_free"))
        ed_done, dch = m.sem("ed_done"), m.sem("dve_edge")
        sc_ready, sc_turned, ends_ready, ends_turned = (m.sem("sc_ready"), m.sem("sc_turned"), m.sem("ends_ready"),
                                                        m.sem("ends_turned"))
        chain_ready, init_done, dl_ready, g_done, enter_ready = (m.sem("chain_ready"), m.sem("init_done"), m.sem("dl_ready"),
                                                    m.sem("g_done"), m.sem("enter_ready"))
        gm_ready, gm_bc, x_ready, x_turned, w_done = (m.sem("gm_ready"), m.sem("gm_bc"), m.sem("x_ready"),
                                                      m.sem("x_turned"), m.sem("w_done"))
        y_ready, mm_done, acc_done = m.sem("y_ready"), m.sem("mm_done"), m.sem("acc_done")
        block = ctx.enter_context(nc.Block())

        def heads(ap):
            return ap.rearrange("a (h k) -> a h k", h=HEADS)

        @block.gpsimd
        def _(pool):
            pool.sem_inc(rows_free, 2)
            with pool.Fori(0, NB // 2) as i:
                for u in range(2):
                    pool.wait_ge(rows_free, i * 2 + (u + 1))
                    nc.gpsimd.tensor_copy(idx[:, u], K["src_idx"][:, bass.ds(i * (2 * SB) + u * SB, SB)]
                                          ).then_inc(idx_c, 1)
                    pool.wait_ge(idx_c, i * 2 + (u + 1))
                    pool.sem_inc(issuing, 1)
                    for k in range(SB):
                        nc.gpsimd.indirect_dma_start(
                            out=rows[:, u, k, :], out_offset=None, in_=dram["z_table"],
                            in_offset=bass.IndirectOffsetOnAxis(ap=idx[:, u, k:k + 1], axis=0)
                        ).then_inc(gath[u], 16)

        @block.tensor
        def _(pe):
            ident = K["ident"][:]
            pe.sem_inc(oht_free, 2)
            pe.sem_inc(oh_free, 2)

            def turn_onehots(b, u, groups):
                for g in groups:
                    pe.wait_ge(oh_built, b * S8 + (g // 2 + 1))
                    for q in range(4):
                        mm = nc.tensor.transpose(t_ps[:, g % 2, q * P:(q + 1) * P], onehot[:, u, g * 4 + q, :], ident)
                    mm.then_inc(oht_ps, 1)
                    if g % 2 == 0:
                        _, node = nc.values_load_multi_w_load_instructions(
                            K["step_node"][0:1, bass.ds(b * SB + g * 4, 8)], engines=PE_ONLY, min_val=0,
                            max_val=NT - 1, skip_runtime_bounds_check_because=WHY_IN_RANGE)
                    pe.wait_ge(oht_sb, b * G4 + (g + 1))
                    for q in range(4):
                        k = g * 4 + q
                        mm = nc.tensor.matmul(ed_ps[:, k * HEADS:(k + 1) * HEADS], onehot_t[:, g % 2, q, :],
                                              K["ed"][:, bass.ds(node[k % 8], 1), :].rearrange("p a h -> p (a h)"),
                                              start=True, stop=True)
                    mm.then_inc(ed_done, 1)

            turn_onehots(0, 0, range(G4))
            with pe.Fori(0, NB // 2) as i:
                for u in range(2):
                    b = i * 2 + u
                    pe.wait_ge(sc_ready, b + 1)
                    nc.tensor.transpose(e_ps[:, 0:P], sc[:].rearrange("p h k -> p (h k)"), ident).then_inc(sc_turned, 1)
                    turn_onehots(b + 1, 1 - u, range(0, 2))
                    pe.wait_ge(ends_ready, b * 2 + 2)
                    for o, col in enumerate((fwd[:, P - 1:P], bwd[:, 0:1])):
                        nc.tensor.transpose(small[0:1, 2 * o * P:(2 * o + 1) * P], col, ident)
                        mm = nc.tensor.transpose(small[0:1, (2 * o + 1) * P:(2 * o + 2) * P], whole_now[:, o:o + 1],
                                                 ident)
                    mm.then_inc(ends_turned, 1)
                    turn_onehots(b + 1, 1 - u, range(2, 6))
                    pe.wait_ge(enter_ready, b * 2 + 2)
                    for o in range(2):
                        mm = nc.tensor.matmul(small[:, o:o + 1], enter[0:1, o],
                                              K["ones"][0:1, 0:1], start=True, stop=True)
                    mm.then_inc(init_done, 1)
                    turn_onehots(b + 1, 1 - u, range(6, 8))
                    pe.wait_ge(gm_ready, b + 1)
                    nc.tensor.matmul(small[:, 0:HEADS], K["ones"][0:1, :], g4[:], start=True, stop=True
                                     ).then_inc(gm_bc, 1)
                    pe.wait_ge(x_ready, b + 1)
                    nc.tensor.transpose(e_ps[:, 0:P], top[:], ident).then_inc(x_turned, 1)
                    for k in range(SB):
                        pe.wait_ge(y_ready, b * SB + (k + 1))
                        mm = nc.tensor.matmul(out_ps[:, k % 2, 0:HEADS * HB], onehot[:, u, k, :], y[:, k % 2],
                                              start=True, stop=True)
                        mm.then_inc(mm_done, 1)

        @block.scalar
        def _(act):
            def copy_turned(b, groups):
                for g in groups:
                    act.wait_ge(oht_ps, b * G4 + (g + 1))
                    act.wait_ge(ed_done, b * G4 + (g - 1)) if not isinstance(b, int) else (
                        act.wait_ge(ed_done, g - 1) if g >= 2 else None)
                    nc.scalar.copy(onehot_t[:, g % 2].rearrange("p q n -> p (q n)"), t_ps[:, g % 2, :]
                                   ).then_inc(oht_sb, 1)

            copy_turned(0, range(G4))
            with act.Fori(0, NB // 2) as i:
                for u in range(2):
                    b = i * 2 + u
                    copy_turned(b + 1, range(0, 6))
                    act.wait_ge(dl_ready, b + 1)
                    nc.scalar.activation(g4[:], dl4[:], ACT.Exp).then_inc(g_done, 1)
                    copy_turned(b + 1, range(6, 8))
                    act.wait_ge(x_turned, b + 1)
                    nc.scalar.activation(wt[:, u].rearrange("p h k -> p (h k)"), e_ps[:, 0:P], ACT.Exp
                                         ).then_inc(w_done, 1)

        @block.vector
        def _(dve):
            v = nc.vector
            PER = 26

            def build_onehots(b, u, groups):
                for g in groups:
                    loc = K["loc_dst"][:, bass.ds(b * SB + g * 8, 8)]
                    v.tensor_tensor(onehot[:, u, g * 8:(g + 1) * 8, :],
                                    loc.unsqueeze(2).broadcast_to([P, 8, P]),
                                    K["iota_row"][:].unsqueeze(1).broadcast_to([P, 8, P]),
                                    ALU.is_equal).then_inc(oh_built, 1)

            start = Chain(dve, dch)
            start(v.memset(ends[:], -BIG))
            build_onehots(0, 0, range(S8))
            with dve.Fori(0, NB // 2) as i:
                for u in range(2):
                    b = i * 2 + u
                    link = Chain(dve, dch, i * (2 * PER) + (u * PER + 1))
                    link(v.tensor_copy(whole_now[:], K["whole"][:, :, bass.ds(b, 1)].rearrange("p o b -> p (o b)")))
                    dve.wait_ge(ed_done, b * G4 + G4)
                    dve.wait_ge(gath[u], i * (16 * SB) + 16 * SB)
                    es = rows[:, u, :, HEADS * HB:ROW].rearrange("p k h -> p h k")
                    link(v.tensor_tensor(sc2[:], ed_ps[:, 0:P].rearrange("p (k h) -> p h k", h=HEADS), es, ALU.add))
                    link(v.scalar_tensor_tensor(out=sc[:], in0=sc2[:], scalar=SLOPE, in1=sc2[:], op0=ALU.mult,
                                                op1=ALU.max))
                    link(v.tensor_scalar(sc2[:], sc[:], 0.0, NEG, ALU.is_equal, ALU.mult))
                    v.tensor_tensor(sc[:], sc[:], sc2[:], ALU.add).then_inc(sc_ready, 1)
                    build_onehots(b + 1, 1 - u, range(0, 1))
                    dve.wait_ge(sc_turned, b + 1)
                    rf = K["reset_fwd"][:, bass.ds(b, 1), :].rearrange("p a i -> p (a i)")
                    rb = K["reset_bwd"][:, bass.ds(b, 1), :].rearrange("p a i -> p (a i)")
                    v.tensor_tensor_scan(fwd[:], rf, e_ps[:, 0:P], -BIG, ALU.add, ALU.max).then_inc(ends_ready, 1)
                    v.tensor_tensor_scan(bwd[:, ::-1], rb, e_ps[:, 0:P][:, ::-1],
                                         -BIG, ALU.add, ALU.max).then_inc(ends_ready, 1)
                    build_onehots(b + 1, 1 - u, range(1, 3))
                    dve.wait_ge(ends_turned, b + 1)
                    for o in range(2):
                        link(v.tensor_copy(
                            ends[0:1, o].rearrange("a x (h k) -> a (x h) k", h=HEADS)[:, :, 1 - o:1 - o + SB],
                            small[0:1, 2 * o * P:(2 * o + 2) * P].rearrange("a (x k) -> a x k", k=SB)))
                    v.tensor_tensor_scan(chain[0:1, 0], ends[0:1, 0, 1], ends[0:1, 0, 0], -BIG, ALU.add, ALU.max
                                         ).then_inc(chain_ready, 1)
                    v.tensor_tensor_scan(chain[0:1, 1, ::-1], ends[0:1, 1, 1, ::-1], ends[0:1, 1, 0, ::-1], -BIG,
                                         ALU.add, ALU.max).then_inc(chain_ready, 1)
                    dve.wait_ge(chain_ready, b * 2 + 2)
                    for o in range(2):
                        v.tensor_copy(heads(enter[0:1, o]), heads(chain[0:1, o])[:, :, o:o + SB]
                                      ).then_inc(enter_ready, 1)
                    carry = heads(ends[0:1, 0, 0])[:, :, 0]
                    link(v.tensor_tensor(mx4[:], carry, heads(chain[0:1, 1])[:, :, 0], ALU.max))
                    link(v.tensor_tensor(dl4[:], carry, mx4[:], ALU.subtract))
                    v.tensor_scalar(dl4[:], dl4[:], K["goes_on"][:, bass.ds(b, 1)], None, ALU.mult
                                    ).then_inc(dl_ready, 1)
                    link(v.tensor_copy(carry, heads(chain[0:1, 0])[:, :, SB]))
                    build_onehots(b + 1, 1 - u, range(3, 4))
                    dve.wait_ge(init_done, b + 1)
                    link(v.tensor_copy(init[:], small[:, 0:2]))
                    v.tensor_tensor_scan(fwd[:], rf, e_ps[:, 0:P], init[:, 0:1], ALU.add, ALU.max).then_inc(dch, 1)
                    link.n += 1
                    link(v.tensor_tensor_scan(bwd[:, ::-1], rb, e_ps[:, 0:P][:, ::-1], init[:, 1:2], ALU.add, ALU.max))
                    dve.wait_ge(g_done, b + 1)
                    v.tensor_scalar(g4[:], g4[:], 1.0, None, ALU.subtract).then_inc(gm_ready, 1)
                    link(v.tensor_tensor(top[:], fwd[:], bwd[:], ALU.max))
                    v.tensor_tensor(top[:], e_ps[:, 0:P], top[:], ALU.subtract).then_inc(x_ready, 1)
                    dve.wait_ge(gm_bc, b + 1)
                    link(v.tensor_scalar(node_scale[:], small[:, 0:HEADS], K["first_node"][:, bass.ds(b, 1)], 1.0,
                                         ALU.mult, ALU.add))
                    dve.wait_ge(w_done, b + 1)
                    for k in range(SB + 1):
                        if k < SB:
                            v.tensor_tensor(y[:, k % 2].rearrange("p (h f) -> p h f", h=HEADS),
                                            rows[:, u, k, 0:HEADS * HB].rearrange("p (h f) -> p h f", h=HEADS),
                                            wt[:, u, :, k:k + 1].broadcast_to([P, HEADS, HB]), ALU.mult
                                            ).then_inc(y_ready, 1)
                        if k % 8 == 0 and k < SB:
                            nodes_before = nodes if k else None
                            _, nodes = nc.values_load_multi_w_load_instructions(
                                K["step_node"][0:1, bass.ds(b * SB + k, 8)], engines=DVE_ONLY, min_val=0,
                                max_val=NT - 1, skip_runtime_bounds_check_because=WHY_IN_RANGE)
                        if k == 0:
                            dve.wait_ge(acc_done, b * SB)
                            a = K["acc"][:, bass.ds(nodes[0], 1), :].rearrange("p a (h f) -> p (a h) f", h=HEADS)
                            link(v.tensor_tensor(a, a, node_scale[:].unsqueeze(2).broadcast_to([P, HEADS, HB]),
                                                 ALU.mult))
                        else:
                            j = k - 1
                            node = (nodes_before if k % 8 == 0 and k < SB else nodes)[j % 8]
                            dve.wait_ge(mm_done, b * SB + k)
                            if j:
                                dve.wait_ge(acc_done, b * SB + j)
                            a = K["acc"][:, bass.ds(node, 1), :].rearrange("p a f -> p (a f)")
                            v.tensor_tensor(a, out_ps[:, j % 2, 0:HEADS * HB], a, ALU.add).then_inc(acc_done, 1)
                        if k == SB - 1:
                            dve.wait_ge(y_ready, b * SB + SB)
                            dve.sem_inc(rows_free, 1)
                    while link.n < PER:
                        link.n += 1
                        dve.sem_inc(dch, 1)
            dve.wait_ge(acc_done, STEPS)


def token_phase(nc, K, M, dram, x, gamma, beta, Wr, br, W1, b1, W2, b2, out):
    CHUNKS = 10
    TC = NT // CHUNKS
    NR = NT * E
    KT = TOPK * NT
    acc, table = K["acc"], dram["slot_table"]
    with ExitStack() as ctx:
        m = Mem(nc, ctx)
        xin = m.sb("x_chunk", [P, 2, TC, D])
        stats, mean, rstd, tmp = (m.sb("stats2", [P, NT, 6]), m.sb("mean2", [P, NT]), m.sb("rstd2", [P, NT]),
                                  m.sb("ln_tmp2", [P, NT]))
        den, den2 = m.sb("den", [P, NT, HEADS]), m.sb("den2", [P, NT, HEADS])
        att = m.sb("att_out", [P, 2, D])
        gam, bet, br_b = m.sb("gamma_b", [P, D]), m.sb("beta_b", [P, D]), m.sb("br_b", [P, E])
        wr = m.sb("wr", [P, 2, E])
        xT = m.sb("xT2", [P, 2, 2, P])
        lg, lg2 = m.sb("logits", [P, NT, E]), m.sb("logits2", [P, NT, E])
        iota_e, valid = m.sb("iota_expert", [P, E]), m.sb("valid", [P, NT])
        tok_f, tok_i = m.sb("token_f", [P, NT]), m.sb("token_i", [P, NT], I32)
        best, which = m.sb("best", [P, TOPK, NT]), m.sb("which", [P, TOPK, NT])
        oh, cand = m.sb("expert_oh", [P, TOPK, NT, E]), m.sb("cand", [P, NT, E])
        tot, inc, keep = m.sb("tot", [P, E, KT]), m.sb("inc", [P, E, KT]), m.sb("keep", [P, E, KT])
        jt, gt = m.sb("jt", [P, ST_]), m.sb("gt", [P, E, ST_])
        ntl, ctl, base = m.sb("ntiles", [P, E]), m.sb("cum_tiles", [P, E]), m.sb("slot_base", [P, E])
        rank = m.sb("rank", [P, TOPK, NT, E])
        pos, pos_i = m.sb("pos", [P, TOPK, NT]), m.sb("pos_i", [P, NT, TOPK], I32)
        wgt, pay = m.sb("wgt", [P, TOPK, NT]), m.sb("payload", [P, NT, TOPK, 2], I32)
        pay_now, pos_now = m.sb("pay_now", [P, 2, TOPK, 2], I32), m.sb("pos_now", [P, 2, TOPK], I32)
        before = m.sb("before", [P, P])
        blank = m.sb("blank_slots", [ST_ + 2, P, 2], I32)
        exp_f = m.sb("tile_expert_f", [1, ST_ + 2, E])
        jrow = m.sb("tile_row", [1, ST_ + 2])
        exp_s = m.sb("tile_expert_s", [1, ST_ + 2])
        t_ps, l_ps, r_ps = m.ps("t2_ps", [P, 2, 512]), m.ps("l_ps", [P, 2, 512]), m.ps("r_ps", [P, 4, 512])

        small_in, w_in, x_in, x_used = m.sem("small_in"), M["weights_in"], m.sems("x2_in", 2), m.sem("x_used")
        dch, x1_done, x1_out, made = m.sem("dve_t"), m.sem("x1_done"), m.sem("x1_out"), m.sem("made")
        st_done, var_ready, std_ready, ach = m.sem("st_done"), m.sem("var2"), m.sem("std2"), m.sem("att_ch")
        xn_out, xt_done, xt_cp = m.sems("xn2_out", 2), m.sem("xt2_done"), m.sem("xt2_cp")
        l_done, l_free, ex_in, ex_out = m.sem("l_done"), m.sem("l_free"), m.sem("ex_in"), m.sem("ex_out")
        oh_done, r_done, blank_out, pay_done = (m.sem("oh_done"), m.sem("r_done"), m.sem("blank_out"),
                                                m.sem("pay_done"))
        issuing = m.sem("slot_scatters_issuing")
        now_c, scat, gb, norm_c = m.sem("now_c"), m.sems("scattered", 2), m.sem("gb"), m.sem("norm_c")
        block = ctx.enter_context(nc.Block())

        def tile(t):
            return acc[:, bass.ds(t, 1), 0:D].rearrange("p a f -> p (a f)")

        @block.sync
        def _(sp):
            for u in range(2):
                sp.dma_start(xin[:, u], x[u * TC * P:(u + 1) * TC * P, :].rearrange("(t p) d -> p t d", p=P)
                             ).then_inc(x_in[u], 16)
            for o, a in ((gam, gamma), (bet, beta), (br_b, br)):
                sp.dma_start(o[:], a.rearrange("(o d) -> o d", o=1).broadcast_to([P, a.shape[0]])
                             ).then_inc(small_in, 16)
            sp.dma_start(wr[:], Wr.rearrange("(k p) e -> p k e", p=P)).then_inc(small_in, 16)
            for c in range(2, CHUNKS):
                sp.wait_ge(x_used, (c - 1) * TC)
                sp.dma_start(xin[:, c % 2], x[c * TC * P:(c + 1) * TC * P, :].rearrange("(t p) d -> p t d", p=P)
                             ).then_inc(x_in[c % 2], 16)
            sp.wait_ge(made, 1)
            sp.dma_start(table[0:(ST_ + 2) * P, :].rearrange("(t p) c -> t (p c)", p=P),
                         blank[:].rearrange("t p c -> t (p c)")).then_inc(blank_out, 16)
            for c in range(CHUNKS):
                sp.wait_ge(x_used, (c + 1) * TC)
                sp.dma_start(out[c * TC * P:(c + 1) * TC * P, :].rearrange("(t p) d -> p t d", p=P),
                             acc[:, c * TC:(c + 1) * TC, 0:D]).then_inc(x1_out, 16)
            with sp.Fori(0, NT // 2) as i:
                for u in range(2):
                    sp.wait_ge(norm_c, i * 2 + (u + 1))
                    sp.dma_start(dram["xn"][bass.ds((i * 2 + u) * P, P), :], M["xn_now"][:, u]).then_inc(xn_out[u], 16)
            for u in range(2):
                sp.wait_ge(xn_out[u], 16 * (NT // 2))
            sp.wait_ge(x1_out, 16 * CHUNKS)
            sp.wait_ge(blank_out, 16)

        @block.gpsimd
        def _(pool):
            g = nc.gpsimd
            link = Chain(pool, gb)
            kw = dict(allow_small_or_imprecise_dtypes=True)
            link(g.iota(blank[:, :, 0], pattern=[[1, P]], base=PAD_ROW, channel_multiplier=0))
            link(g.memset(blank[:, :, 1], 0))
            pool.sem_inc(made, 1)
            link(g.iota(iota_e[:], pattern=[[1, E]], base=0, channel_multiplier=0, **kw))
            link(g.iota(tok_f[:], pattern=[[P, NT]], base=0, channel_multiplier=1, **kw))
            link(g.iota(tok_i[:], pattern=[[P, NT]], base=0, channel_multiplier=1))
            link(g.iota(jt[:], pattern=[[P, ST_]], base=0, channel_multiplier=0, **kw))
            link(g.iota(jrow[:], pattern=[[1, ST_ + 2]], base=0, channel_multiplier=0, **kw))
            link(g.memset(keep[:], 1.0))
            link(g.memset(keep[:, :, 0:1], 0.0))
            link(g.affine_select(out=before[:], in_=K["ones"][:], compare_op=ALU.is_gt, fill=0.0, base=0,
                                 pattern=[[1, P]], channel_multiplier=-1))
            pool.sem_inc(made, 1)
            pool.wait_ge(pay_done, 1)
            pool.wait_ge(blank_out, 16)
            with pool.Fori(0, NT // 2) as i:
                for u in range(2):
                    pool.wait_ge(scat[u], i * (16 * TOPK))
                    g.tensor_copy(pay_now[:, u].rearrange("p k c -> p (k c)"),
                                  pay[:, bass.ds(i * 2 + u, 1)].rearrange("p a k c -> p (a k c)")).then_inc(now_c, 1)
                    g.tensor_copy(pos_now[:, u], pos_i[:, bass.ds(i * 2 + u, 1)].rearrange("p a k -> p (a k)")
                                  ).then_inc(now_c, 1)
                    pool.wait_ge(now_c, i * 4 + (2 * u + 2))
                    pool.sem_inc(issuing, 1)
                    for k in range(TOPK):
                        g.indirect_dma_start(out=table, in_=pay_now[:, u, k, :], in_offset=None,
                                             out_offset=bass.IndirectOffsetOnAxis(ap=pos_now[:, u, k:k + 1], axis=0)
                                             ).then_inc(scat[u], 16)
            for u in range(2):
                pool.wait_ge(scat[u], 16 * TOPK * (NT // 2))

        @block.tensor
        def _(pe):
            pe.wait_ge(small_in, 64)
            with pe.Fori(0, NT // 2) as i:
                for u in range(2):
                    pe.wait_ge(norm_c, i * 2 + (u + 1))
                    for k in range(2):
                        mm = nc.tensor.transpose(t_ps[:, u, k * P:(k + 1) * P], M["xn_now"][:, u, k * P:(k + 1) * P],
                                                 K["ident"][:])
                    mm.then_inc(xt_done, 1)
                    pe.wait_ge(xt_cp, i * 2 + (u + 1))
                    pe.wait_ge(l_free, i * 2 + (u + 1))
                    for k in range(2):
                        mm = nc.tensor.matmul(l_ps[:, u, 0:E], xT[:, u, k, :], wr[:, k, :], start=(k == 0),
                                              stop=(k == 1))
                    mm.then_inc(l_done, 1)
            pe.wait_ge(oh_done, 1)
            pe.wait_ge(made, 2)
            for k in range(TOPK):
                rhs = oh[:, k].rearrange("p t e -> p (t e)")
                nc.tensor.matmul(r_ps[:, k, 0:NR], before[:], rhs, start=True, stop=True)
                mm = nc.tensor.matmul(r_ps[:, 2 + k, 0:NR], K["ones"][:], rhs, start=True, stop=True)
            mm.then_inc(r_done, 1)

        @block.scalar
        def _(act):
            for k in range(2):
                act.dma_start(M["w1"][:, k].rearrange("p (e h) -> p e h", e=E),
                              W1[:, k * P:(k + 1) * P, :].rearrange("e p h -> p e h")).then_inc(w_in, 16)
            for k in range(4):
                act.dma_start(M["w2"][:, k].rearrange("p (e h) -> p e h", e=E),
                              W2[:, k * P:(k + 1) * P, :].rearrange("e p h -> p e h")).then_inc(w_in, 16)
            act.dma_start(M["b1"][:], b1.rearrange("(o e) h -> o (e h)", o=1).broadcast_to([P, E * HID])
                          ).then_inc(w_in, 16)
            act.dma_start(M["b2"][:], b2.rearrange("(o e) h -> o (e h)", o=1).broadcast_to([P, E * D])
                          ).then_inc(w_in, 16)
            for n in range(2):
                act.wait_ge(var_ready, n + 1)
                nc.scalar.activation(rstd[:], rstd[:], ACT.Sqrt, bias=K["eps"][:, 0:1]).then_inc(std_ready, 1)
            with act.Fori(0, NT // 2) as i:
                for u in range(2):
                    act.wait_ge(xt_done, i * 2 + (u + 1))
                    act.wait_ge(l_free, i * 2 + (u + 1))
                    nc.scalar.copy(xT[:, u].rearrange("p k n -> p (k n)"), t_ps[:, u, 0:2 * P]).then_inc(xt_cp, 1)
            act.wait_ge(ex_in, 1)
            nc.scalar.activation(wgt[:, 1, :], wgt[:, 1, :], ACT.Exp).then_inc(ex_out, 1)
            act.wait_ge(w_in, 16 * 8)

        @block.vector
        def _(dve):
            v = nc.vector
            link = Chain(dve, dch)
            dve.sem_inc(l_free, 2)
            d_in = acc[:].rearrange("p t (h f) -> p t h f", h=HEADS)[:, :, :, HD]
            link(v.tensor_scalar(den2[:], d_in, 0.0, None, ALU.is_le))
            link(v.tensor_tensor(den[:], d_in, den2[:], ALU.add))
            link(v.reciprocal(den[:], den[:]))
            for c in range(CHUNKS):
                dve.wait_ge(x_in[c % 2], 16 * (c // 2 + 1))
                with dve.Fori(0, TC) as i:
                    t = i + c * TC
                    a = acc[:, bass.ds(t, 1), :].rearrange("p a (h f) -> p (a h) f", h=HEADS)
                    v.tensor_tensor(att[:, 0].rearrange("p (h f) -> p h f", h=HEADS), a[:, :, 0:HD],
                                    den[:, bass.ds(t, 1), :].rearrange("p a h -> p (a h)").unsqueeze(2)
                                    .broadcast_to([P, HEADS, HD]), ALU.mult).then_inc(ach, 1)
                    dve.wait_ge(ach, t + 1)
                    v.tensor_tensor(tile(t), att[:, 0], xin[:, c % 2, bass.ds(i, 1), :].rearrange("p a d -> p (a d)"),
                                    ALU.add).then_inc(x_used, 1)
                    dve.wait_ge(x_used, t + 1)
                    v.bn_stats(stats[:, bass.ds(t, 1), :].rearrange("p a c -> p (a c)"), tile(t)).then_inc(st_done, 1)
            dve.wait_ge(st_done, NT)
            mean_and_rstd(nc, dve, link, stats[:], mean[:], rstd[:], tmp[:], var_ready, std_ready, 1)
            dve.wait_ge(x1_out, 16 * CHUNKS)
            with dve.Fori(0, NT) as t:
                v.tensor_scalar(tile(t), tile(t), mean[:, bass.ds(t, 1)], rstd[:, bass.ds(t, 1)],
                                ALU.subtract, ALU.mult).then_inc(ach, 1)
                dve.wait_ge(ach, t + (NT + 1))
                v.bn_stats(stats[:, bass.ds(t, 1), :].rearrange("p a c -> p (a c)"), tile(t)).then_inc(st_done, 1)
            dve.wait_ge(st_done, 2 * NT)
            mean_and_rstd(nc, dve, link, stats[:], mean[:], rstd[:], tmp[:], var_ready, std_ready, 2)
            dve.wait_ge(small_in, 64)

            def normalise(t, u):
                xn = M["xn_now"][:, u]
                v.tensor_scalar(xn, tile(t), mean[:, bass.ds(t, 1)], rstd[:, bass.ds(t, 1)],
                                ALU.subtract, ALU.mult).then_inc(ach, 1)
                dve.wait_ge(ach, t * 2 + (2 * NT + 1))
                v.tensor_tensor(xn, xn, gam[:], ALU.mult).then_inc(ach, 1)
                dve.wait_ge(ach, t * 2 + (2 * NT + 2))
                v.tensor_tensor(xn, xn, bet[:], ALU.add).then_inc(norm_c, 1)

            def take_logits(t, u):
                dve.wait_ge(l_done, t + 1)
                v.tensor_tensor(lg[:, bass.ds(t, 1), :].rearrange("p a e -> p (a e)"), l_ps[:, u, 0:E], br_b[:],
                                ALU.add).then_inc(l_free, 1)

            for u in range(2):
                normalise(u, u)
            with dve.Fori(0, NT // 2 - 1) as i:
                for u in range(2):
                    take_logits(i * 2 + u, u)
                    dve.wait_ge(xn_out[u], i * 16 + 16)
                    normalise(i * 2 + (2 + u), u)
            for u in range(2):
                take_logits(NT - 2 + u, u)
            dve.wait_ge(l_free, NT + 2)
            dve.wait_ge(made, 2)
            ie = iota_e[:].unsqueeze(1).broadcast_to([P, NT, E])
            link(v.tensor_scalar(valid[:], tok_f[:], float(N_NODES), None, ALU.is_lt))
            for k in range(TOPK):
                src_l = (lg, lg2)[k]
                bk, wk = best[:, k].unsqueeze(2), which[:, k].unsqueeze(2)
                link(v.tensor_reduce(best[:, k], src_l[:], AX_X, ALU.max))
                link(v.tensor_tensor(cand[:], src_l[:], bk.broadcast_to([P, NT, E]), ALU.is_equal))
                link(v.tensor_scalar(cand[:], cand[:], 1.0, -float(E), ALU.subtract, ALU.mult))
                link(v.tensor_tensor(cand[:], cand[:], ie, ALU.add))
                link(v.tensor_reduce(which[:, k], cand[:], AX_X, ALU.min))
                link(v.tensor_tensor(oh[:, k], ie, wk.broadcast_to([P, NT, E]), ALU.is_equal))
                if k == 0:
                    link(v.tensor_scalar(cand[:], oh[:, 0], -BIG, None, ALU.mult))
                    link(v.tensor_tensor(lg2[:], lg[:], cand[:], ALU.add))
                link(v.tensor_tensor(oh[:, k], oh[:, k], valid[:].unsqueeze(2).broadcast_to([P, NT, E]), ALU.mult))
            dve.sem_inc(oh_done, 1)
            v.tensor_tensor(wgt[:, 1, :], best[:, 1, :], best[:, 0, :], ALU.subtract).then_inc(ex_in, 1)
            dve.wait_ge(ex_out, 1)
            link(v.tensor_scalar(wgt[:, 0, :], wgt[:, 1, :], 1.0, None, ALU.add))
            link(v.reciprocal(wgt[:, 0, :], wgt[:, 0, :]))
            link(v.tensor_tensor(wgt[:, 1, :], wgt[:, 1, :], wgt[:, 0, :], ALU.mult))
            dve.wait_ge(r_done, 1)
            for k in range(TOPK):
                link(v.tensor_copy(tot[:, :, k * NT:(k + 1) * NT],
                                   r_ps[:, 2 + k, 0:NR].rearrange("p (t e) -> p e t", e=E)))
            fl = "p e s -> p (e s)"
            link(v.tensor_tensor_scan(inc[:].rearrange(fl), keep[:].rearrange(fl), tot[:].rearrange(fl), 0.0,
                                      ALU.mult, ALU.add))
            link(v.tensor_tensor(gt[:], inc[:, :, KT - 1:KT].broadcast_to([P, E, ST_]),
                                 jt[:].unsqueeze(1).broadcast_to([P, E, ST_]), ALU.is_gt))
            link(v.tensor_reduce(ntl[:], gt[:], AX_X, ALU.add))
            link(v.tensor_tensor_scan(ctl[:], K["ones"][:, 0:E], ntl[:], 0.0, ALU.mult, ALU.add))
            link(v.tensor_tensor(base[:], ctl[:], ntl[:], ALU.subtract))
            link(v.tensor_scalar(base[:], base[:], float(P), None, ALU.mult))
            link(v.tensor_tensor(inc[:], inc[:], tot[:], ALU.subtract))
            link(v.tensor_tensor(inc[:], inc[:], base[:].unsqueeze(2).broadcast_to([P, E, KT]), ALU.add))
            for k in range(TOPK):
                link(v.tensor_tensor(rank[:, k], r_ps[:, k, 0:NR].rearrange("p (t e) -> p t e", e=E),
                                     inc[:, :, k * NT:(k + 1) * NT].rearrange("p e t -> p t e"), ALU.add))
            link(v.tensor_tensor(rank[:], rank[:], oh[:], ALU.mult))
            link(v.tensor_reduce(pos[:], rank[:], AX_X, ALU.add))
            link(v.tensor_scalar(tmp[:], valid[:], 0.0, None, ALU.is_equal))
            link(v.tensor_scalar(mean[:], tok_f[:], float((ST_ + 2) * P - (NT - 2) * P), None, ALU.add))
            link(v.tensor_tensor(mean[:], mean[:], tmp[:], ALU.mult))
            link(v.tensor_scalar(tmp[:], tmp[:], 2.0 * P, None, ALU.mult))
            for k in range(TOPK):
                if k:
                    link(v.tensor_tensor(mean[:], mean[:], tmp[:], ALU.add))
                link(v.tensor_tensor(pos_i[:, :, k], pos[:, k], mean[:], ALU.add))
                link(v.tensor_copy(pay[:, :, k, 0], tok_i[:]))
                link(v.tensor_copy(pay[:, :, k, 1].bitcast(F32), wgt[:, k]))
            dve.sem_inc(pay_done, 1)
            link(v.tensor_tensor(exp_f[:], ctl[0:1].unsqueeze(1).broadcast_to([1, ST_ + 2, E]),
                                 jrow[:].unsqueeze(2).broadcast_to([1, ST_ + 2, E]), ALU.is_le))
            link(v.tensor_reduce(exp_s[:], exp_f[:], AX_X, ALU.add))
            link(v.tensor_scalar(M["tile_expert"][:], exp_s[:], float(E - 1), None, ALU.min))


def expert_phase(nc, K, M, dram, out):
    table = dram["slot_table"]
    with ExitStack() as ctx:
        m = Mem(nc, ctx)
        raw, rawf = m.sb("slots", [ST_ + 2, P, 2], I32), m.sb("slot_tok_f", [ST_ + 2, P])
        tok, wgt = m.sb("slot_token", [P, ST_ + 2], I32), m.sb("slot_weight", [P, ST_ + 2])
        g_idx, s_idx = m.sb("gather_idx", [P, 2], I32), m.sb("scatter_idx", [P, 2], I32)
        xg, xT = m.sb("xg", [P, 2, D]), m.sb("xgT", [P, 2, 2, P])
        hb, hg, hT = m.sb("h_biased", [P, 2, HID]), m.sb("h_gelu", [P, 2, HID]), m.sb("hT", [P, 2, 4, P])
        ysb = m.sb("y_out", [P, 2, D])
        x_ps, h_ps, t_ps, y_ps = (m.ps("x_ps", [P, 1, 512]), m.ps("h_ps", [P, 2, 512]), m.ps("ht_ps", [P, 2, 512]),
                                  m.ps("y_ps", [P, 2, 512]))
        s_ps = m.ps("s_ps", [P, 512])
        raw_in, dch, rawf_done, s_t, ready = (m.sem("raw_in"), m.sem("dve_x"), m.sem("rawf"), m.sem("s_t"),
                                              m.sem("slots_ready"))
        ic, gath, scat = m.sem("idx_c"), m.sems("xg_in", 2), m.sem("y_added")
        xt_done, xt_cp, h_done, hb_done, hg_done = (m.sem("xt3"), m.sem("xt3_cp"), m.sem("h_done"),
                                                    m.sem("hb_done"), m.sem("hg_done"))
        ht_done, ht_cp, y_done, yb_done, ysb_done, y_ps_free = (m.sem("ht_done"), m.sem("ht_cp"), m.sem("y_done"),
                                                                m.sem("yb_done"), m.sem("ysb_done"), m.sem("y_ps_free"))
        y_free, issuing = m.sem("y_free"), m.sem("indirect_issuing")
        block = ctx.enter_context(nc.Block())

        @block.sync
        def _(sp):
            sp.dma_start(raw[:].rearrange("t p c -> t (p c)"),
                         table[0:(ST_ + 2) * P, :].rearrange("(t p) c -> t (p c)", p=P)).then_inc(raw_in, 16)

        @block.gpsimd
        def _(pool):
            g = nc.gpsimd

            def gather(t, u, n):
                g.tensor_copy(g_idx[:, u:u + 1], tok[:, bass.ds(t, 1)]).then_inc(ic, 1)
                pool.wait_ge(ic, n + 1)
                pool.sem_inc(issuing, 1)
                g.indirect_dma_start(out=xg[:, u], out_offset=None, in_=dram["xn"],
                                     in_offset=bass.IndirectOffsetOnAxis(ap=g_idx[:, u:u + 1], axis=0)
                                     ).then_inc(gath[u], 16)

            pool.wait_ge(ready, 1)
            gather(0, 0, 0)
            gather(1, 1, 1)
            with pool.Fori(0, ST_ // 2) as i:
                for u in range(2):
                    pool.wait_ge(xt_done, i * 2 + (u + 1))
                    gather(i * 2 + (u + 2), u, i * 4 + (2 * u + 2))
                    pool.wait_ge(ysb_done, i * 2 + (u + 1))
                    pool.wait_ge(scat, i * 32 + 16 * u)
                    pool.sem_inc(y_free, 1)
                    g.tensor_copy(s_idx[:, u:u + 1], tok[:, bass.ds(i * 2 + u, 1)]).then_inc(ic, 1)
                    pool.wait_ge(ic, i * 4 + (2 * u + 4))
                    pool.sem_inc(issuing, 1)
                    g.indirect_dma_start(out=out, in_=ysb[:, u], in_offset=None, compute_op=ALU.add,
                                         out_offset=bass.IndirectOffsetOnAxis(ap=s_idx[:, u:u + 1], axis=0)
                                         ).then_inc(scat, 16)
            pool.wait_ge(scat, 16 * ST_)
            for u in range(2):
                pool.wait_ge(gath[u], 16 * (ST_ // 2 + 1))

        @block.tensor
        def _(pe):
            ident = K["ident"][:]
            pe.wait_ge(rawf_done, 1)
            n = ST_ + 2
            nc.tensor.transpose(s_ps[:, 0:n], rawf[:], ident[0:n, 0:n])
            nc.tensor.transpose(s_ps[:, P:P + n], M["slot_w"][0:n, :], ident[0:n, 0:n]).then_inc(s_t, 1)

            def turn_x(u, i, t):
                pe.wait_ge(gath[u], i * 16 + 16)
                if t is not None:
                    pe.wait_ge(xt_cp, t)
                for k in range(2):
                    mm = nc.tensor.transpose(x_ps[:, 0, k * P:(k + 1) * P], xg[:, u, k * P:(k + 1) * P], ident)
                mm.then_inc(xt_done, 1)

            def up(u, t, e):
                pe.wait_ge(xt_cp, t + 1)
                for k in range(2):
                    mm = nc.tensor.matmul(h_ps[:, u, :], xT[:, u, k, :],
                                          M["w1"][:, k, bass.ds(e * HID, HID)], start=(k == 0), stop=(k == 1))
                mm.then_inc(h_done, 1)

            def turn_h(u, t):
                pe.wait_ge(hg_done, t + 1)
                for k in range(4):
                    mm = nc.tensor.transpose(t_ps[:, u, k * P:(k + 1) * P], hg[:, u, k * P:(k + 1) * P], ident)
                mm.then_inc(ht_done, 1)

            def down(u, t, e):
                pe.wait_ge(ht_cp, t + 1)
                for k in range(4):
                    mm = nc.tensor.matmul(y_ps[:, u, 0:D], hT[:, u, k, :], M["w2"][:, k, bass.ds(e * D, D)],
                                          start=(k == 0), stop=(k == 3))
                mm.then_inc(y_done, 1)

            def experts(t, n):
                return nc.values_load_multi_w_load_instructions(
                    M["tile_expert"][0:1, bass.ds(t, n)], engines=PE_ONLY, min_val=0, max_val=E - 1,
                    skip_runtime_bounds_check_because=WHY_IN_RANGE)[1]

            turn_x(0, 0, None)
            up(0, 0, experts(0, 1)[0])
            turn_x(1, 0, 1)
            with pe.Fori(0, ST_ // 2) as i:
                ex = experts(i * 2, 3)
                for u in range(2):
                    t = i * 2 + u
                    turn_h(u, t)
                    pe.wait_ge(hb_done, t)
                    up(1 - u, t + 1, ex[u + 1])
                    turn_x(u, i + 1, t + 2)
                    pe.wait_ge(y_ps_free, t + 1)
                    down(u, t, ex[u])

        @block.scalar
        def _(act):
            def copy_x(u, t):
                act.wait_ge(xt_done, t + 1)
                nc.scalar.copy(xT[:, u].rearrange("p k n -> p (k n)"), x_ps[:, 0, 0:2 * P]).then_inc(xt_cp, 1)

            copy_x(0, 0)
            copy_x(1, 1)
            with act.Fori(0, ST_ // 2) as i:
                for u in range(2):
                    t = i * 2 + u
                    act.wait_ge(hb_done, t + 1)
                    nc.scalar.activation(hg[:, u], hb[:, u], ACT.Gelu).then_inc(hg_done, 1)
                    copy_x(u, t + 2)

        @block.vector
        def _(dve):
            v = nc.vector
            link = Chain(dve, dch)
            dve.sem_inc(y_ps_free, 2)
            dve.wait_ge(raw_in, 16)
            link(v.tensor_copy(M["slot_w"][0:ST_ + 2, :], raw[:, :, 1].bitcast(F32)))
            v.tensor_copy(rawf[:], raw[:, :, 0]).then_inc(rawf_done, 1)
            dve.wait_ge(s_t, 1)
            link(v.tensor_copy(tok[:], s_ps[:, 0:ST_ + 2]))
            link(v.tensor_copy(wgt[:], s_ps[:, P:P + ST_ + 2]))
            dve.sem_inc(ready, 1)
            dve.wait_ge(M["weights_in"], 16 * 8)

            def experts(t, n):
                return nc.values_load_multi_w_load_instructions(
                    M["tile_expert"][0:1, bass.ds(t, n)], engines=DVE_ONLY, min_val=0, max_val=E - 1,
                    skip_runtime_bounds_check_because=WHY_IN_RANGE)[1]

            def bias_h(u, t, e):
                dve.wait_ge(h_done, t + 1)
                v.tensor_tensor(hb[:, u], h_ps[:, u, :], M["b1"][:, bass.ds(e * HID, HID)], ALU.add
                                ).then_inc(hb_done, 1)

            bias_h(0, 0, experts(0, 1)[0])
            with dve.Fori(0, ST_ // 2) as i:
                ex = experts(i * 2, 3)
                for u in range(2):
                    t = i * 2 + u
                    dve.wait_ge(ht_done, t + 1)
                    v.tensor_copy(hT[:, u].rearrange("p k n -> p (k n)"), t_ps[:, u, :]).then_inc(ht_cp, 1)
                    bias_h(1 - u, t + 1, ex[u + 1])
                    dve.wait_ge(y_done, t + 1)
                    dve.wait_ge(y_free, t)
                    v.tensor_tensor(ysb[:, u], y_ps[:, u, 0:D], M["b2"][:, bass.ds(ex[u] * D, D)], ALU.add
                                    ).then_inc(y_ps_free, 1)
                    dve.wait_ge(y_ps_free, t + 3)
                    v.tensor_scalar(ysb[:, u], ysb[:, u], wgt[:, bass.ds(t, 1)], None, ALU.mult).then_inc(ysb_done, 1)


def build(nc, x, src, dst, W, att, gamma, beta, Wr, br, W1, b1, W2, b2, out):
    def scratch(name, shape, dt):
        return nc.dram_tensor(name, shape, dt, kind="Internal").ap()

    dram = {
        "z_table": scratch("z_table", (NP, ROW), F32), "xn": scratch("xn_rows", (NP, D), F32),
        "step_edge_tile": scratch("step_edge_tile", (SP + 2,), I32),
        "step_node_tile": scratch("step_node_tile", (SP,), I32), "flags": scratch("step_flags", (2, SP, P), F32),
        "slot_table": scratch("slot_table", ((ST_ + 2 + 2 * TOPK) * P, 2), I32),
    }
    with ExitStack() as ctx:
        K = lasting(nc, ctx)
        constants_phase(nc, K)
        with ExitStack() as graph:
            K.update(graph_tables(nc, graph))
            step_table_phase(nc, K, dram, src, dst)
            chain_table_phase(nc, K)
            node_phase(nc, K, dram, x, W, att)
            edge_phase(nc, K, dram)
        M = expert_buffers(nc, ctx)
        token_phase(nc, K, M, dram, x, gamma, beta, Wr, br, W1, b1, W2, b2, out)
        expert_phase(nc, K, M, dram, out)


def kernel(x, src, dst, L0_gnn_W, L0_gnn_att, L0_ffn_gamma, L0_ffn_beta, L0_ffn_Wr, L0_ffn_br, L0_ffn_W1,
           L0_ffn_b1, L0_ffn_W2, L0_ffn_b2):
    import numpy as np
    import concourse.bacc as bacc
    from concourse.bass_utils import run_bass_kernel_spmd

    def padded(a, shape, fill):
        a = np.asarray(a)
        out = np.full(shape, fill, a.dtype)
        out[:a.shape[0]] = a
        return out

    arrays = {
        "x": padded(x, (NP, D), 0), "src": padded(src, (ET * P,), 0).reshape(ET, P),
        "dst": padded(dst, (ET * P,), PAD_DST).reshape(ET, P), "W": L0_gnn_W, "att": L0_gnn_att,
        "gamma": L0_ffn_gamma, "beta": L0_ffn_beta, "Wr": L0_ffn_Wr, "br": L0_ffn_br, "W1": L0_ffn_W1,
        "b1": L0_ffn_b1, "W2": L0_ffn_W2, "b2": L0_ffn_b2,
    }
    arrays = {name: np.ascontiguousarray(a) for name, a in arrays.items()}
    nc = bacc.Bacc("TRN2", target_bir_lowering=False, num_devices=1)
    args = [nc.dram_tensor(name, a.shape, mybir.dt.from_np(a.dtype), kind="ExternalInput").ap()
            for name, a in arrays.items()]
    out = nc.dram_tensor("out", (NP, D), F32, kind="ExternalOutput").ap()
    build(nc, *args, out)
    r = run_bass_kernel_spmd(nc, [arrays], core_ids=[0])
    return r.results[0]["out"][:N_NODES]
```

```python
from contextlib import ExitStack

import concourse.bass as bass
from concourse import mybir

P = 128
F32 = mybir.dt.float32
I32 = mybir.dt.int32
ALU = mybir.AluOpType
ACT = mybir.ActivationFunctionType
AX_X = mybir.AxisListType.X
DVE_ONLY = (mybir.EngineType.DVE,)
PE_ONLY = (mybir.EngineType.PE,)
WHY_IN_RANGE = "the table is clamped on the chip to the buffer's range"

N_NODES, N_EDGES = 6250, 100000
D = 256
HEADS, HD = 4, 64
HB = HD + 1
ROW = HEADS * HB + HEADS
E, TOPK, HID = 8, 2, 512

NT = -(-N_NODES // P) + 1
NP = NT * P
PAD_ROW = (NT - 1) * P
ET = -(-N_EDGES // P)
PAD_DST = 8191
SB = 32
NB = -(-(ET + NT - 2) // SB)
NB += NB % 2
STEPS = NB * SB
SJ = -(-(STEPS + 1) // P)
SP = SJ * P
ST_ = (TOPK * N_NODES + E * (P - 1)) // P
XB = 4
ST_ += -ST_ % XB
STX = ST_ + XB
SLOTS = ST_ * P
BIG = 1e30
EPS = 1e-5
SLOPE, NEG = 0.01, -1000.0


class Chain:

    def __init__(self, eng, sem, base=0):
        self.eng, self.sem, self.base, self.n = eng, sem, base, 0

    def __call__(self, ins):
        self.n += 1
        ins.then_inc(self.sem, 1)
        self.eng.wait_ge(self.sem, self.base + self.n)


class Mem:

    def __init__(self, nc, ctx):
        self.nc, self.ctx = nc, ctx

    def sb(self, name, shape, dt=F32):
        return self.ctx.enter_context(self.nc.sbuf_tensor(name, shape, dt))

    def ps(self, name, shape):
        return self.ctx.enter_context(self.nc.psum_tensor(name, shape, F32))

    def sem(self, name):
        return self.ctx.enter_context(self.nc.semaphore(name))

    def sems(self, name, n):
        return [self.sem(f"{name}{i}") for i in range(n)]


def constants_phase(nc, K):
    with ExitStack() as ctx:
        m = Mem(nc, ctx)
        made = m.sem("const_made")
        block = ctx.enter_context(nc.Block())

        @block.gpsimd
        def _(pool):
            link = Chain(pool, made)
            link(nc.gpsimd.memset(K["ident"][:], 0.0))
            link(nc.gpsimd.affine_select(out=K["ident"][:], in_=K["ident"][:], compare_op=ALU.not_equal, fill=1.0,
                                         base=0, pattern=[[-1, P]], channel_multiplier=1))
            link(nc.gpsimd.iota(K["iota_row"][:], pattern=[[1, P]], base=0, channel_multiplier=0,
                                allow_small_or_imprecise_dtypes=True))
            link(nc.gpsimd.iota(K["iota_col"][:], pattern=[[0, 1]], base=0, channel_multiplier=1,
                                allow_small_or_imprecise_dtypes=True))
            link(nc.gpsimd.memset(K["ones"][:], 1.0))
            link(nc.gpsimd.memset(K["eps"][:], EPS))


def step_table_phase(nc, K, dram, src, dst):
    CH = ET // 2
    with ExitStack() as ctx:
        m = Mem(nc, ctx)
        ends = m.sb("tile_ends", [1, 2, ET], I32)
        tiles = m.sb("tile_ends_node_tile", [1, 2, ET])
        row = m.sb("cum_and_shift", [1, 2, ET])
        cb = m.sb("cum_and_shift_all", [P, 2, ET])
        one_row = m.sb("one_row", [1, ET])
        junk = m.sb("junk", [P, ET])
        iota_e = m.sb("iota_e", [P, ET])
        s_col = m.sb("s_col", [P, SJ])
        e_col, d_col, n_col = m.sb("e_col", [P, SJ]), m.sb("d_col", [P, SJ]), m.sb("n_col", [P, SJ])
        e_int, n_int = m.sb("e_int", [P, SJ], I32), m.sb("n_int", [P, SJ], I32)
        base_col = m.sb("node_base_col", [P, SJ])
        idx = m.sb("step_rows_idx", [P, 3, SJ], I32)
        rows = m.sb("step_dst", [P, 3, SJ, P], I32)
        srow = m.sb("step_src", [P, SJ, P], I32)
        same = m.sb("same_flags", [P, 2, SJ, P])
        locf, srcf = m.sb("loc_rows", [P, SJ, P]), m.sb("src_rows", [P, SJ, P])
        last_tile = m.sb("last_tile", [1, 1], I32)
        pb = m.ps("bcast_ps", [P, 4, 512])
        pt = m.ps("turn_ps", [P, 2, 512])

        in_s, row_done, bc_done, pool_c = m.sem("ends_in"), m.sem("row_done"), m.sem("bcast_done"), m.sem("pool_tbl")
        dch, e_done, tbl_out = m.sem("dve_tbl"), m.sem("e_done"), m.sem("tbl_out")
        idx_in, rows_in, flags_done, flags_out = (m.sem("idx_in"), m.sem("rows_in"), m.sem("flags_done"),
                                                  m.sem("flags_out"))
        turned, copied, rep_in = m.sem("turned"), m.sem("turn_copied"), m.sem("flags_rep_in")
        ctx.enter_context(nc.allow_non_contiguous_dma(reason="one word for an edge tile or a step, once"))
        block = ctx.enter_context(nc.Block())
        e_dram, n_dram, flag_dram = dram["step_edge_tile"], dram["step_node_tile"], dram["flags"]

        @block.sync
        def _(sp):
            for j, col in ((0, 0), (1, P - 1)):
                sp.dma_start(ends[0:1, j, :], dst[:, col:col + 1].rearrange("e o -> o e")).then_inc(in_s, 16)
            sp.wait_ge(in_s, 32)
            lp = (N_EDGES - 1) % P
            sp.dma_start(ends[0:1, 1, ET - 1:ET], dst[ET - 1:ET, lp:lp + 1]).then_inc(in_s, 16)
            sp.wait_ge(e_done, 1)
            sp.dma_start(e_dram[1:1 + SP].rearrange("(j p) -> p j", p=P), e_int[:]).then_inc(tbl_out, 16)
            for at in (0, SP + 1):
                sp.dma_start(e_dram[at:at + 1].rearrange("(a b) -> a b", b=1), last_tile[:]).then_inc(tbl_out, 16)
            sp.dma_start(n_dram[0:SP].rearrange("(j p) -> p j", p=P), n_int[:]).then_inc(tbl_out, 16)
            sp.wait_ge(tbl_out, 64)
            for o in range(2):
                sp.dma_start(idx[:, o * 2, :], e_dram[2 * o:2 * o + SP].rearrange("(j p) -> p j", p=P)
                             ).then_inc(idx_in, 16)
            sp.dma_start(K["step_node"][:], n_dram[0:STEPS + SB].rearrange("(a s) -> a s", a=1)).then_inc(idx_in, 16)
            sp.wait_ge(flags_done, 1)
            for o in range(2):
                sp.dma_start(flag_dram[o].rearrange("(j p) i -> p j i", p=P), same[:, o]).then_inc(flags_out, 16)
            sp.wait_ge(flags_out, 32)
            for o, name in enumerate(("reset_fwd", "reset_bwd")):
                for h in range(HEADS):
                    sp.dma_start(K[name][h * SB:(h + 1) * SB],
                                 flag_dram[o, 0:STEPS].rearrange("(b k) i -> k b i", k=SB)).then_inc(rep_in, 16)
            sp.wait_ge(rep_in, 16 * 2 * HEADS)
            sp.wait_ge(idx_in, 48)

        @block.gpsimd
        def _(pool):
            nc.gpsimd.iota(iota_e[:], pattern=[[1, ET]], base=0, channel_multiplier=0,
                           allow_small_or_imprecise_dtypes=True).then_inc(pool_c, 1)
            nc.gpsimd.iota(s_col[:], pattern=[[P, SJ]], base=0, channel_multiplier=1,
                           allow_small_or_imprecise_dtypes=True).then_inc(pool_c, 1)
            nc.gpsimd.memset(last_tile[:], ET - 1).then_inc(pool_c, 1)
            pool.wait_ge(idx_in, 48)
            pool.wait_ge(e_done, 1)
            for j in range(SJ):
                for o in (0, 2):
                    nc.gpsimd.indirect_dma_start(
                        out=rows[:, o, j, :], out_offset=None, in_=dst,
                        in_offset=bass.IndirectOffsetOnAxis(ap=idx[:, o, j:j + 1], axis=0)).then_inc(rows_in, 16)
                for out, table in ((rows[:, 1, j, :], dst), (srow[:, j, :], src)):
                    nc.gpsimd.indirect_dma_start(
                        out=out, out_offset=None, in_=table,
                        in_offset=bass.IndirectOffsetOnAxis(ap=e_int[:, j:j + 1], axis=0)).then_inc(rows_in, 16)

        @block.tensor
        def _(pe):
            pe.wait_ge(row_done, 1)
            for a in range(2):
                for c in range(2):
                    mm = nc.tensor.matmul(pb[:, 2 * a + c, 0:CH], K["ones"][0:1, :], row[0:1, a, c * CH:(c + 1) * CH],
                                          start=True, stop=True)
            mm.then_inc(bc_done, 1)
            pe.wait_ge(flags_done, 1)
            for n in range(2 * SJ):
                if n >= 2:
                    pe.wait_ge(copied, n - 1)
                source = (locf, srcf)[n % 2]
                nc.tensor.transpose(pt[:, n % 2, 0:P], source[:, n // 2, :], K["ident"][:]).then_inc(turned, 1)

        @block.vector
        def _(dve):
            v = nc.vector
            link = Chain(dve, dch)
            dve.wait_ge(in_s, 48)
            link(v.tensor_scalar(ends[:], ends[:], 7, None, ALU.arith_shift_right))
            link(v.tensor_copy(tiles[:], ends[:]))
            link(v.memset(one_row[:], 1.0))
            link(v.tensor_tensor(row[0:1, 1, :], tiles[0:1, 1, :], tiles[0:1, 0, :], ALU.subtract))
            link(v.tensor_scalar(row[0:1, 1, :], row[0:1, 1, :], 1.0, None, ALU.add))
            link(v.tensor_tensor_scan(row[0:1, 0, :], one_row[:], row[0:1, 1, :], 0.0, ALU.mult, ALU.add))
            link(v.tensor_tensor(row[0:1, 1, :], row[0:1, 0, :], row[0:1, 1, :], ALU.subtract))
            v.tensor_tensor(row[0:1, 1, :], row[0:1, 1, :], tiles[0:1, 0, :], ALU.subtract).then_inc(row_done, 1)
            dve.wait_ge(bc_done, 1)
            for a in range(2):
                link(v.tensor_copy(cb[:, a].rearrange("p (c x) -> p c x", c=2), pb[:, 2 * a:2 * a + 2, 0:CH]))
            dve.wait_ge(pool_c, 3)
            for j in range(SJ):
                link(v.tensor_scalar(junk[:], cb[:, 0], s_col[:, j:j + 1], 0.0, ALU.is_le, ALU.add,
                                     accum_out=e_col[:, j:j + 1]))
            link(v.tensor_scalar(e_col[:], e_col[:], float(ET - 1), None, ALU.min))
            for j in range(SJ):
                link(v.scalar_tensor_tensor(out=junk[:], in0=iota_e[:], scalar=e_col[:, j:j + 1], in1=cb[:, 1],
                                            op0=ALU.is_equal, op1=ALU.mult, accum_out=d_col[:, j:j + 1]))
            link(v.tensor_tensor(n_col[:], s_col[:], d_col[:], ALU.subtract))
            link(v.tensor_scalar(n_col[:], n_col[:], float(NT - 1), 0.0, ALU.min, ALU.max))
            link(v.tensor_scalar(base_col[:], n_col[:], float(P), None, ALU.mult))
            link(v.tensor_copy(e_int[:], e_col[:]))
            v.tensor_copy(n_int[:], n_col[:]).then_inc(e_done, 1)
            dve.wait_ge(e_done, 1)
            dve.wait_ge(rows_in, 16 * 4 * SJ)
            cur = rows[:, 1]
            link(v.tensor_tensor(same[:, 0, :, 1:P], cur[:, :, 1:P], cur[:, :, 0:P - 1], ALU.is_equal))
            link(v.tensor_tensor(same[:, 0, :, 0:1], cur[:, :, 0:1], rows[:, 0, :, P - 1:P], ALU.is_equal))
            link(v.tensor_tensor(same[:, 1, :, P - 1:0:-1], cur[:, :, 1:P], cur[:, :, 0:P - 1], ALU.is_equal))
            link(v.tensor_tensor(same[:, 1, :, 0:1], cur[:, :, P - 1:P], rows[:, 2, :, 0:1], ALU.is_equal))
            link(v.tensor_scalar(same[:], same[:], 1.0, BIG, ALU.subtract, ALU.mult))
            for j in range(SJ):
                link(v.tensor_scalar(locf[:, j, :], cur[:, j, :], base_col[:, j:j + 1], None, ALU.subtract))
            v.tensor_copy(srcf[:], srow[:]).then_inc(flags_done, 1)
            for n in range(2 * SJ):
                dve.wait_ge(turned, n + 1)
                out = (K["loc_dst"], K["src_idx"])[n % 2]
                v.tensor_copy(out[:, (n // 2) * P:(n // 2 + 1) * P], pt[:, n % 2, 0:P]).then_inc(copied, 1)


def chain_table_phase(nc, K):
    with ExitStack() as ctx:
        m = Mem(nc, ctx)
        first = m.sb("first_loc", [1, NB])
        pf = m.ps("first_ps", [P, 512])
        dch, first_done, f_bc = m.sem("dve_ch"), m.sem("first_done"), m.sem("first_bcast")
        block = ctx.enter_context(nc.Block())

        @block.tensor
        def _(pe):
            pe.wait_ge(first_done, 1)
            nc.tensor.matmul(pf[:, 0:NB], K["ones"][0:1, :], first[:], start=True, stop=True).then_inc(f_bc, 1)

        @block.vector
        def _(dve):
            v = nc.vector
            link = Chain(dve, dch)
            v.tensor_copy(first[:], K["loc_dst"][0:1, 0:STEPS].rearrange("a (b k) -> a b k", k=SB)[:, :, 0]
                          ).then_inc(first_done, 1)
            for o, name in enumerate(("reset_fwd", "reset_bwd")):
                link(v.tensor_reduce(K["whole"][:, o, :], K[name][:], AX_X, ALU.min))
            link(v.tensor_scalar(K["goes_on"][:], K["reset_fwd"][0:1, :, 0], 0.0, None, ALU.is_equal))
            dve.wait_ge(f_bc, 1)
            link(v.tensor_scalar(K["first_node"][:], pf[:, 0:NB], K["iota_col"][:, 0:1], None, ALU.is_equal))


def mean_and_rstd(nc, dve, link, stats, mean, rstd, tmp, var_ready, std_ready, n):
    v = nc.vector
    half = stats.rearrange("p t (o c) -> p t o c", o=2)
    me, mo = half[:, :, 0, 1], half[:, :, 1, 1]
    link(v.tensor_tensor(mean, me, mo, ALU.add))
    link(v.tensor_scalar(mean, mean, 0.5, None, ALU.mult))
    link(v.tensor_tensor(tmp, me, mo, ALU.subtract))
    link(v.tensor_tensor(tmp, tmp, tmp, ALU.mult))
    link(v.tensor_scalar(tmp, tmp, D / 4.0, None, ALU.mult))
    link(v.tensor_tensor(tmp, tmp, half[:, :, 0, 2], ALU.add))
    link(v.tensor_tensor(tmp, tmp, half[:, :, 1, 2], ALU.add))
    v.tensor_scalar(rstd, tmp, 1.0 / D, None, ALU.mult).then_inc(var_ready, 1)
    dve.wait_ge(std_ready, n)
    link(v.reciprocal(rstd, rstd))


def node_phase(nc, K, dram, x, W, att):
    ZC = HEADS * HD
    CHUNKS = 5
    TC = NT // CHUNKS
    with ExitStack() as ctx:
        m = Mem(nc, ctx)
        xr = m.sb("x_all", [P, NT, D])
        stats = m.sb("stats", [P, NT, 6])
        mean, rstd, tmp = m.sb("mean", [P, NT]), m.sb("rstd", [P, NT]), m.sb("ln_tmp", [P, NT])
        w_all = m.sb("w_all", [P, 2, ZC + 2 * HEADS])
        w_in = m.sb("w_in", [P, 2, HEADS, HD])
        att_in, prod = m.sb("att_in", [1, HEADS * 2 * HD]), m.sb("att_prod", [P, 2, 2, HEADS, HD])
        xn, xT = m.sb("xn", [P, 2, D]), m.sb("xT", [P, 2, 2, P])
        zrow = m.sb("zrow", [P, 2, ROW])
        t_ps, z_ps, a_ps = m.ps("t_ps", [P, 2, 512]), m.ps("z_ps", [P, 2, 512]), m.ps("a_ps", [P, 512])

        x_in, w_s, z_out = m.sems("x_in", CHUNKS), m.sem("w_in_s"), m.sems("z_out", 2)
        dch, zch, att_bc, w_ready = m.sem("dve_n"), m.sem("dve_z"), m.sem("att_bc"), m.sem("w_ready")
        stats_done, var_ready, std_ready = m.sem("stats_done"), m.sem("var_ready"), m.sem("std_ready")
        xn_free, xn_done, xt_done, xt_copied = m.sem("xn_free"), m.sem("xn_done"), m.sem("xt_done"), m.sem("xt_cp")
        z_done, z_copied, z_free = m.sem("z_done"), m.sem("z_copied"), m.sem("z_free")
        block = ctx.enter_context(nc.Block())

        @block.sync
        def _(sp):
            for c in range(CHUNKS):
                sp.dma_start(xr[:, c * TC:(c + 1) * TC, :],
                             x[c * TC * P:(c + 1) * TC * P, :].rearrange("(t p) d -> p t d", p=P)
                             ).then_inc(x_in[c], 16)
                if c == 0:
                    for h in range(HEADS):
                        sp.dma_start(w_in[:, :, h, :], W[h].rearrange("(k p) f -> p k f", p=P)).then_inc(w_s, 16)
                    sp.dma_start(att_in[:], att.rearrange("(a h) c -> a (h c)", a=1)).then_inc(w_s, 16)
            with sp.Fori(0, NT // 2) as i:
                for u in range(2):
                    sp.wait_ge(z_copied, i * 2 + (u + 1))
                    sp.dma_start(dram["z_table"][bass.ds((i * 2 + u) * P, P), :], zrow[:, u, :]
                                 ).then_inc(z_out[u], 16)
            for u in range(2):
                sp.wait_ge(z_out[u], 16 * (NT // 2))

        @block.tensor
        def _(pe):
            pe.sem_inc(xn_free, 2)
            pe.wait_ge(w_s, 16 * (HEADS + 1))
            pe.wait_ge(K["setup"], 1)
            nc.tensor.matmul(a_ps[:], K["ones"][0:1, :], att_in[:], start=True, stop=True).then_inc(att_bc, 1)
            pe.wait_ge(w_ready, 1)
            with pe.Fori(0, NT // 2) as i:
                for u in range(2):
                    pe.wait_ge(xn_done, i * 2 + (u + 1))
                    for k in range(2):
                        mm = nc.tensor.transpose(t_ps[:, u, k * P:(k + 1) * P], xn[:, u, k * P:(k + 1) * P],
                                                 K["ident"][:])
                    mm.then_inc(xt_done, 1)
                    pe.wait_ge(xt_copied, i * 2 + (u + 1))
                    pe.wait_ge(z_free, i * 2 + (u + 1))
                    for k in range(2):
                        mm = nc.tensor.matmul(z_ps[:, u, 0:ZC + 2 * HEADS], xT[:, u, k, :], w_all[:, k, :],
                                              start=(k == 0), stop=(k == 1))
                    mm.then_inc(z_done, 1)

        @block.scalar
        def _(act):
            act.wait_ge(var_ready, 1)
            nc.scalar.activation(rstd[:], rstd[:], ACT.Sqrt, bias=K["eps"][:, 0:1]).then_inc(std_ready, 1)
            with act.Fori(0, NT // 2) as i:
                for u in range(2):
                    act.wait_ge(xt_done, i * 2 + (u + 1))
                    act.wait_ge(z_free, i * 2 + (u + 1))
                    nc.scalar.copy(xT[:, u].rearrange("p k n -> p (k n)"), t_ps[:, u, 0:2 * P]).then_inc(xt_copied, 1)

        @block.vector
        def _(dve):
            v = nc.vector
            link = Chain(dve, dch)
            dve.sem_inc(z_free, 2)
            link(v.memset(zrow[:], 1.0))
            link(v.memset(K["acc"][:], 0.0))
            dve.sem_inc(K["setup"], 1)
            dve.wait_ge(att_bc, 1)
            a4 = a_ps[:].rearrange("p (h o f) -> p o h f", h=HEADS, o=2)
            for k in range(2):
                link(v.tensor_copy(w_all[:, k, 0:ZC].rearrange("p (h f) -> p h f", h=HEADS), w_in[:, k]))
                for o in range(2):
                    link(v.tensor_tensor(prod[:, k, o], w_in[:, k], a4[:, o], ALU.mult))
                    link(v.tensor_reduce(w_all[:, k, ZC + o * HEADS:ZC + (o + 1) * HEADS], prod[:, k, o], AX_X,
                                         ALU.add))
            dve.sem_inc(w_ready, 1)
            for c in range(CHUNKS):
                dve.wait_ge(x_in[c], 16)
                with dve.Fori(c * TC, (c + 1) * TC) as t:
                    v.bn_stats(stats[:, bass.ds(t, 1), :].rearrange("p a c -> p (a c)"),
                               xr[:, bass.ds(t, 1), :].rearrange("p a c -> p (a c)")).then_inc(stats_done, 1)
            dve.wait_ge(stats_done, NT)
            mean_and_rstd(nc, dve, link, stats[:], mean[:], rstd[:], tmp[:], var_ready, std_ready, 1)

            def normalise(t, u, count):
                dve.wait_ge(xt_done, count) if count is not None else None
                v.tensor_scalar(xn[:, u], xr[:, bass.ds(t, 1), :].rearrange("p a c -> p (a c)"),
                                mean[:, bass.ds(t, 1)], rstd[:, bass.ds(t, 1)],
                                ALU.subtract, ALU.mult).then_inc(xn_done, 1)

            v.tensor_scalar(xn[:, 0], xr[:, 0, :], mean[:, 0:1], rstd[:, 0:1], ALU.subtract, ALU.mult
                            ).then_inc(xn_done, 1)
            v.tensor_scalar(xn[:, 1], xr[:, 1, :], mean[:, 1:2], rstd[:, 1:2], ALU.subtract, ALU.mult
                            ).then_inc(xn_done, 1)

            def take_rows(t, u, i):
                dve.wait_ge(z_done, t + 1)
                if i is not None:
                    dve.wait_ge(z_out[u], i * 16)
                v.tensor_copy(zrow[:, u, 0:HEADS * HB].rearrange("p (h f) -> p h f", h=HEADS)[:, :, 0:HD],
                              z_ps[:, u, 0:ZC].rearrange("p (h f) -> p h f", h=HEADS)).then_inc(zch, 1)
                v.tensor_copy(zrow[:, u, HEADS * HB:], z_ps[:, u, ZC:ZC + HEADS]).then_inc(zch, 1)
                v.tensor_copy(K["ed"][:, bass.ds(t, 1), :].rearrange("p a h -> p (a h)"),
                              z_ps[:, u, ZC + HEADS:ZC + 2 * HEADS]).then_inc(z_free, 1)
                dve.wait_ge(zch, t * 2 + 2)
                dve.sem_inc(z_copied, 1)

            for u in range(2):
                take_rows(u, u, None)
                normalise(2 + u, u, u + 1)
            with dve.Fori(1, NT // 2 - 1) as i:
                for u in range(2):
                    take_rows(i * 2 + u, u, i)
                    normalise(i * 2 + (u + 2), u, i * 2 + (u + 1))
            for u in range(2):
                take_rows(NT - 2 + u, u, NT // 2 - 1)
            dve.wait_ge(z_free, NT + 2)


def lasting(nc, ctx):
    m = Mem(nc, ctx)
    return {
        "ident": m.sb("ident", [P, P]), "iota_row": m.sb("iota_row", [P, P]), "iota_col": m.sb("iota_col", [P, 1]),
        "ones": m.sb("ones", [P, P]), "eps": m.sb("eps", [P, 1]), "setup": m.sem("setup"),
        "acc": m.sb("acc", [P, NT, HEADS * HB]),
    }


def graph_tables(nc, ctx):
    m = Mem(nc, ctx)
    return {
        "step_node": m.sb("step_node", [1, STEPS + SB], I32),
        "loc_dst": m.sb("loc_dst", [P, SP]),
        "src_idx": m.sb("src_idx", [P, SP], I32),
        "reset_fwd": m.sb("reset_fwd", [P, NB, P]),
        "reset_bwd": m.sb("reset_bwd", [P, NB, P]),
        "whole": m.sb("whole", [P, 2, NB]),
        "goes_on": m.sb("goes_on", [1, NB]), "first_node": m.sb("first_node", [P, NB]),
        "ed": m.sb("ed", [P, NT, HEADS]),
    }


def expert_buffers(nc, ctx):
    m = Mem(nc, ctx)
    return {
        "w1": m.sb("w1_all", [P, 2, E * HID]), "w2": m.sb("w2_all", [P, 4, E * D]),
        "b1": m.sb("b1_all", [P, E * HID]), "b2": m.sb("b2_all", [P, E * D]), "weights_in": m.sem("weights_in"),
        "tile_expert": m.sb("tile_expert", [1, STX], I32), "slot_w": m.sb("slot_w", [STX, P]),
        "xn_now": m.sb("xn_now", [P, 2, D]),
    }


def edge_phase(nc, K, dram):
    G4 = SB // 4
    S8 = SB // 8
    HK = HEADS * (SB + 1)
    Y = 4
    with ExitStack() as ctx:
        m = Mem(nc, ctx)
        rows = m.sb("edge_rows", [P, 2, SB, ROW])
        onehot = m.sb("onehot", [P, 2, SB, P])
        onehot_t = m.sb("onehot_t", [P, 2, 4, P])
        idx = m.sb("edge_idx", [P, 2, SB], I32)
        sc, sc2 = m.sb("scores", [P, HEADS, SB]), m.sb("scores2", [P, HEADS, SB])
        fwd, bwd, top = m.sb("fwd", [P, P]), m.sb("bwd", [P, P]), m.sb("top", [P, P])
        ends = m.sb("chain_in", [1, 2, 2, HK])
        chain = m.sb("chain_max", [1, 2, HK])
        enter = m.sb("chain_enter", [1, 2, P])
        init = m.sb("chain_init", [P, 2])
        mx4, dl4, g4 = m.sb("mx4", [1, HEADS]), m.sb("dl4", [1, HEADS]), m.sb("g4", [1, HEADS])
        node_scale = m.sb("node_scale", [P, HEADS])
        whole_now = m.sb("whole_now", [P, 2])
        wt = m.sb("weights", [P, 2, HEADS, SB])
        y = m.sb("weighted", [P, Y, HEADS * HB])
        t_ps, ed_ps, e_ps = m.ps("oh_ps", [P, 2, 512]), m.ps("ed_ps", [P, 512]), m.ps("e_ps", [P, 512])
        small, out_ps = m.ps("small_ps", [P, 512]), m.ps("out_ps", [P, 2, 512])

        gath, rows_free, idx_c = m.sems("gathered", 2), m.sem("rows_free"), m.sem("idx_copied")
        issuing = m.sem("edge_gathers_issuing")
        oh_built, oh_free, oht_ps, oht_sb, oht_free = (m.sem("oh_built"), m.sem("oh_free"), m.sem("oht_ps"),
                                                       m.sem("oht_sb"), m.sem("oht_free"))
        ed_done, dch = m.sem("ed_done"), m.sem("dve_edge")
        sc_ready, sc_turned, ends_ready, ends_turned = (m.sem("sc_ready"), m.sem("sc_turned"), m.sem("ends_ready"),
                                                        m.sem("ends_turned"))
        chain_ready, init_done, dl_ready, g_done, enter_ready = (m.sem("chain_ready"), m.sem("init_done"), m.sem("dl_ready"),
                                                    m.sem("g_done"), m.sem("enter_ready"))
        gm_ready, gm_bc, x_ready, x_turned, w_done = (m.sem("gm_ready"), m.sem("gm_bc"), m.sem("x_ready"),
                                                      m.sem("x_turned"), m.sem("w_done"))
        y_ready, mm_done, acc_done = m.sem("y_ready"), m.sem("mm_done"), m.sem("acc_done")
        sums_ok = m.sem("sums_ok")
        block = ctx.enter_context(nc.Block())

        def heads(ap):
            return ap.rearrange("a (h k) -> a h k", h=HEADS)

        @block.gpsimd
        def _(pool):
            pool.sem_inc(rows_free, 2)
            with pool.Fori(0, NB // 2) as i:
                for u in range(2):
                    pool.wait_ge(rows_free, i * 2 + (u + 1))
                    nc.gpsimd.tensor_copy(idx[:, u], K["src_idx"][:, bass.ds(i * (2 * SB) + u * SB, SB)]
                                          ).then_inc(idx_c, 1)
                    pool.wait_ge(idx_c, i * 2 + (u + 1))
                    pool.sem_inc(issuing, 1)
                    for k in range(SB):
                        nc.gpsimd.indirect_dma_start(
                            out=rows[:, u, k, :], out_offset=None, in_=dram["z_table"],
                            in_offset=bass.IndirectOffsetOnAxis(ap=idx[:, u, k:k + 1], axis=0)
                        ).then_inc(gath[u], 16)

        @block.tensor
        def _(pe):
            ident = K["ident"][:]
            pe.sem_inc(oht_free, 2)
            pe.sem_inc(oh_free, 2)

            def turn_group(b, u, g):
                pe.wait_ge(oh_built, b * S8 + (g // 2 + 1))
                for q in range(4):
                    mm = nc.tensor.transpose(t_ps[:, g % 2, q * P:(q + 1) * P], onehot[:, u, g * 4 + q, :], ident)
                mm.then_inc(oht_ps, 1)

            def dst_scores(b, g, node):
                pe.wait_ge(oht_sb, b * G4 + (g + 1))
                for q in range(4):
                    k = g * 4 + q
                    mm = nc.tensor.matmul(ed_ps[:, k * HEADS:(k + 1) * HEADS], onehot_t[:, g % 2, q, :],
                                          K["ed"][:, bass.ds(node[k % 8], 1), :].rearrange("p a h -> p (a h)"),
                                          start=True, stop=True)
                mm.then_inc(ed_done, 1)

            def nodes_of(b, g):
                return nc.values_load_multi_w_load_instructions(
                    K["step_node"][0:1, bass.ds(b * SB + g * 4, 8)], engines=PE_ONLY, min_val=0,
                    max_val=NT - 1, skip_runtime_bounds_check_because=WHY_IN_RANGE)[1]

            pe.sem_inc(mm_done, Y)
            node = None
            for g in range(G4):
                turn_group(0, 0, g)
                if g % 2 == 0:
                    node = nodes_of(0, g)
                dst_scores(0, g, node)
            with pe.Fori(0, NB // 2) as i:
                for u in range(2):
                    b = i * 2 + u
                    pe.wait_ge(sc_ready, b + 1)
                    nc.tensor.transpose(e_ps[:, 0:P], sc[:].rearrange("p h k -> p (h k)"), ident).then_inc(sc_turned, 1)
                    pe.wait_ge(ends_ready, b * 2 + 2)
                    for o, col in enumerate((fwd[:, P - 1:P], bwd[:, 0:1])):
                        nc.tensor.transpose(small[0:1, 2 * o * P:(2 * o + 1) * P], col, ident)
                        mm = nc.tensor.transpose(small[0:1, (2 * o + 1) * P:(2 * o + 2) * P], whole_now[:, o:o + 1],
                                                 ident)
                    mm.then_inc(ends_turned, 1)
                    pe.wait_ge(enter_ready, b * 2 + 2)
                    for o in range(2):
                        mm = nc.tensor.matmul(small[:, o:o + 1], enter[0:1, o], K["ones"][0:1, 0:1], start=True,
                                              stop=True)
                    mm.then_inc(init_done, 1)
                    pe.wait_ge(gm_ready, b + 1)
                    nc.tensor.matmul(small[:, 0:HEADS], K["ones"][0:1, :], g4[:], start=True, stop=True
                                     ).then_inc(gm_bc, 1)
                    pe.wait_ge(x_ready, b + 1)
                    nc.tensor.transpose(e_ps[:, 0:P], top[:], ident).then_inc(x_turned, 1)
                    for g in range(G4):
                        for q in range(4):
                            k = g * 4 + q
                            pe.wait_ge(y_ready, b * SB + (k + 1))
                            if k:
                                pe.wait_ge(sums_ok, b * SB + k)
                            nc.tensor.matmul(out_ps[:, u, 0:HEADS * HB], onehot[:, u, k, :], y[:, k % Y],
                                             start=(k == 0), stop=True, skip_group_check=True).then_inc(mm_done, 1)
                        if g:
                            dst_scores(b + 1, g - 1, node)
                        if g % 2 == 0:
                            node = nodes_of(b + 1, g)
                        turn_group(b + 1, 1 - u, g)
                    dst_scores(b + 1, G4 - 1, node)

        @block.scalar
        def _(act):
            def copy_turned(b, groups):
                for g in groups:
                    act.wait_ge(oht_ps, b * G4 + (g + 1))
                    act.wait_ge(ed_done, b * G4 + (g - 1)) if not isinstance(b, int) else (
                        act.wait_ge(ed_done, g - 1) if g >= 2 else None)
                    nc.scalar.copy(onehot_t[:, g % 2].rearrange("p q n -> p (q n)"), t_ps[:, g % 2, :]
                                   ).then_inc(oht_sb, 1)

            copy_turned(0, range(G4))
            with act.Fori(0, NB // 2) as i:
                for u in range(2):
                    b = i * 2 + u
                    act.wait_ge(dl_ready, b + 1)
                    nc.scalar.activation(g4[:], dl4[:], ACT.Exp).then_inc(g_done, 1)
                    act.wait_ge(x_turned, b + 1)
                    nc.scalar.activation(wt[:, u].rearrange("p h k -> p (h k)"), e_ps[:, 0:P], ACT.Exp
                                         ).then_inc(w_done, 1)
                    copy_turned(b + 1, range(G4))

        @block.vector
        def _(dve):
            v = nc.vector
            PER = 26

            def build_onehots(b, u, groups):
                for g in groups:
                    loc = K["loc_dst"][:, bass.ds(b * SB + g * 8, 8)]
                    v.tensor_tensor(onehot[:, u, g * 8:(g + 1) * 8, :],
                                    loc.unsqueeze(2).broadcast_to([P, 8, P]),
                                    K["iota_row"][:].unsqueeze(1).broadcast_to([P, 8, P]),
                                    ALU.is_equal).then_inc(oh_built, 1)

            start = Chain(dve, dch)
            start(v.memset(ends[:], -BIG))
            dve.sem_inc(acc_done, 1)
            build_onehots(0, 0, range(S8))
            with dve.Fori(0, NB // 2) as i:
                for u in range(2):
                    b = i * 2 + u
                    link = Chain(dve, dch, i * (2 * PER) + (u * PER + 1))
                    link(v.tensor_copy(whole_now[:], K["whole"][:, :, bass.ds(b, 1)].rearrange("p o b -> p (o b)")))
                    dve.wait_ge(ed_done, b * G4 + G4)
                    dve.wait_ge(gath[u], i * (16 * SB) + 16 * SB)
                    es = rows[:, u, :, HEADS * HB:ROW].rearrange("p k h -> p h k")
                    link(v.tensor_tensor(sc2[:], ed_ps[:, 0:P].rearrange("p (k h) -> p h k", h=HEADS), es, ALU.add))
                    link(v.scalar_tensor_tensor(out=sc[:], in0=sc2[:], scalar=SLOPE, in1=sc2[:], op0=ALU.mult,
                                                op1=ALU.max))
                    link(v.tensor_scalar(sc2[:], sc[:], 0.0, NEG, ALU.is_equal, ALU.mult))
                    v.tensor_tensor(sc[:], sc[:], sc2[:], ALU.add).then_inc(sc_ready, 1)
                    dve.wait_ge(sc_turned, b + 1)
                    rf = K["reset_fwd"][:, bass.ds(b, 1), :].rearrange("p a i -> p (a i)")
                    rb = K["reset_bwd"][:, bass.ds(b, 1), :].rearrange("p a i -> p (a i)")
                    v.tensor_tensor_scan(fwd[:], rf, e_ps[:, 0:P], -BIG, ALU.add, ALU.max).then_inc(ends_ready, 1)
                    v.tensor_tensor_scan(bwd[:, ::-1], rb, e_ps[:, 0:P][:, ::-1],
                                         -BIG, ALU.add, ALU.max).then_inc(ends_ready, 1)
                    dve.wait_ge(ends_turned, b + 1)
                    for o in range(2):
                        link(v.tensor_copy(
                            ends[0:1, o].rearrange("a x (h k) -> a (x h) k", h=HEADS)[:, :, 1 - o:1 - o + SB],
                            small[0:1, 2 * o * P:(2 * o + 2) * P].rearrange("a (x k) -> a x k", k=SB)))
                    v.tensor_tensor_scan(chain[0:1, 0], ends[0:1, 0, 1], ends[0:1, 0, 0], -BIG, ALU.add, ALU.max
                                         ).then_inc(chain_ready, 1)
                    v.tensor_tensor_scan(chain[0:1, 1, ::-1], ends[0:1, 1, 1, ::-1], ends[0:1, 1, 0, ::-1], -BIG,
                                         ALU.add, ALU.max).then_inc(chain_ready, 1)
                    dve.wait_ge(chain_ready, b * 2 + 2)
                    for o in range(2):
                        v.tensor_copy(heads(enter[0:1, o]), heads(chain[0:1, o])[:, :, o:o + SB]
                                      ).then_inc(enter_ready, 1)
                    carry = heads(ends[0:1, 0, 0])[:, :, 0]
                    link(v.tensor_tensor(mx4[:], carry, heads(chain[0:1, 1])[:, :, 0], ALU.max))
                    link(v.tensor_tensor(dl4[:], carry, mx4[:], ALU.subtract))
                    v.tensor_scalar(dl4[:], dl4[:], K["goes_on"][:, bass.ds(b, 1)], None, ALU.mult
                                    ).then_inc(dl_ready, 1)
                    link(v.tensor_copy(carry, heads(chain[0:1, 0])[:, :, SB]))
                    dve.wait_ge(init_done, b + 1)
                    link(v.tensor_copy(init[:], small[:, 0:2]))
                    v.tensor_tensor_scan(fwd[:], rf, e_ps[:, 0:P], init[:, 0:1], ALU.add, ALU.max).then_inc(dch, 1)
                    link.n += 1
                    link(v.tensor_tensor_scan(bwd[:, ::-1], rb, e_ps[:, 0:P][:, ::-1], init[:, 1:2], ALU.add, ALU.max))
                    dve.wait_ge(g_done, b + 1)
                    v.tensor_scalar(g4[:], g4[:], 1.0, None, ALU.subtract).then_inc(gm_ready, 1)
                    link(v.tensor_tensor(top[:], fwd[:], bwd[:], ALU.max))
                    v.tensor_tensor(top[:], e_ps[:, 0:P], top[:], ALU.subtract).then_inc(x_ready, 1)
                    dve.wait_ge(gm_bc, b + 1)
                    link(v.tensor_scalar(node_scale[:], small[:, 0:HEADS], K["first_node"][:, bass.ds(b, 1)], 1.0,
                                         ALU.mult, ALU.add))
                    dve.wait_ge(w_done, b + 1)
                    for k in range(SB + 1):
                        if k < SB:
                            dve.wait_ge(mm_done, b * SB + (k + 1))
                            v.tensor_tensor(y[:, k % Y].rearrange("p (h f) -> p h f", h=HEADS),
                                            rows[:, u, k, 0:HEADS * HB].rearrange("p (h f) -> p h f", h=HEADS),
                                            wt[:, u, :, k:k + 1].broadcast_to([P, HEADS, HB]), ALU.mult
                                            ).then_inc(y_ready, 1)
                        j = k - 1
                        if j >= 0 and j % 8 == 0 or k == 0:
                            first = max(j, 0)
                            if k == 0 or j:
                                _, nodes = nc.values_load_multi_w_load_instructions(
                                    K["step_node"][0:1, bass.ds(b * SB + first, 9)], engines=DVE_ONLY, min_val=0,
                                    max_val=NT - 1, skip_runtime_bounds_check_because=WHY_IN_RANGE)
                        sums = K["acc"][:, bass.ds(nodes[max(j, 0) % 8], 1), :]
                        flat = sums.rearrange("p a f -> p (a f)")
                        if k == 0:
                            dve.wait_ge(acc_done, b + 1)
                            link(v.tensor_tensor(sums.rearrange("p a (h f) -> p (a h) f", h=HEADS),
                                                 sums.rearrange("p a (h f) -> p (a h) f", h=HEADS),
                                                 node_scale[:].unsqueeze(2).broadcast_to([P, HEADS, HB]), ALU.mult))
                        elif k < SB:
                            with dve.If(nodes[j % 8] != nodes[j % 8 + 1]):
                                dve.wait_ge(mm_done, b * SB + (j + 1 + Y))
                                v.tensor_tensor(flat, out_ps[:, u, 0:HEADS * HB], flat, ALU.add)
                                dve.drain()
                                v.memset(out_ps[:, u, 0:HEADS * HB], 0.0)
                                dve.drain().then_inc(sums_ok, 1)
                            with dve.Else():
                                dve.sem_inc(sums_ok, 1)
                        else:
                            dve.wait_ge(mm_done, b * SB + (SB + Y))
                            v.tensor_tensor(flat, out_ps[:, u, 0:HEADS * HB], flat, ALU.add).then_inc(acc_done, 1)
                            dve.sem_inc(sums_ok, 1)
                            dve.sem_inc(rows_free, 1)
                        if k % 8 == 0 and k < SB:
                            build_onehots(b + 1, 1 - u, range(k // 8, k // 8 + 1))
                    while link.n < PER:
                        link.n += 1
                        dve.sem_inc(dch, 1)
            dve.wait_ge(acc_done, NB + 1)


def token_phase(nc, K, M, dram, x, gamma, beta, Wr, br, W1, b1, W2, b2, out):
    CHUNKS = 10
    TC = NT // CHUNKS
    NR = NT * E
    KT = TOPK * NT
    acc, table = K["acc"], dram["slot_table"]
    with ExitStack() as ctx:
        m = Mem(nc, ctx)
        xin = m.sb("x_chunk", [P, 2, TC, D])
        stats, mean, rstd, tmp = (m.sb("stats2", [P, NT, 6]), m.sb("mean2", [P, NT]), m.sb("rstd2", [P, NT]),
                                  m.sb("ln_tmp2", [P, NT]))
        den, den2 = m.sb("den", [P, NT, HEADS]), m.sb("den2", [P, NT, HEADS])
        att = m.sb("att_out", [P, 2, D])
        gam, bet, br_b = m.sb("gamma_b", [P, D]), m.sb("beta_b", [P, D]), m.sb("br_b", [P, E])
        wr = m.sb("wr", [P, 2, E])
        xT = m.sb("xT2", [P, 2, 2, P])
        lg, lg2 = m.sb("logits", [P, NT, E]), m.sb("logits2", [P, NT, E])
        iota_e, valid = m.sb("iota_expert", [P, E]), m.sb("valid", [P, NT])
        tok_f, tok_i = m.sb("token_f", [P, NT]), m.sb("token_i", [P, NT], I32)
        best, which = m.sb("best", [P, TOPK, NT]), m.sb("which", [P, TOPK, NT])
        oh, cand = m.sb("expert_oh", [P, TOPK, NT, E]), m.sb("cand", [P, NT, E])
        tot, inc, keep = m.sb("tot", [P, E, KT]), m.sb("inc", [P, E, KT]), m.sb("keep", [P, E, KT])
        jt, gt = m.sb("jt", [P, ST_]), m.sb("gt", [P, E, ST_])
        ntl, ctl, base = m.sb("ntiles", [P, E]), m.sb("cum_tiles", [P, E]), m.sb("slot_base", [P, E])
        rank = m.sb("rank", [P, TOPK, NT, E])
        pos, pos_i = m.sb("pos", [P, TOPK, NT]), m.sb("pos_i", [P, NT, TOPK], I32)
        wgt, pay = m.sb("wgt", [P, TOPK, NT]), m.sb("payload", [P, NT, TOPK, 2], I32)
        pay_now, pos_now = m.sb("pay_now", [P, 2, TOPK, 2], I32), m.sb("pos_now", [P, 2, TOPK], I32)
        before = m.sb("before", [P, P])
        blank = m.sb("blank_slots", [STX, P, 2], I32)
        exp_f = m.sb("tile_expert_f", [1, STX, E])
        jrow = m.sb("tile_row", [1, STX])
        exp_s = m.sb("tile_expert_s", [1, STX])
        t_ps, l_ps, r_ps = m.ps("t2_ps", [P, 2, 512]), m.ps("l_ps", [P, 2, 512]), m.ps("r_ps", [P, 4, 512])

        small_in, w_in, x_in, x_used = m.sem("small_in"), M["weights_in"], m.sems("x2_in", 2), m.sem("x_used")
        dch, x1_done, x1_out, made = m.sem("dve_t"), m.sem("x1_done"), m.sem("x1_out"), m.sem("made")
        st_done, var_ready, std_ready, ach = m.sem("st_done"), m.sem("var2"), m.sem("std2"), m.sem("att_ch")
        xn_out, xt_done, xt_cp = m.sems("xn2_out", 2), m.sem("xt2_done"), m.sem("xt2_cp")
        l_done, l_free, ex_in, ex_out = m.sem("l_done"), m.sem("l_free"), m.sem("ex_in"), m.sem("ex_out")
        oh_done, r_done, blank_out, pay_done = (m.sem("oh_done"), m.sem("r_done"), m.sem("blank_out"),
                                                m.sem("pay_done"))
        issuing = m.sem("slot_scatters_issuing")
        now_c, scat, gb, norm_c = m.sem("now_c"), m.sems("scattered", 2), m.sem("gb"), m.sem("norm_c")
        block = ctx.enter_context(nc.Block())

        def tile(t):
            return acc[:, bass.ds(t, 1), 0:D].rearrange("p a f -> p (a f)")

        @block.sync
        def _(sp):
            for u in range(2):
                sp.dma_start(xin[:, u], x[u * TC * P:(u + 1) * TC * P, :].rearrange("(t p) d -> p t d", p=P)
                             ).then_inc(x_in[u], 16)
            for o, a in ((gam, gamma), (bet, beta), (br_b, br)):
                sp.dma_start(o[:], a.rearrange("(o d) -> o d", o=1).broadcast_to([P, a.shape[0]])
                             ).then_inc(small_in, 16)
            sp.dma_start(wr[:], Wr.rearrange("(k p) e -> p k e", p=P)).then_inc(small_in, 16)
            for c in range(2, CHUNKS):
                sp.wait_ge(x_used, (c - 1) * TC)
                sp.dma_start(xin[:, c % 2], x[c * TC * P:(c + 1) * TC * P, :].rearrange("(t p) d -> p t d", p=P)
                             ).then_inc(x_in[c % 2], 16)
            sp.wait_ge(made, 1)
            sp.dma_start(table[0:STX * P, :].rearrange("(t p) c -> t (p c)", p=P),
                         blank[:].rearrange("t p c -> t (p c)")).then_inc(blank_out, 16)
            for c in range(CHUNKS):
                sp.wait_ge(x_used, (c + 1) * TC)
                sp.dma_start(out[c * TC * P:(c + 1) * TC * P, :].rearrange("(t p) d -> p t d", p=P),
                             acc[:, c * TC:(c + 1) * TC, 0:D]).then_inc(x1_out, 16)
            with sp.Fori(0, NT // 2) as i:
                for u in range(2):
                    sp.wait_ge(norm_c, i * 2 + (u + 1))
                    sp.dma_start(dram["xn"][bass.ds((i * 2 + u) * P, P), :], M["xn_now"][:, u]).then_inc(xn_out[u], 16)
            for u in range(2):
                sp.wait_ge(xn_out[u], 16 * (NT // 2))
            sp.wait_ge(x1_out, 16 * CHUNKS)
            sp.wait_ge(blank_out, 16)

        @block.gpsimd
        def _(pool):
            g = nc.gpsimd
            link = Chain(pool, gb)
            kw = dict(allow_small_or_imprecise_dtypes=True)
            link(g.iota(blank[:, :, 0], pattern=[[1, P]], base=PAD_ROW, channel_multiplier=0))
            link(g.memset(blank[:, :, 1], 0))
            pool.sem_inc(made, 1)
            link(g.iota(iota_e[:], pattern=[[1, E]], base=0, channel_multiplier=0, **kw))
            link(g.iota(tok_f[:], pattern=[[P, NT]], base=0, channel_multiplier=1, **kw))
            link(g.iota(tok_i[:], pattern=[[P, NT]], base=0, channel_multiplier=1))
            link(g.iota(jt[:], pattern=[[P, ST_]], base=0, channel_multiplier=0, **kw))
            link(g.iota(jrow[:], pattern=[[1, STX]], base=0, channel_multiplier=0, **kw))
            link(g.memset(keep[:], 1.0))
            link(g.memset(keep[:, :, 0:1], 0.0))
            link(g.affine_select(out=before[:], in_=K["ones"][:], compare_op=ALU.is_gt, fill=0.0, base=0,
                                 pattern=[[1, P]], channel_multiplier=-1))
            pool.sem_inc(made, 1)
            pool.wait_ge(pay_done, 1)
            pool.wait_ge(blank_out, 16)

            def scatter_pair(i):
                for u in range(2):
                    if not isinstance(i, int):
                        pool.wait_ge(scat[u], i * (16 * TOPK))
                    g.tensor_copy(pay_now[:, u].rearrange("p k c -> p (k c)"),
                                  pay[:, bass.ds(i * 2 + u, 1)].rearrange("p a k c -> p (a k c)")).then_inc(now_c, 1)
                    g.tensor_copy(pos_now[:, u], pos_i[:, bass.ds(i * 2 + u, 1)].rearrange("p a k -> p (a k)")
                                  ).then_inc(now_c, 1)
                    pool.wait_ge(now_c, i * 4 + (2 * u + 2))
                    pool.sem_inc(issuing, 1)
                    for k in range(TOPK):
                        g.indirect_dma_start(out=table, in_=pay_now[:, u, k, :], in_offset=None,
                                             out_offset=bass.IndirectOffsetOnAxis(ap=pos_now[:, u, k:k + 1], axis=0)
                                             ).then_inc(scat[u], 16)

            scatter_pair(0)
            with pool.Fori(1, NT // 2) as i:
                scatter_pair(i)
            for u in range(2):
                pool.wait_ge(scat[u], 16 * TOPK * (NT // 2))

        @block.tensor
        def _(pe):
            pe.wait_ge(small_in, 64)
            with pe.Fori(0, NT // 2) as i:
                for u in range(2):
                    pe.wait_ge(norm_c, i * 2 + (u + 1))
                    for k in range(2):
                        mm = nc.tensor.transpose(t_ps[:, u, k * P:(k + 1) * P], M["xn_now"][:, u, k * P:(k + 1) * P],
                                                 K["ident"][:])
                    mm.then_inc(xt_done, 1)
                    pe.wait_ge(xt_cp, i * 2 + (u + 1))
                    pe.wait_ge(l_free, i * 2 + (u + 1))
                    for k in range(2):
                        mm = nc.tensor.matmul(l_ps[:, u, 0:E], xT[:, u, k, :], wr[:, k, :], start=(k == 0),
                                              stop=(k == 1))
                    mm.then_inc(l_done, 1)
            pe.wait_ge(oh_done, 1)
            pe.wait_ge(made, 2)
            for k in range(TOPK):
                rhs = oh[:, k].rearrange("p t e -> p (t e)")
                nc.tensor.matmul(r_ps[:, k, 0:NR], before[:], rhs, start=True, stop=True)
                mm = nc.tensor.matmul(r_ps[:, 2 + k, 0:NR], K["ones"][:], rhs, start=True, stop=True)
            mm.then_inc(r_done, 1)

        @block.scalar
        def _(act):
            for k in range(2):
                act.dma_start(M["w1"][:, k].rearrange("p (e h) -> p e h", e=E),
                              W1[:, k * P:(k + 1) * P, :].rearrange("e p h -> p e h")).then_inc(w_in, 16)
            for k in range(4):
                act.dma_start(M["w2"][:, k].rearrange("p (e h) -> p e h", e=E),
                              W2[:, k * P:(k + 1) * P, :].rearrange("e p h -> p e h")).then_inc(w_in, 16)
            act.dma_start(M["b1"][:], b1.rearrange("(o e) h -> o (e h)", o=1).broadcast_to([P, E * HID])
                          ).then_inc(w_in, 16)
            act.dma_start(M["b2"][:], b2.rearrange("(o e) h -> o (e h)", o=1).broadcast_to([P, E * D])
                          ).then_inc(w_in, 16)
            for n in range(2):
                act.wait_ge(var_ready, n + 1)
                nc.scalar.activation(rstd[:], rstd[:], ACT.Sqrt, bias=K["eps"][:, 0:1]).then_inc(std_ready, 1)
            with act.Fori(0, NT // 2) as i:
                for u in range(2):
                    act.wait_ge(xt_done, i * 2 + (u + 1))
                    act.wait_ge(l_free, i * 2 + (u + 1))
                    nc.scalar.copy(xT[:, u].rearrange("p k n -> p (k n)"), t_ps[:, u, 0:2 * P]).then_inc(xt_cp, 1)
            act.wait_ge(ex_in, 1)
            nc.scalar.activation(wgt[:, 1, :], wgt[:, 1, :], ACT.Exp).then_inc(ex_out, 1)
            act.wait_ge(w_in, 16 * 8)

        @block.vector
        def _(dve):
            v = nc.vector
            link = Chain(dve, dch)
            dve.sem_inc(l_free, 2)
            d_in = acc[:].rearrange("p t (h f) -> p t h f", h=HEADS)[:, :, :, HD]
            link(v.tensor_scalar(den2[:], d_in, 0.0, None, ALU.is_le))
            link(v.tensor_tensor(den[:], d_in, den2[:], ALU.add))
            link(v.reciprocal(den[:], den[:]))
            for c in range(CHUNKS):
                dve.wait_ge(x_in[c % 2], 16 * (c // 2 + 1))
                with dve.Fori(0, TC) as i:
                    t = i + c * TC
                    a = acc[:, bass.ds(t, 1), :].rearrange("p a (h f) -> p (a h) f", h=HEADS)
                    v.tensor_tensor(att[:, 0].rearrange("p (h f) -> p h f", h=HEADS), a[:, :, 0:HD],
                                    den[:, bass.ds(t, 1), :].rearrange("p a h -> p (a h)").unsqueeze(2)
                                    .broadcast_to([P, HEADS, HD]), ALU.mult).then_inc(ach, 1)
                    dve.wait_ge(ach, t + 1)
                    v.tensor_tensor(tile(t), att[:, 0], xin[:, c % 2, bass.ds(i, 1), :].rearrange("p a d -> p (a d)"),
                                    ALU.add).then_inc(x_used, 1)
                    dve.wait_ge(x_used, t + 1)
                    v.bn_stats(stats[:, bass.ds(t, 1), :].rearrange("p a c -> p (a c)"), tile(t)).then_inc(st_done, 1)
            dve.wait_ge(st_done, NT)
            mean_and_rstd(nc, dve, link, stats[:], mean[:], rstd[:], tmp[:], var_ready, std_ready, 1)
            dve.wait_ge(x1_out, 16 * CHUNKS)
            with dve.Fori(0, NT) as t:
                v.tensor_scalar(tile(t), tile(t), mean[:, bass.ds(t, 1)], rstd[:, bass.ds(t, 1)],
                                ALU.subtract, ALU.mult).then_inc(ach, 1)
                dve.wait_ge(ach, t + (NT + 1))
                v.bn_stats(stats[:, bass.ds(t, 1), :].rearrange("p a c -> p (a c)"), tile(t)).then_inc(st_done, 1)
            dve.wait_ge(st_done, 2 * NT)
            mean_and_rstd(nc, dve, link, stats[:], mean[:], rstd[:], tmp[:], var_ready, std_ready, 2)
            dve.wait_ge(small_in, 64)

            def normalise(t, u):
                xn = M["xn_now"][:, u]
                v.tensor_scalar(xn, tile(t), mean[:, bass.ds(t, 1)], rstd[:, bass.ds(t, 1)],
                                ALU.subtract, ALU.mult).then_inc(ach, 1)
                dve.wait_ge(ach, t * 2 + (2 * NT + 1))
                v.tensor_tensor(xn, xn, gam[:], ALU.mult).then_inc(ach, 1)
                dve.wait_ge(ach, t * 2 + (2 * NT + 2))
                v.tensor_tensor(xn, xn, bet[:], ALU.add).then_inc(norm_c, 1)

            def take_logits(t, u):
                dve.wait_ge(l_done, t + 1)
                v.tensor_tensor(lg[:, bass.ds(t, 1), :].rearrange("p a e -> p (a e)"), l_ps[:, u, 0:E], br_b[:],
                                ALU.add).then_inc(l_free, 1)

            for u in range(2):
                normalise(u, u)
            with dve.Fori(0, NT // 2 - 1) as i:
                for u in range(2):
                    take_logits(i * 2 + u, u)
                    dve.wait_ge(xn_out[u], i * 16 + 16)
                    normalise(i * 2 + (2 + u), u)
            for u in range(2):
                take_logits(NT - 2 + u, u)
            dve.wait_ge(l_free, NT + 2)
            dve.wait_ge(made, 2)
            ie = iota_e[:].unsqueeze(1).broadcast_to([P, NT, E])
            link(v.tensor_scalar(valid[:], tok_f[:], float(N_NODES), None, ALU.is_lt))
            for k in range(TOPK):
                src_l = (lg, lg2)[k]
                bk, wk = best[:, k].unsqueeze(2), which[:, k].unsqueeze(2)
                link(v.tensor_reduce(best[:, k], src_l[:], AX_X, ALU.max))
                link(v.tensor_tensor(cand[:], src_l[:], bk.broadcast_to([P, NT, E]), ALU.is_equal))
                link(v.tensor_scalar(cand[:], cand[:], 1.0, -float(E), ALU.subtract, ALU.mult))
                link(v.tensor_tensor(cand[:], cand[:], ie, ALU.add))
                link(v.tensor_reduce(which[:, k], cand[:], AX_X, ALU.min))
                link(v.tensor_tensor(oh[:, k], ie, wk.broadcast_to([P, NT, E]), ALU.is_equal))
                if k == 0:
                    link(v.tensor_scalar(cand[:], oh[:, 0], -BIG, None, ALU.mult))
                    link(v.tensor_tensor(lg2[:], lg[:], cand[:], ALU.add))
                link(v.tensor_tensor(oh[:, k], oh[:, k], valid[:].unsqueeze(2).broadcast_to([P, NT, E]), ALU.mult))
            dve.sem_inc(oh_done, 1)
            v.tensor_tensor(wgt[:, 1, :], best[:, 1, :], best[:, 0, :], ALU.subtract).then_inc(ex_in, 1)
            dve.wait_ge(ex_out, 1)
            link(v.tensor_scalar(wgt[:, 0, :], wgt[:, 1, :], 1.0, None, ALU.add))
            link(v.reciprocal(wgt[:, 0, :], wgt[:, 0, :]))
            link(v.tensor_tensor(wgt[:, 1, :], wgt[:, 1, :], wgt[:, 0, :], ALU.mult))
            dve.wait_ge(r_done, 1)
            for k in range(TOPK):
                link(v.tensor_copy(tot[:, :, k * NT:(k + 1) * NT],
                                   r_ps[:, 2 + k, 0:NR].rearrange("p (t e) -> p e t", e=E)))
            fl = "p e s -> p (e s)"
            link(v.tensor_tensor_scan(inc[:].rearrange(fl), keep[:].rearrange(fl), tot[:].rearrange(fl), 0.0,
                                      ALU.mult, ALU.add))
            link(v.tensor_tensor(gt[:], inc[:, :, KT - 1:KT].broadcast_to([P, E, ST_]),
                                 jt[:].unsqueeze(1).broadcast_to([P, E, ST_]), ALU.is_gt))
            link(v.tensor_reduce(ntl[:], gt[:], AX_X, ALU.add))
            link(v.tensor_tensor_scan(ctl[:], K["ones"][:, 0:E], ntl[:], 0.0, ALU.mult, ALU.add))
            link(v.tensor_tensor(base[:], ctl[:], ntl[:], ALU.subtract))
            link(v.tensor_scalar(base[:], base[:], float(P), None, ALU.mult))
            link(v.tensor_tensor(inc[:], inc[:], tot[:], ALU.subtract))
            link(v.tensor_tensor(inc[:], inc[:], base[:].unsqueeze(2).broadcast_to([P, E, KT]), ALU.add))
            for k in range(TOPK):
                link(v.tensor_tensor(rank[:, k], r_ps[:, k, 0:NR].rearrange("p (t e) -> p t e", e=E),
                                     inc[:, :, k * NT:(k + 1) * NT].rearrange("p e t -> p t e"), ALU.add))
            link(v.tensor_tensor(rank[:], rank[:], oh[:], ALU.mult))
            link(v.tensor_reduce(pos[:], rank[:], AX_X, ALU.add))
            link(v.tensor_scalar(tmp[:], valid[:], 0.0, None, ALU.is_equal))
            link(v.tensor_scalar(mean[:], tok_f[:], float(STX * P - (NT - 2) * P), None, ALU.add))
            link(v.tensor_tensor(mean[:], mean[:], tmp[:], ALU.mult))
            link(v.tensor_scalar(tmp[:], tmp[:], 2.0 * P, None, ALU.mult))
            for k in range(TOPK):
                if k:
                    link(v.tensor_tensor(mean[:], mean[:], tmp[:], ALU.add))
                link(v.tensor_tensor(pos_i[:, :, k], pos[:, k], mean[:], ALU.add))
                link(v.tensor_copy(pay[:, :, k, 0], tok_i[:]))
                link(v.tensor_copy(pay[:, :, k, 1].bitcast(F32), wgt[:, k]))
            dve.sem_inc(pay_done, 1)
            link(v.tensor_tensor(exp_f[:], ctl[0:1].unsqueeze(1).broadcast_to([1, STX, E]),
                                 jrow[:].unsqueeze(2).broadcast_to([1, STX, E]), ALU.is_le))
            link(v.tensor_reduce(exp_s[:], exp_f[:], AX_X, ALU.add))
            link(v.tensor_scalar(M["tile_expert"][:], exp_s[:], float(E - 1), None, ALU.min))


def expert_phase(nc, K, M, dram, out):
    table = dram["slot_table"]
    with ExitStack() as ctx:
        m = Mem(nc, ctx)
        raw, rawf = m.sb("slots", [STX, P, 2], I32), m.sb("slot_tok_f", [STX, P])
        tok, wgt = m.sb("slot_token", [P, STX], I32), m.sb("slot_weight", [P, STX])
        g_idx, s_idx = m.sb("gather_idx", [P, XB], I32), m.sb("scatter_idx", [P, XB], I32)
        xg, xT = m.sb("xg", [P, XB, D]), m.sb("xgT", [P, 2, 2, P])
        hb, hg, hT = m.sb("h_biased", [P, 2, HID]), m.sb("h_gelu", [P, 2, HID]), m.sb("hT", [P, 2, 4, P])
        ysb = m.sb("y_out", [P, XB, D])
        x_ps, h_ps, t_ps, y_ps = (m.ps("x_ps", [P, 1, 512]), m.ps("h_ps", [P, 2, 512]), m.ps("ht_ps", [P, 2, 512]),
                                  m.ps("y_ps", [P, 2, 512]))
        s_ps = m.ps("s_ps", [P, 512])
        raw_in, dch, rawf_done, s_t, ready = (m.sem("raw_in"), m.sem("dve_x"), m.sem("rawf"), m.sem("s_t"),
                                              m.sem("slots_ready"))
        ic, gath, scat = m.sem("idx_c"), m.sems("xg_in", XB), m.sem("y_added")
        xt_done, xt_cp, h_done, hb_done, hg_done = (m.sem("xt3"), m.sem("xt3_cp"), m.sem("h_done"),
                                                    m.sem("hb_done"), m.sem("hg_done"))
        ht_done, ht_cp, y_done, yb_done, ysb_done, y_ps_free = (m.sem("ht_done"), m.sem("ht_cp"), m.sem("y_done"),
                                                                m.sem("yb_done"), m.sem("ysb_done"), m.sem("y_ps_free"))
        y_free, issuing = m.sem("y_free"), m.sem("indirect_issuing")
        block = ctx.enter_context(nc.Block())

        @block.sync
        def _(sp):
            sp.dma_start(raw[:].rearrange("t p c -> t (p c)"),
                         table[0:STX * P, :].rearrange("(t p) c -> t (p c)", p=P)).then_inc(raw_in, 16)

        @block.gpsimd
        def _(pool):
            g = nc.gpsimd

            def gather(t, u, n):
                g.tensor_copy(g_idx[:, u:u + 1], tok[:, bass.ds(t, 1)]).then_inc(ic, 1)
                pool.wait_ge(ic, n + 1)
                pool.sem_inc(issuing, 1)
                g.indirect_dma_start(out=xg[:, u], out_offset=None, in_=dram["xn"],
                                     in_offset=bass.IndirectOffsetOnAxis(ap=g_idx[:, u:u + 1], axis=0)
                                     ).then_inc(gath[u], 16)

            pool.wait_ge(ready, 1)
            for u in range(XB):
                gather(u, u, u)

            def tiles(i):
                for u in range(XB):
                    pool.wait_ge(xt_done, i * XB + (u + 1))
                    gather(i * XB + (u + XB), u, i * (2 * XB) + (2 * u + XB))
                    pool.wait_ge(ysb_done, i * XB + (u + 1))
                    if u or not isinstance(i, int):
                        pool.wait_ge(scat, i * (16 * XB) + 16 * u)
                    pool.sem_inc(y_free, 1)
                    g.tensor_copy(s_idx[:, u:u + 1], tok[:, bass.ds(i * XB + u, 1)]).then_inc(ic, 1)
                    pool.wait_ge(ic, i * (2 * XB) + (2 * u + XB + 2))
                    pool.sem_inc(issuing, 1)
                    g.indirect_dma_start(out=out, in_=ysb[:, u], in_offset=None, compute_op=ALU.add,
                                         out_offset=bass.IndirectOffsetOnAxis(ap=s_idx[:, u:u + 1], axis=0)
                                         ).then_inc(scat, 16)

            tiles(0)
            with pool.Fori(1, ST_ // XB) as i:
                tiles(i)
            pool.wait_ge(scat, 16 * ST_)
            for u in range(XB):
                pool.wait_ge(gath[u], 16 * (ST_ // XB + 1))

        @block.tensor
        def _(pe):
            ident = K["ident"][:]
            pe.wait_ge(rawf_done, 1)
            n = STX
            nc.tensor.transpose(s_ps[:, 0:n], rawf[:], ident[0:n, 0:n])
            nc.tensor.transpose(s_ps[:, P:P + n], M["slot_w"][0:n, :], ident[0:n, 0:n]).then_inc(s_t, 1)

            def turn_x(u, i, t):
                pe.wait_ge(gath[u], i * 16 + 16)
                if not isinstance(t, int) or t:
                    pe.wait_ge(xt_cp, t)
                for k in range(2):
                    mm = nc.tensor.transpose(x_ps[:, 0, k * P:(k + 1) * P], xg[:, u, k * P:(k + 1) * P], ident)
                mm.then_inc(xt_done, 1)

            def up(u, t, e):
                pe.wait_ge(xt_cp, t + 1)
                for k in range(2):
                    mm = nc.tensor.matmul(h_ps[:, u, :], xT[:, u, k, :],
                                          M["w1"][:, k, bass.ds(e * HID, HID)], start=(k == 0), stop=(k == 1))
                mm.then_inc(h_done, 1)

            def turn_h(u, t):
                pe.wait_ge(hg_done, t + 1)
                for k in range(4):
                    mm = nc.tensor.transpose(t_ps[:, u, k * P:(k + 1) * P], hg[:, u, k * P:(k + 1) * P], ident)
                mm.then_inc(ht_done, 1)

            def down(u, t, e):
                pe.wait_ge(ht_cp, t + 1)
                for k in range(4):
                    mm = nc.tensor.matmul(y_ps[:, u, 0:D], hT[:, u, k, :], M["w2"][:, k, bass.ds(e * D, D)],
                                          start=(k == 0), stop=(k == 3))
                mm.then_inc(y_done, 1)

            def experts(t, n):
                return nc.values_load_multi_w_load_instructions(
                    M["tile_expert"][0:1, bass.ds(t, n)], engines=PE_ONLY, min_val=0, max_val=E - 1,
                    skip_runtime_bounds_check_because=WHY_IN_RANGE)[1]

            turn_x(0, 0, 0)
            up(0, 0, experts(0, 1)[0])
            turn_x(1, 0, 1)
            with pe.Fori(0, ST_ // XB) as i:
                ex = experts(i * XB, XB + 1)
                for u in range(XB):
                    t = i * XB + u
                    h, n = u % 2, (u + 2) % XB
                    turn_h(h, t)
                    pe.wait_ge(hb_done, t + 1)
                    up(1 - h, t + 1, ex[u + 1])
                    turn_x(n, i + (u + 2) // XB, t + 2)
                    pe.wait_ge(y_ps_free, t + 1)
                    down(h, t, ex[u])

        @block.scalar
        def _(act):
            with act.Fori(0, ST_ // XB) as i:
                for u in range(XB):
                    act.wait_ge(hb_done, i * XB + (u + 2))
                    nc.scalar.activation(hg[:, u % 2], hb[:, u % 2], ACT.Gelu).then_inc(hg_done, 1)

        @block.vector
        def _(dve):
            v = nc.vector
            link = Chain(dve, dch)
            dve.sem_inc(y_free, XB - 1)
            dve.sem_inc(y_ps_free, 2)
            dve.sem_inc(hb_done, 1)
            dve.wait_ge(raw_in, 16)
            link(v.tensor_copy(M["slot_w"][0:STX, :], raw[:, :, 1].bitcast(F32)))
            v.tensor_copy(rawf[:], raw[:, :, 0]).then_inc(rawf_done, 1)
            dve.wait_ge(s_t, 1)
            link(v.tensor_copy(tok[:], s_ps[:, 0:STX]))
            link(v.tensor_copy(wgt[:], s_ps[:, P:P + STX]))
            dve.sem_inc(ready, 1)
            dve.wait_ge(M["weights_in"], 16 * 8)

            def experts(t, n):
                return nc.values_load_multi_w_load_instructions(
                    M["tile_expert"][0:1, bass.ds(t, n)], engines=DVE_ONLY, min_val=0, max_val=E - 1,
                    skip_runtime_bounds_check_because=WHY_IN_RANGE)[1]

            def bias_h(u, t, e):
                dve.wait_ge(h_done, t + 1)
                v.tensor_tensor(hb[:, u], h_ps[:, u, :], M["b1"][:, bass.ds(e * HID, HID)], ALU.add
                                ).then_inc(hb_done, 1)

            def copy_x(u, t):
                dve.wait_ge(xt_done, t + 1)
                v.tensor_copy(xT[:, u].rearrange("p k n -> p (k n)"), x_ps[:, 0, 0:2 * P]).then_inc(xt_cp, 1)

            copy_x(0, 0)
            bias_h(0, 0, experts(0, 1)[0])
            copy_x(1, 1)
            with dve.Fori(0, ST_ // XB) as i:
                ex = experts(i * XB, XB + 1)
                for u in range(XB):
                    t = i * XB + u
                    h = u % 2
                    dve.wait_ge(ht_done, t + 1)
                    v.tensor_copy(hT[:, h].rearrange("p k n -> p (k n)"), t_ps[:, h, :]).then_inc(ht_cp, 1)
                    bias_h(1 - h, t + 1, ex[u + 1])
                    copy_x(h, t + 2)
                    dve.wait_ge(y_done, t + 1)
                    dve.wait_ge(y_free, t + 1)
                    v.tensor_tensor(ysb[:, u], y_ps[:, h, 0:D], M["b2"][:, bass.ds(ex[u] * D, D)], ALU.add
                                    ).then_inc(y_ps_free, 1)
                    dve.wait_ge(y_ps_free, t + 3)
                    v.tensor_scalar(ysb[:, u], ysb[:, u], wgt[:, bass.ds(t, 1)], None, ALU.mult).then_inc(ysb_done, 1)


def build(nc, x, src, dst, W, att, gamma, beta, Wr, br, W1, b1, W2, b2, out):
    def scratch(name, shape, dt):
        return nc.dram_tensor(name, shape, dt, kind="Internal").ap()

    dram = {
        "z_table": scratch("z_table", (NP, ROW), F32), "xn": scratch("xn_rows", (NP, D), F32),
        "step_edge_tile": scratch("step_edge_tile", (SP + 2,), I32),
        "step_node_tile": scratch("step_node_tile", (SP,), I32), "flags": scratch("step_flags", (2, SP, P), F32),
        "slot_table": scratch("slot_table", ((STX + 2 * TOPK) * P, 2), I32),
    }
    with ExitStack() as ctx:
        K = lasting(nc, ctx)
        constants_phase(nc, K)
        with ExitStack() as graph:
            K.update(graph_tables(nc, graph))
            step_table_phase(nc, K, dram, src, dst)
            chain_table_phase(nc, K)
            node_phase(nc, K, dram, x, W, att)
            edge_phase(nc, K, dram)
        M = expert_buffers(nc, ctx)
        token_phase(nc, K, M, dram, x, gamma, beta, Wr, br, W1, b1, W2, b2, out)
        expert_phase(nc, K, M, dram, out)


def kernel(x, src, dst, L0_gnn_W, L0_gnn_att, L0_ffn_gamma, L0_ffn_beta, L0_ffn_Wr, L0_ffn_br, L0_ffn_W1,
           L0_ffn_b1, L0_ffn_W2, L0_ffn_b2):
    import numpy as np
    import concourse.bacc as bacc
    from concourse.bass_utils import run_bass_kernel_spmd

    def padded(a, shape, fill):
        a = np.asarray(a)
        out = np.full(shape, fill, a.dtype)
        out[:a.shape[0]] = a
        return out

    arrays = {
        "x": padded(x, (NP, D), 0), "src": padded(src, (ET * P,), 0).reshape(ET, P),
        "dst": padded(dst, (ET * P,), PAD_DST).reshape(ET, P), "W": L0_gnn_W, "att": L0_gnn_att,
        "gamma": L0_ffn_gamma, "beta": L0_ffn_beta, "Wr": L0_ffn_Wr, "br": L0_ffn_br, "W1": L0_ffn_W1,
        "b1": L0_ffn_b1, "W2": L0_ffn_W2, "b2": L0_ffn_b2,
    }
    arrays = {name: np.ascontiguousarray(a) for name, a in arrays.items()}
    nc = bacc.Bacc("TRN2", target_bir_lowering=False, num_devices=1)
    args = [nc.dram_tensor(name, a.shape, mybir.dt.from_np(a.dtype), kind="ExternalInput").ap()
            for name, a in arrays.items()]
    out = nc.dram_tensor("out", (NP, D), F32, kind="ExternalOutput").ap()
    build(nc, *args, out)
    r = run_bass_kernel_spmd(nc, [arrays], core_ids=[0])
    return r.results[0]["out"][:N_NODES]
```

```python
from contextlib import ExitStack

import concourse.bass as bass
from concourse import mybir

P = 128
F32 = mybir.dt.float32
I32 = mybir.dt.int32
ALU = mybir.AluOpType
ACT = mybir.ActivationFunctionType
AX_X = mybir.AxisListType.X
DVE_ONLY = (mybir.EngineType.DVE,)
PE_ONLY = (mybir.EngineType.PE,)
WHY_IN_RANGE = "the table is clamped on the chip to the buffer's range"

N_NODES, N_EDGES = 6250, 100000
D = 256
HEADS, HD = 4, 64
HB = HD + 1
ROW = HEADS * HB + HEADS
E, TOPK, HID = 8, 2, 512

NT = -(-N_NODES // P) + 1
NP = NT * P
PAD_ROW = (NT - 1) * P
ET = -(-N_EDGES // P)
EROW = 2 * P + 2
PAD_DST = 8191
SB = 32
NB = -(-(ET + NT - 2) // SB)
NB += NB % 2
STEPS = NB * SB
SJ = -(-(STEPS + 1) // P)
SP = SJ * P
ST_ = (TOPK * N_NODES + E * (P - 1)) // P
XB = 4
ST_ += -ST_ % XB
STX = ST_ + XB
SLOTS = ST_ * P
BIG = 1e30
EPS = 1e-5
SLOPE, NEG = 0.01, -1000.0


class Chain:

    def __init__(self, eng, sem, base=0):
        self.eng, self.sem, self.base, self.n = eng, sem, base, 0

    def __call__(self, ins):
        self.n += 1
        ins.then_inc(self.sem, 1)
        self.eng.wait_ge(self.sem, self.base + self.n)


class Mem:

    def __init__(self, nc, ctx):
        self.nc, self.ctx = nc, ctx

    def sb(self, name, shape, dt=F32):
        return self.ctx.enter_context(self.nc.sbuf_tensor(name, shape, dt))

    def ps(self, name, shape):
        return self.ctx.enter_context(self.nc.psum_tensor(name, shape, F32))

    def sem(self, name):
        return self.ctx.enter_context(self.nc.semaphore(name))

    def sems(self, name, n):
        return [self.sem(f"{name}{i}") for i in range(n)]


def constants_phase(nc, K):
    with ExitStack() as ctx:
        m = Mem(nc, ctx)
        made = m.sem("const_made")
        block = ctx.enter_context(nc.Block())

        @block.gpsimd
        def _(pool):
            link = Chain(pool, made)
            link(nc.gpsimd.memset(K["ident"][:], 0.0))
            link(nc.gpsimd.affine_select(out=K["ident"][:], in_=K["ident"][:], compare_op=ALU.not_equal, fill=1.0,
                                         base=0, pattern=[[-1, P]], channel_multiplier=1))
            link(nc.gpsimd.iota(K["iota_row"][:], pattern=[[1, P]], base=0, channel_multiplier=0,
                                allow_small_or_imprecise_dtypes=True))
            link(nc.gpsimd.iota(K["iota_col"][:], pattern=[[0, 1]], base=0, channel_multiplier=1,
                                allow_small_or_imprecise_dtypes=True))
            link(nc.gpsimd.memset(K["ones"][:], 1.0))
            link(nc.gpsimd.memset(K["eps"][:], EPS))
            link(nc.gpsimd.memset(K["zero"][:], 0.0))


def step_table_phase(nc, K, dram, edges):
    CH = ET // 2
    with ExitStack() as ctx:
        m = Mem(nc, ctx)
        ends = m.sb("tile_ends", [1, 2, ET], I32)
        tiles = m.sb("tile_ends_node_tile", [1, 2, ET])
        row = m.sb("cum_and_shift", [1, 2, ET])
        cb = m.sb("cum_and_shift_all", [P, 2, ET])
        one_row = m.sb("one_row", [1, ET])
        junk = m.sb("junk", [P, ET])
        iota_e = m.sb("iota_e", [P, ET])
        s_col = m.sb("s_col", [P, SJ])
        e_col, d_col, n_col = m.sb("e_col", [P, SJ]), m.sb("d_col", [P, SJ]), m.sb("n_col", [P, SJ])
        e_int, n_int = m.sb("e_int", [P, SJ], I32), m.sb("n_int", [P, SJ], I32)
        base_col = m.sb("node_base_col", [P, SJ])
        rows = m.sb("step_edges", [P, SJ, EROW], I32)
        same = m.sb("same_flags", [P, 2, SJ, P])
        locf, srcf = m.sb("loc_rows", [P, SJ, P]), m.sb("src_rows", [P, SJ, P])
        pb = m.ps("bcast_ps", [P, 4, 512])
        pt = m.ps("turn_ps", [P, 2, 512])

        in_s, row_done, bc_done, pool_c = m.sem("ends_in"), m.sem("row_done"), m.sem("bcast_done"), m.sem("pool_tbl")
        dch, e_done, tbl_out = m.sem("dve_tbl"), m.sem("e_done"), m.sem("tbl_out")
        idx_in, rows_in, flags_done, flags_out = (m.sem("idx_in"), m.sem("rows_in"), m.sem("flags_done"),
                                                  m.sem("flags_out"))
        turned, copied, rep_in = m.sem("turned"), m.sem("turn_copied"), m.sem("flags_rep_in")
        ctx.enter_context(nc.allow_non_contiguous_dma(reason="one word for an edge tile or a step, once"))
        block = ctx.enter_context(nc.Block())
        n_dram, flag_dram = dram["step_node_tile"], dram["flags"]

        @block.sync
        def _(sp):
            for j, col in ((0, 1), (1, P)):
                sp.dma_start(ends[0:1, j, :], edges[:, col:col + 1].rearrange("e o -> o e")).then_inc(in_s, 16)
            sp.wait_ge(in_s, 32)
            lp = (N_EDGES - 1) % P + 1
            sp.dma_start(ends[0:1, 1, ET - 1:ET], edges[ET - 1:ET, lp:lp + 1]).then_inc(in_s, 16)
            sp.wait_ge(e_done, 1)
            sp.dma_start(n_dram[0:SP].rearrange("(j p) -> p j", p=P), n_int[:]).then_inc(tbl_out, 16)
            sp.wait_ge(tbl_out, 16)
            sp.dma_start(K["step_node"][0:1, 1:], n_dram[0:STEPS + SB].rearrange("(a s) -> a s", a=1)).then_inc(idx_in, 16)
            sp.wait_ge(flags_done, 1)
            for o in range(2):
                sp.dma_start(flag_dram[o].rearrange("(j p) i -> p j i", p=P), same[:, o]).then_inc(flags_out, 16)
            sp.wait_ge(flags_out, 32)
            for o, name in enumerate(("reset_fwd", "reset_bwd")):
                for h in range(HEADS):
                    sp.dma_start(K[name][h * SB:(h + 1) * SB],
                                 flag_dram[o, 0:STEPS].rearrange("(b k) i -> k b i", k=SB)).then_inc(rep_in, 16)
            sp.wait_ge(rep_in, 16 * 2 * HEADS)
            sp.wait_ge(idx_in, 16)

        @block.gpsimd
        def _(pool):
            nc.gpsimd.iota(iota_e[:], pattern=[[1, ET]], base=0, channel_multiplier=0,
                           allow_small_or_imprecise_dtypes=True).then_inc(pool_c, 1)
            nc.gpsimd.iota(s_col[:], pattern=[[P, SJ]], base=0, channel_multiplier=1,
                           allow_small_or_imprecise_dtypes=True).then_inc(pool_c, 1)
            pool.wait_ge(e_done, 1)
            for j in range(SJ):
                nc.gpsimd.indirect_dma_start(
                    out=rows[:, j, :], out_offset=None, in_=edges,
                    in_offset=bass.IndirectOffsetOnAxis(ap=e_int[:, j:j + 1], axis=0)).then_inc(rows_in, 16)

        @block.tensor
        def _(pe):
            pe.wait_ge(row_done, 1)
            for a in range(2):
                for c in range(2):
                    mm = nc.tensor.matmul(pb[:, 2 * a + c, 0:CH], K["ones"][0:1, :], row[0:1, a, c * CH:(c + 1) * CH],
                                          start=True, stop=True)
            mm.then_inc(bc_done, 1)
            pe.wait_ge(flags_done, 1)
            for n in range(2 * SJ):
                if n >= 2:
                    pe.wait_ge(copied, n - 1)
                source = (locf, srcf)[n % 2]
                nc.tensor.transpose(pt[:, n % 2, 0:P], source[:, n // 2, :], K["ident"][:]).then_inc(turned, 1)

        @block.vector
        def _(dve):
            v = nc.vector
            link = Chain(dve, dch)
            dve.wait_ge(in_s, 48)
            link(v.tensor_scalar(ends[:], ends[:], 7, None, ALU.arith_shift_right))
            link(v.tensor_copy(tiles[:], ends[:]))
            link(v.memset(one_row[:], 1.0))
            link(v.tensor_tensor(row[0:1, 1, :], tiles[0:1, 1, :], tiles[0:1, 0, :], ALU.subtract))
            link(v.tensor_scalar(row[0:1, 1, :], row[0:1, 1, :], 1.0, None, ALU.add))
            link(v.tensor_tensor_scan(row[0:1, 0, :], one_row[:], row[0:1, 1, :], 0.0, ALU.mult, ALU.add))
            link(v.tensor_tensor(row[0:1, 1, :], row[0:1, 0, :], row[0:1, 1, :], ALU.subtract))
            v.tensor_tensor(row[0:1, 1, :], row[0:1, 1, :], tiles[0:1, 0, :], ALU.subtract).then_inc(row_done, 1)
            dve.wait_ge(bc_done, 1)
            for a in range(2):
                link(v.tensor_copy(cb[:, a].rearrange("p (c x) -> p c x", c=2), pb[:, 2 * a:2 * a + 2, 0:CH]))
            dve.wait_ge(pool_c, 2)
            for j in range(SJ):
                link(v.tensor_scalar(junk[:], cb[:, 0], s_col[:, j:j + 1], 0.0, ALU.is_le, ALU.add,
                                     accum_out=e_col[:, j:j + 1]))
            link(v.tensor_scalar(e_col[:], e_col[:], float(ET - 1), None, ALU.min))
            for j in range(SJ):
                link(v.scalar_tensor_tensor(out=junk[:], in0=iota_e[:], scalar=e_col[:, j:j + 1], in1=cb[:, 1],
                                            op0=ALU.is_equal, op1=ALU.mult, accum_out=d_col[:, j:j + 1]))
            link(v.tensor_tensor(n_col[:], s_col[:], d_col[:], ALU.subtract))
            link(v.tensor_scalar(n_col[:], n_col[:], float(NT - 1), 0.0, ALU.min, ALU.max))
            link(v.tensor_scalar(base_col[:], n_col[:], float(P), None, ALU.mult))
            link(v.tensor_copy(e_int[:], e_col[:]))
            v.tensor_copy(n_int[:], n_col[:]).then_inc(e_done, 1)
            dve.wait_ge(e_done, 1)
            dve.wait_ge(rows_in, 16 * SJ)
            cur = rows[:, :, 1:P + 1]
            link(v.tensor_tensor(same[:, 0, :, 1:P], cur[:, :, 1:P], cur[:, :, 0:P - 1], ALU.is_equal))
            link(v.tensor_tensor(same[:, 0, :, 0:1], cur[:, :, 0:1], rows[:, :, 0:1], ALU.is_equal))
            link(v.tensor_tensor(same[:, 1, :, P - 1:0:-1], cur[:, :, 1:P], cur[:, :, 0:P - 1], ALU.is_equal))
            link(v.tensor_tensor(same[:, 1, :, 0:1], cur[:, :, P - 1:P], rows[:, :, P + 1:P + 2], ALU.is_equal))
            link(v.tensor_scalar(same[:], same[:], 1.0, BIG, ALU.subtract, ALU.mult))
            for j in range(SJ):
                link(v.tensor_scalar(locf[:, j, :], cur[:, j, :], base_col[:, j:j + 1], None, ALU.subtract))
            v.tensor_copy(srcf[:], rows[:, :, P + 2:EROW]).then_inc(flags_done, 1)
            for n in range(2 * SJ):
                dve.wait_ge(turned, n + 1)
                out = (K["loc_dst"], K["src_idx"])[n % 2]
                v.tensor_copy(out[:, (n // 2) * P:(n // 2 + 1) * P], pt[:, n % 2, 0:P]).then_inc(copied, 1)


def chain_table_phase(nc, K):
    with ExitStack() as ctx:
        m = Mem(nc, ctx)
        first = m.sb("first_loc", [1, NB])
        pf = m.ps("first_ps", [P, 512])
        dch, first_done, f_bc = m.sem("dve_ch"), m.sem("first_done"), m.sem("first_bcast")
        block = ctx.enter_context(nc.Block())

        @block.tensor
        def _(pe):
            pe.wait_ge(first_done, 1)
            nc.tensor.matmul(pf[:, 0:NB], K["ones"][0:1, :], first[:], start=True, stop=True).then_inc(f_bc, 1)

        @block.vector
        def _(dve):
            v = nc.vector
            link = Chain(dve, dch)
            v.tensor_copy(first[:], K["loc_dst"][0:1, 0:STEPS].rearrange("a (b k) -> a b k", k=SB)[:, :, 0]
                          ).then_inc(first_done, 1)
            for o, name in enumerate(("reset_fwd", "reset_bwd")):
                link(v.tensor_reduce(K["whole"][:, o, :], K[name][:], AX_X, ALU.min))
            link(v.tensor_scalar(K["goes_on"][:], K["reset_fwd"][0:1, :, 0], 0.0, None, ALU.is_equal))
            dve.wait_ge(f_bc, 1)
            link(v.tensor_scalar(K["first_node"][:], pf[:, 0:NB], K["iota_col"][:, 0:1], None, ALU.is_equal))


def mean_and_rstd(nc, dve, link, stats, mean, rstd, tmp, var_ready, std_ready, n):
    v = nc.vector
    half = stats.rearrange("p t (o c) -> p t o c", o=2)
    me, mo = half[:, :, 0, 1], half[:, :, 1, 1]
    link(v.tensor_tensor(mean, me, mo, ALU.add))
    link(v.tensor_scalar(mean, mean, 0.5, None, ALU.mult))
    link(v.tensor_tensor(tmp, me, mo, ALU.subtract))
    link(v.tensor_tensor(tmp, tmp, tmp, ALU.mult))
    link(v.tensor_scalar(tmp, tmp, D / 4.0, None, ALU.mult))
    link(v.tensor_tensor(tmp, tmp, half[:, :, 0, 2], ALU.add))
    link(v.tensor_tensor(tmp, tmp, half[:, :, 1, 2], ALU.add))
    v.tensor_scalar(rstd, tmp, 1.0 / D, None, ALU.mult).then_inc(var_ready, 1)
    dve.wait_ge(std_ready, n)
    link(v.reciprocal(rstd, rstd))


def node_phase(nc, K, dram, x, W, att):
    ZC = HEADS * HD
    CHUNKS = 5
    TC = NT // CHUNKS
    ZT = TC // 2
    with ExitStack() as ctx:
        m = Mem(nc, ctx)
        xr = m.sb("x_all", [P, NT, D])
        stats = m.sb("stats", [P, NT, 6])
        mean, rstd, tmp = m.sb("mean", [P, NT]), m.sb("rstd", [P, NT]), m.sb("ln_tmp", [P, NT])
        shift = m.sb("ln_shift1", [P, NT])
        w_all = m.sb("w_all", [P, 2, ZC + 2 * HEADS])
        w_in = m.sb("w_in", [P, 2, HEADS, HD])
        att_in, prod = m.sb("att_in", [1, HEADS * 2 * HD]), m.sb("att_prod", [P, 2, 2, HEADS, HD])
        xn, xT = m.sb("xn", [P, 2, D]), m.sb("xT", [P, 2, 2, P])
        zrow = m.sb("zrow", [P, 2, ZT, ROW])
        t_ps, z_ps, a_ps = m.ps("t_ps", [P, 2, 512]), m.ps("z_ps", [P, 2, 512]), m.ps("a_ps", [P, 512])

        x_in, w_s, z_out = m.sems("x_in", CHUNKS), m.sem("w_in_s"), m.sems("z_out", 2)
        dch, zch, att_bc, w_ready = m.sem("dve_n"), m.sem("dve_z"), m.sem("att_bc"), m.sem("w_ready")
        stats_done, var_ready, std_ready = m.sem("stats_done"), m.sem("var_ready"), m.sem("std_ready")
        xn_done, xt_done, xt_copied = m.sem("xn_done"), m.sem("xt_done"), m.sem("xt_cp")
        acc_zero, ln_ready = m.sem("acc_zero"), m.sem("ln1_ready")
        z_done, z_copied, z_free = m.sem("z_done"), m.sem("z_copied"), m.sem("z_free")
        block = ctx.enter_context(nc.Block())

        @block.sync
        def _(sp):
            for c in range(CHUNKS):
                sp.dma_start(xr[:, c * TC:(c + 1) * TC, :],
                             x[c * TC * P:(c + 1) * TC * P, :].rearrange("(t p) d -> p t d", p=P)
                             ).then_inc(x_in[c], 16)
                if c == 0:
                    for h in range(HEADS):
                        sp.dma_start(w_in[:, :, h, :], W[h].rearrange("(k p) f -> p k f", p=P)).then_inc(w_s, 16)
                    sp.dma_start(att_in[:], att.rearrange("(a h) c -> a (h c)", a=1)).then_inc(w_s, 16)
            with sp.Fori(0, CHUNKS) as i:
                for u in range(2):
                    c = i * 2 + u
                    sp.wait_ge(z_copied, c + 1)
                    sp.dma_start(dram["z_table"][bass.ds(c * (ZT * P), ZT * P), :].rearrange("(t p) d -> p t d", p=P),
                                 zrow[:, u]).then_inc(z_out[u], 16)
            for u in range(2):
                sp.wait_ge(z_out[u], 16 * CHUNKS)

        @block.gpsimd
        def _(pool):
            nc.gpsimd.memset(K["acc"][:], 0.0).then_inc(acc_zero, 1)
            pool.wait_ge(acc_zero, 1)

        @block.tensor
        def _(pe):
            pe.wait_ge(w_s, 16 * (HEADS + 1))
            pe.wait_ge(K["setup"], 1)
            nc.tensor.matmul(a_ps[:], K["ones"][0:1, :], att_in[:], start=True, stop=True).then_inc(att_bc, 1)
            pe.wait_ge(w_ready, 1)

            def turn(t, u):
                pe.wait_ge(xn_done, t + 1)
                for k in range(2):
                    mm = nc.tensor.transpose(t_ps[:, u, k * P:(k + 1) * P], xn[:, u, k * P:(k + 1) * P],
                                             K["ident"][:])
                mm.then_inc(xt_done, 1)

            def product(t, u):
                pe.wait_ge(xt_copied, t + 1)
                pe.wait_ge(z_free, t + 1)
                for k in range(2):
                    mm = nc.tensor.matmul(z_ps[:, u, 0:ZC + 2 * HEADS], xT[:, u, k, :], w_all[:, k, :],
                                          start=(k == 0), stop=(k == 1))
                mm.then_inc(z_done, 1)

            turn(0, 0)
            with pe.Fori(0, NT // 2 - 1) as i:
                for u in range(2):
                    turn(i * 2 + (u + 1), 1 - u)
                    product(i * 2 + u, u)
            turn(NT - 1, 1)
            for u in range(2):
                product(NT - 2 + u, u)

        @block.scalar
        def _(act):
            act.wait_ge(var_ready, 1)
            nc.scalar.activation(rstd[:], rstd[:], ACT.Sqrt, bias=K["eps"][:, 0:1]).then_inc(std_ready, 1)
            act.wait_ge(ln_ready, 1)

            def normalise(t, u):
                nc.scalar.activation(xn[:, u], xr[:, bass.ds(t, 1), :].rearrange("p a c -> p (a c)"), ACT.Identity,
                                     bias=shift[:, bass.ds(t, 1)], scale=rstd[:, bass.ds(t, 1)]
                                     ).then_inc(xn_done, 1)

            def copy_turned(t, u):
                act.wait_ge(xt_done, t + 1)
                act.wait_ge(z_free, t + 1)
                nc.scalar.copy(xT[:, u].rearrange("p k n -> p (k n)"), t_ps[:, u, 0:2 * P]).then_inc(xt_copied, 1)

            for u in range(2):
                normalise(u, u)
            with act.Fori(0, NT // 2 - 1) as i:
                for u in range(2):
                    copy_turned(i * 2 + u, u)
                    normalise(i * 2 + (u + 2), u)
            for u in range(2):
                copy_turned(NT - 2 + u, u)

        @block.vector
        def _(dve):
            v = nc.vector
            link = Chain(dve, dch)
            dve.sem_inc(z_free, 2)
            link(v.memset(zrow[:], 1.0))
            dve.sem_inc(K["setup"], 1)
            dve.wait_ge(att_bc, 1)
            a4 = a_ps[:].rearrange("p (h o f) -> p o h f", h=HEADS, o=2)
            for k in range(2):
                link(v.tensor_copy(w_all[:, k, 0:ZC].rearrange("p (h f) -> p h f", h=HEADS), w_in[:, k]))
                for o in range(2):
                    link(v.tensor_tensor(prod[:, k, o], w_in[:, k], a4[:, o], ALU.mult))
                    link(v.tensor_reduce(w_all[:, k, ZC + o * HEADS:ZC + (o + 1) * HEADS], prod[:, k, o], AX_X,
                                         ALU.add))
            dve.sem_inc(w_ready, 1)
            for c in range(CHUNKS):
                dve.wait_ge(x_in[c], 16)
                with dve.Fori(0, 2) as i:
                    for q in range(ZT):
                        t = i * ZT + (c * TC + q)
                        v.bn_stats(stats[:, bass.ds(t, 1), :].rearrange("p a c -> p (a c)"),
                                   xr[:, bass.ds(t, 1), :].rearrange("p a c -> p (a c)")).then_inc(stats_done, 1)
            dve.wait_ge(stats_done, NT)
            mean_and_rstd(nc, dve, link, stats[:], mean[:], rstd[:], tmp[:], var_ready, std_ready, 1)

            v.scalar_tensor_tensor(out=shift[:], in0=mean[:], scalar=-1.0, in1=rstd[:], op0=ALU.mult, op1=ALU.mult
                                   ).then_inc(ln_ready, 1)

            def take_rows(i):
                for u in range(2):
                    if not isinstance(i, int):
                        dve.wait_ge(z_out[u], i * 16)
                    for q in range(ZT):
                        t = i * TC + (u * ZT + q)
                        b = (u * ZT + q) % 2
                        dve.wait_ge(z_done, t + 1)
                        v.tensor_copy(zrow[:, u, q, 0:HEADS * HB].rearrange("p (h f) -> p h f", h=HEADS)[:, :, 0:HD],
                                      z_ps[:, b, 0:ZC].rearrange("p (h f) -> p h f", h=HEADS)).then_inc(zch, 1)
                        v.tensor_copy(zrow[:, u, q, HEADS * HB:], z_ps[:, b, ZC:ZC + HEADS]).then_inc(zch, 1)
                        v.tensor_copy(K["ed"][:, bass.ds(t, 1), :].rearrange("p a h -> p (a h)"),
                                      z_ps[:, b, ZC + HEADS:ZC + 2 * HEADS]).then_inc(z_free, 1)
                    dve.wait_ge(zch, i * (2 * TC) + (2 * (u + 1) * ZT))
                    dve.sem_inc(z_copied, 1)

            take_rows(0)
            with dve.Fori(1, CHUNKS) as i:
                take_rows(i)
            dve.wait_ge(z_free, NT + 2)


def lasting(nc, ctx):
    m = Mem(nc, ctx)
    return {
        "ident": m.sb("ident", [P, P]), "iota_row": m.sb("iota_row", [P, P]), "iota_col": m.sb("iota_col", [P, 1]),
        "ones": m.sb("ones", [P, P]), "eps": m.sb("eps", [P, 1]), "zero": m.sb("zero", [P, 1]), "setup": m.sem("setup"),
        "acc": m.sb("acc", [P, NT, HEADS * HB]),
    }


def graph_tables(nc, ctx):
    m = Mem(nc, ctx)
    return {
        "step_node": m.sb("step_node", [1, 1 + STEPS + SB], I32),
        "loc_dst": m.sb("loc_dst", [P, SP]),
        "src_idx": m.sb("src_idx", [P, SP], I32),
        "reset_fwd": m.sb("reset_fwd", [P, NB, P]),
        "reset_bwd": m.sb("reset_bwd", [P, NB, P]),
        "whole": m.sb("whole", [P, 2, NB]),
        "goes_on": m.sb("goes_on", [1, NB]), "first_node": m.sb("first_node", [P, NB]),
        "ed": m.sb("ed", [P, NT, HEADS]),
    }


def expert_buffers(nc, ctx):
    m = Mem(nc, ctx)
    return {
        "w1": m.sb("w1_all", [P, 2, E * HID]), "w2": m.sb("w2_all", [P, 4, E * D]),
        "b1": m.sb("b1_all", [P, E * HID]), "b2": m.sb("b2_all", [P, E * D]), "weights_in": m.sem("weights_in"),
        "tile_expert": m.sb("tile_expert", [1, STX], I32),
        "slot_token": m.sb("slot_token", [P, STX], I32), "slot_weight": m.sb("slot_weight", [P, STX]),
    }


def edge_phase(nc, K, dram):
    G4 = SB // 4
    S8 = SB // 8
    HK = HEADS * (SB + 1)
    YG = 4
    Y = 2 * YG
    GROUPS = SB // YG
    with ExitStack() as ctx:
        m = Mem(nc, ctx)
        rows = m.sb("edge_rows", [P, 2, SB, ROW])
        onehot = m.sb("onehot", [P, 2, SB, P])
        onehot_t = m.sb("onehot_t", [P, 2, 4, P])
        idx = m.sb("edge_idx", [P, 2, SB], I32)
        sc, sc2 = m.sb("scores", [P, HEADS, SB]), m.sb("scores2", [P, HEADS, SB])
        fwd, bwd = m.sb("fwd", [P, P]), m.sb("bwd", [P, P])
        top = sc2[:].rearrange("p h k -> p (h k)")
        ends = m.sb("chain_in", [1, 2, 2, HK])
        chain = m.sb("chain_max", [1, 2, HK])
        enter = m.sb("chain_enter", [1, 2, P])
        init = m.sb("chain_init", [P, 2])
        mx4, dl4, g4 = m.sb("mx4", [1, HEADS]), m.sb("dl4", [1, HEADS]), m.sb("g4", [1, HEADS])
        node_scale = m.sb("node_scale", [P, HEADS])
        whole_now = m.sb("whole_now", [P, 2])
        wt = m.sb("weights", [P, 2, HEADS, SB])
        y = m.sb("weighted", [P, 2, YG, HEADS * HB])
        t_ps, ed_ps, e_ps = m.ps("oh_ps", [P, 2, 512]), m.ps("ed_ps", [P, 512]), m.ps("e_ps", [P, 512])
        small, out_ps = m.ps("small_ps", [P, 512]), m.ps("out_ps", [P, 2, 512])

        gath, rows_free, idx_c = m.sems("gathered", 2), m.sem("rows_free"), m.sem("idx_copied")
        issuing = m.sem("edge_gathers_issuing")
        oh_built, oh_free, oht_ps, oht_sb, oht_free = (m.sem("oh_built"), m.sem("oh_free"), m.sem("oht_ps"),
                                                       m.sem("oht_sb"), m.sem("oht_free"))
        ed_done, dch = m.sem("ed_done"), m.sem("dve_edge")
        sc_ready, sc_turned, ends_ready, ends_turned = (m.sem("sc_ready"), m.sem("sc_turned"), m.sem("ends_ready"),
                                                        m.sem("ends_turned"))
        chain_ready, init_done, dl_ready, g_done, enter_ready = (m.sem("chain_ready"), m.sem("init_done"), m.sem("dl_ready"),
                                                    m.sem("g_done"), m.sem("enter_ready"))
        gm_ready, gm_bc, x_ready, x_turned, w_done = (m.sem("gm_ready"), m.sem("gm_bc"), m.sem("x_ready"),
                                                      m.sem("x_turned"), m.sem("w_done"))
        y_ready, mm_done = m.sem("y_ready"), m.sem("mm_done")
        sums_ok = m.sem("sums_ok")
        dmain, prepared = m.sem("dve_steps"), m.sem("edge_prepared")
        stage_over = m.sem("stage_over")
        BUILD = {0: (1, 3), 4: (2, 0), 6: (2, 1), 7: (2, 2)}
        SCORES, MAXIMA, CHAINS, ENTER, FIRST = 2, 3, 4, 5, 7
        TURN = {0: (1, "D2 D3 T4 T5"), 1: (1, "D4 T6 D5 T7"), 2: (1, "D6 D7"),
                5: (2, "T0 T1"), 6: (2, "D0 D1"), 7: (2, "T2 T3")}
        T_SCORES, T_ENDS, T_ENTER, T_WEIGHTS = 3, 4, 5, 6
        block = ctx.enter_context(nc.Block())

        def heads(ap):
            return ap.rearrange("a (h k) -> a h k", h=HEADS)

        @block.gpsimd
        def _(pool):
            Q = SB // 4
            pool.sem_inc(rows_free, 7)
            with pool.Fori(0, NB // 2) as i:
                for u in range(2):
                    for q in range(4):
                        pool.wait_ge(rows_free, i * 8 + (4 * u + q + 1))
                        if q == 0:
                            nc.gpsimd.tensor_copy(idx[:, u], K["src_idx"][:, bass.ds(i * (2 * SB) + u * SB, SB)]
                                                  ).then_inc(idx_c, 1)
                            pool.wait_ge(idx_c, i * 2 + (u + 1))
                        pool.sem_inc(issuing, 1)
                        for k in range(q * Q, (q + 1) * Q):
                            nc.gpsimd.indirect_dma_start(
                                out=rows[:, u, k, :], out_offset=None, in_=dram["z_table"],
                                in_offset=bass.IndirectOffsetOnAxis(ap=idx[:, u, k:k + 1], axis=0)
                            ).then_inc(gath[u], 16)

        @block.tensor
        def _(pe):
            ident = K["ident"][:]

            def turn_group(b, u, g):
                pe.wait_ge(oh_built, b * S8 + (g // 2 + 1))
                for q in range(4):
                    mm = nc.tensor.transpose(t_ps[:, g % 2, q * P:(q + 1) * P], onehot[:, u, g * 4 + q, :], ident)
                mm.then_inc(oht_ps, 1)

            def dst_scores(b, g, node):
                pe.wait_ge(oht_sb, b * G4 + (g + 1))
                for q in range(4):
                    k = g * 4 + q
                    mm = nc.tensor.matmul(ed_ps[:, k * HEADS:(k + 1) * HEADS], onehot_t[:, g % 2, q, :],
                                          K["ed"][:, bass.ds(node[k % 8], 1), :].rearrange("p a h -> p (a h)"),
                                          start=True, stop=True)
                mm.then_inc(ed_done, 1)

            def nodes_of(b, g):
                return nc.values_load_multi_w_load_instructions(
                    K["step_node"][0:1, bass.ds(b * SB + (g * 4 + 1), 8)], engines=PE_ONLY, min_val=0,
                    max_val=NT - 1, skip_runtime_bounds_check_because=WHY_IN_RANGE)[1]

            def turn_scores(b):
                pe.wait_ge(sc_ready, b + 1)
                nc.tensor.transpose(e_ps[:, 0:P], sc[:].rearrange("p h k -> p (h k)"), ident).then_inc(sc_turned, 1)

            def turn_ends(b):
                pe.wait_ge(ends_ready, b * 2 + 2)
                for o, col in enumerate((fwd[:, P - 1:P], bwd[:, 0:1])):
                    nc.tensor.transpose(small[0:1, 2 * o * P:(2 * o + 1) * P], col, ident)
                    mm = nc.tensor.transpose(small[0:1, (2 * o + 1) * P:(2 * o + 2) * P], whole_now[:, o:o + 1],
                                             ident)
                mm.then_inc(ends_turned, 1)

            def turn_entering(b):
                pe.wait_ge(enter_ready, b * 2 + 2)
                for o in range(2):
                    mm = nc.tensor.matmul(small[:, o:o + 1], enter[0:1, o], K["ones"][0:1, 0:1], start=True,
                                          stop=True)
                mm.then_inc(init_done, 1)

            def turn_weights(b):
                pe.wait_ge(gm_ready, b + 1)
                nc.tensor.matmul(small[:, 0:HEADS], K["ones"][0:1, :], g4[:], start=True, stop=True
                                 ).then_inc(gm_bc, 1)
                pe.wait_ge(x_ready, b + 1)
                nc.tensor.transpose(e_ps[:, 0:P], top, ident).then_inc(x_turned, 1)

            def turns(b, u, ops):
                for op in ops.split():
                    g = int(op[1:])
                    if op[0] == "T":
                        turn_group(b, u, g)
                    else:
                        if g % 2 == 0:
                            node = nodes_of(b, g)
                        dst_scores(b, g, node)

            def steps(b, u, ahead):
                for g in range(GROUPS):
                    pe.wait_ge(y_ready, b * GROUPS + (g + 1))
                    for k in range(g * YG, (g + 1) * YG):
                        if k:
                            pe.wait_ge(sums_ok, b * SB + (k + 1))
                        nc.tensor.matmul(out_ps[:, u, 0:HEADS * HB], onehot[:, u, k, :], y[:, g % 2, k % YG],
                                         start=(k == 0), stop=True, skip_group_check=True).then_inc(mm_done, 1)
                    if g in TURN and ahead >= TURN[g][0]:
                        turns(b + TURN[g][0], (u + TURN[g][0]) % 2, TURN[g][1])
                    if not ahead:
                        continue
                    if g == T_SCORES:
                        turn_scores(b + 1)
                    if g == T_ENDS:
                        turn_ends(b + 1)
                    if g == T_ENTER:
                        turn_entering(b + 1)
                    if g == T_WEIGHTS:
                        turn_weights(b + 1)

            pe.sem_inc(mm_done, Y)
            turns(0, 0, "T0 T1 D0 T2 D1 T3 D2 T4 D3 T5 D4 T6 D5 T7 D6 D7")
            turn_scores(0)
            turn_ends(0)
            turn_entering(0)
            turn_weights(0)
            turns(1, 1, "T0 T1 D0 D1 T2 T3")
            with pe.Fori(0, NB // 2 - 1) as i:
                for u in range(2):
                    steps(i * 2 + u, u, 2)
            steps(NB - 2, 0, 1)
            steps(NB - 1, 1, 0)

        @block.scalar
        def _(act):
            def copy_turned(b, groups):
                for g in groups:
                    act.wait_ge(oht_ps, b * G4 + (g + 1))
                    if not isinstance(b, int) or b * G4 + g >= 2:
                        act.wait_ge(ed_done, b * G4 + (g - 1))
                    nc.scalar.copy(onehot_t[:, g % 2].rearrange("p q n -> p (q n)"), t_ps[:, g % 2, :]
                                   ).then_inc(oht_sb, 1)

            def weights_of(b, u):
                act.wait_ge(dl_ready, b + 1)
                nc.scalar.activation(g4[:], dl4[:], ACT.Exp).then_inc(g_done, 1)
                act.wait_ge(x_turned, b + 1)
                nc.scalar.activation(wt[:, u].rearrange("p h k -> p (h k)"), e_ps[:, 0:P], ACT.Exp
                                     ).then_inc(w_done, 1)

            copy_turned(0, range(G4))
            weights_of(0, 0)
            copy_turned(1, range(4))
            with act.Fori(0, NB // 2 - 1) as i:
                for u in range(2):
                    b = i * 2 + u
                    copy_turned(b + 1, range(4, G4))
                    copy_turned(b + 2, range(2))
                    weights_of(b + 1, 1 - u)
                    copy_turned(b + 2, range(2, 4))
            copy_turned(NB - 1, range(4, G4))
            weights_of(NB - 1, 1)

        @block.vector
        def _(dve):
            v = nc.vector
            PER = 14

            def reset(o, b):
                return K[("reset_fwd", "reset_bwd")[o]][:, bass.ds(b, 1), :].rearrange("p a i -> p (a i)")

            def build_onehots(b, u, g):
                loc = K["loc_dst"][:, bass.ds(b * SB + g * 8, 8)]
                v.tensor_tensor(onehot[:, u, g * 8:(g + 1) * 8, :],
                                loc.unsqueeze(2).broadcast_to([P, 8, P]),
                                K["iota_row"][:].unsqueeze(1).broadcast_to([P, 8, P]),
                                ALU.is_equal).then_inc(oh_built, 1)

            def scores(b, u, link, gathered):
                link(v.tensor_copy(whole_now[:], K["whole"][:, :, bass.ds(b, 1)].rearrange("p o b -> p (o b)")))
                dve.wait_ge(ed_done, b * G4 + G4)
                dve.wait_ge(gath[u], gathered)
                es = rows[:, u, :, HEADS * HB:ROW].rearrange("p k h -> p h k")
                link(v.tensor_tensor(sc2[:], ed_ps[:, 0:P].rearrange("p (k h) -> p h k", h=HEADS), es, ALU.add))
                link(v.scalar_tensor_tensor(out=sc[:], in0=sc2[:], scalar=SLOPE, in1=sc2[:], op0=ALU.mult,
                                            op1=ALU.max))
                link(v.tensor_scalar(sc2[:], sc[:], 0.0, NEG, ALU.is_equal, ALU.mult))
                v.tensor_tensor(sc[:], sc[:], sc2[:], ALU.add).then_inc(sc_ready, 1)

            def maxima(b):
                dve.wait_ge(sc_turned, b + 1)
                v.tensor_tensor_scan(fwd[:], reset(0, b), e_ps[:, 0:P], -BIG, ALU.add, ALU.max
                                     ).then_inc(ends_ready, 1)
                v.tensor_tensor_scan(bwd[:, ::-1], reset(1, b), e_ps[:, 0:P][:, ::-1],
                                     -BIG, ALU.add, ALU.max).then_inc(ends_ready, 1)

            def chains(b, link):
                dve.wait_ge(ends_turned, b + 1)
                for o in range(2):
                    link(v.tensor_copy(
                        ends[0:1, o].rearrange("a x (h k) -> a (x h) k", h=HEADS)[:, :, 1 - o:1 - o + SB],
                        small[0:1, 2 * o * P:(2 * o + 2) * P].rearrange("a (x k) -> a x k", k=SB)))
                v.tensor_tensor_scan(chain[0:1, 0], ends[0:1, 0, 1], ends[0:1, 0, 0], -BIG, ALU.add, ALU.max
                                     ).then_inc(chain_ready, 1)
                v.tensor_tensor_scan(chain[0:1, 1, ::-1], ends[0:1, 1, 1, ::-1], ends[0:1, 1, 0, ::-1], -BIG,
                                     ALU.add, ALU.max).then_inc(chain_ready, 1)
                dve.wait_ge(chain_ready, b * 2 + 2)
                for o in range(2):
                    v.tensor_copy(heads(enter[0:1, o]), heads(chain[0:1, o])[:, :, o:o + SB]
                                  ).then_inc(enter_ready, 1)
                carry = heads(ends[0:1, 0, 0])[:, :, 0]
                link(v.tensor_tensor(mx4[:], carry, heads(chain[0:1, 1])[:, :, 0], ALU.max))
                link(v.tensor_tensor(dl4[:], carry, mx4[:], ALU.subtract))
                v.tensor_scalar(dl4[:], dl4[:], K["goes_on"][:, bass.ds(b, 1)], None, ALU.mult
                                ).then_inc(dl_ready, 1)
                link(v.tensor_copy(carry, heads(chain[0:1, 0])[:, :, SB]))

            def exponents(b, link):
                dve.wait_ge(init_done, b + 1)
                link(v.tensor_copy(init[:], small[:, 0:2]))
                v.tensor_tensor_scan(fwd[:], reset(0, b), e_ps[:, 0:P], init[:, 0:1], ALU.add, ALU.max
                                     ).then_inc(dch, 1)
                link.n += 1
                link(v.tensor_tensor_scan(bwd[:, ::-1], reset(1, b), e_ps[:, 0:P][:, ::-1], init[:, 1:2], ALU.add,
                                          ALU.max))
                dve.wait_ge(g_done, b + 1)
                v.tensor_scalar(g4[:], g4[:], 1.0, None, ALU.subtract).then_inc(gm_ready, 1)
                link(v.tensor_tensor(top, fwd[:], bwd[:], ALU.max))
                v.tensor_tensor(top, e_ps[:, 0:P], top, ALU.subtract).then_inc(x_ready, 1)

            def first_scale(b, link):
                dve.wait_ge(gm_bc, b + 1)
                link(v.tensor_scalar(node_scale[:], small[:, 0:HEADS], K["first_node"][:, bass.ds(b, 1)], 1.0,
                                     ALU.mult, ALU.add))

            def move_last(b, u, node, linked):
                dve.wait_ge(mm_done, b * SB + Y)
                flat = K["acc"][:, bass.ds(node, 1), :].rearrange("p a f -> p (a f)")
                v.tensor_tensor(flat, out_ps[:, u, 0:HEADS * HB], flat, ALU.add).then_inc(dmain, 1)
                dve.wait_ge(dmain, linked)

            def load_nodes(at, n):
                return nc.values_load_multi_w_load_instructions(
                    K["step_node"][0:1, bass.ds(at, n)], engines=DVE_ONLY, min_val=0, max_val=NT - 1,
                    skip_runtime_bounds_check_because=WHY_IN_RANGE)[1]

            def weigh(b, u, g):
                dve.wait_ge(mm_done, b * SB + (g + 1) * YG)
                ks = slice(g * YG, (g + 1) * YG)
                v.tensor_tensor(y[:, g % 2].rearrange("p s (h f) -> p s h f", h=HEADS),
                                rows[:, u, ks, 0:HEADS * HB].rearrange("p s (h f) -> p s h f", h=HEADS),
                                wt[:, u, :, ks].rearrange("p h s -> p s h").unsqueeze(3)
                                .broadcast_to([P, YG, HEADS, HB]), ALU.mult).then_inc(y_ready, 1)
                if g % 2 and g > 2:
                    dve.sem_inc(rows_free, 1)

            def move_changed(b, u, nodes, at, first, last):
                for j in range(first, last):
                    with dve.If(nodes[j - at] == nodes[j + 1 - at]):
                        dve.sem_inc(sums_ok, 1)
                    with dve.Else():
                        dve.wait_ge(mm_done, b * SB + (j + 1 + Y))
                        flat = K["acc"][:, bass.ds(nodes[j - at], 1), :].rearrange("p a f -> p (a f)")
                        v.tensor_tensor(flat, out_ps[:, u, 0:HEADS * HB], flat, ALU.add)
                        dve.drain()
                        v.memset(out_ps[:, u, 0:HEADS * HB], 0.0)
                        dve.drain().then_inc(sums_ok, 1)

            def settle(b, u, g, nodes, at):
                first, last = g * YG - 1, (g + 1) * YG - 1
                with dve.If(nodes[first - at] == nodes[last - at]):
                    dve.sem_inc(sums_ok, last - first)
                with dve.Else():
                    move_changed(b, u, nodes, at, first, last)

            def steps(b, u, ahead, gathered):
                link = Chain(dve, dch, b * PER + (PER + 1))
                nodes, at = load_nodes(b * SB, 9), -1
                with dve.If(nodes[1] == nodes[YG]):
                    dve.sem_inc(sums_ok, YG)
                move_last(b, 1 - u, nodes[0], b * 2 + 1)
                sums = K["acc"][:, bass.ds(nodes[1], 1), :].rearrange("p a (h f) -> p (a h) f", h=HEADS)
                v.tensor_tensor(sums, sums, node_scale[:].unsqueeze(2).broadcast_to([P, HEADS, HB]), ALU.mult
                                ).then_inc(dmain, 1)
                dve.wait_ge(dmain, b * 2 + 2)
                dve.sem_inc(rows_free, 1)
                with dve.If(nodes[1] != nodes[YG]):
                    dve.sem_inc(sums_ok, 1)
                    move_changed(b, u, nodes, at, 0, YG - 1)
                for g in range(GROUPS):
                    if g + 1 < GROUPS:
                        weigh(b, u, g + 1)
                        if g % 2:
                            at = (g + 1) * YG - 1
                            nodes = load_nodes(b * SB + (at + 1), 9)
                        settle(b, u, g + 1, nodes, at)
                    if ahead and g == FIRST:
                        first_scale(b + 1, link)
                        dve.wait_ge(w_done, b + 2)
                        weigh(b + 1, 1 - u, 0)
                    if g in BUILD and ahead >= BUILD[g][0]:
                        build_onehots(b + BUILD[g][0], (u + BUILD[g][0]) % 2, BUILD[g][1])
                    if not ahead:
                        continue
                    if g == SCORES:
                        scores(b + 1, 1 - u, link, gathered)
                    if g == MAXIMA:
                        maxima(b + 1)
                    if g == CHAINS:
                        chains(b + 1, link)
                    if g == ENTER:
                        exponents(b + 1, link)
                    dve.sem_inc(stage_over, 1)
                assert not ahead or link.n == PER

            link = Chain(dve, dch)
            link(v.memset(ends[:], -BIG))
            v.memset(out_ps[:, 1, :], 0.0).then_inc(prepared, 1)
            v.memset(K["step_node"][0:1, 0:1], 0).then_inc(prepared, 1)
            dve.wait_ge(prepared, 2)
            for g in range(S8):
                build_onehots(0, 0, g)
            link = Chain(dve, dch, 1)
            scores(0, 0, link, 16 * SB)
            maxima(0)
            chains(0, link)
            exponents(0, link)
            first_scale(0, link)
            dve.wait_ge(w_done, 1)
            weigh(0, 0, 0)
            for g in range(3):
                build_onehots(1, 1, g)
            with dve.Fori(0, NB // 2 - 1) as i:
                for u in range(2):
                    steps(i * 2 + u, u, 2, i * (16 * SB) + 16 * SB * (u + 1))
            steps(NB - 2, 0, 1, 16 * SB * (NB // 2))
            steps(NB - 1, 1, 0, None)
            move_last(NB, 1, load_nodes(NB * SB, 1)[0], NB * 2 + 1)


def token_phase(nc, K, M, dram, x, gamma, beta, Wr, br, W1, b1, W2, b2, out):
    CHUNKS = 10
    TC = NT // CHUNKS
    NR = NT * E
    KT = TOPK * NT
    acc = K["acc"]
    with ExitStack() as ctx:
        m = Mem(nc, ctx)
        xin = m.sb("x_chunk", [P, 2, TC, D])
        stats, mean, rstd, tmp = (m.sb("stats2", [P, NT, 6]), m.sb("mean2", [P, NT]), m.sb("rstd2", [P, NT]),
                                  m.sb("ln_tmp2", [P, NT]))
        den, den2 = m.sb("den", [P, NT, HEADS]), m.sb("den2", [P, NT, HEADS])
        att, shift = m.sb("att_out", [P, 2, TC, D]), m.sb("ln_shift", [P, NT])
        gam, bet, br_b = m.sb("gamma_b", [P, D]), m.sb("beta_b", [P, D]), m.sb("br_b", [P, E])
        wr = m.sb("wr", [P, 2, E])
        xT = m.sb("xT2", [P, 2, TC, 2 * P])
        lg, lg2 = m.sb("logits", [P, NT, E]), m.sb("logits2", [P, NT, E])
        iota_e, valid = m.sb("iota_expert", [P, E]), m.sb("valid", [P, NT])
        tok_f = m.sb("token_f", [P, NT])
        best, which = m.sb("best", [P, TOPK, NT]), m.sb("which", [P, TOPK, NT])
        oh, cand = m.sb("expert_oh", [P, TOPK, NT, E]), m.sb("cand", [P, NT, E])
        tot, running = m.sb("tot", [P, E, KT]), m.sb("running", [P, 2, E, KT])
        inc, keep = running[:, 0], running[:, 1]
        jt, gt = m.sb("jt", [P, ST_]), m.sb("gt", [P, E, ST_])
        ntl, ctl, base = m.sb("ntiles", [P, E]), m.sb("cum_tiles", [P, E]), m.sb("slot_base", [P, E])
        rank = m.sb("rank", [P, TOPK, NT, E])
        pos, pos_i = m.sb("pos", [P, TOPK, NT]), m.sb("pos_i", [P, TOPK, NT], I32)
        wgt = m.sb("wgt", [P, TOPK, NT])
        hi, lo, w_of = m.sb("slot_hi", [P, NT, TOPK]), m.sb("slot_lo", [P, NT, TOPK]), m.sb("w_of", [P, NT, TOPK])
        id1, pad1, free = m.sb("token_plus_1", [P, NT, TOPK]), m.sb("pad_plus_1", [P, 1]), m.sb("free_slot", [P, STX])
        before = m.sb("before", [P, P])
        exp_f = att[0:1].rearrange("a u t d -> a (u t d)")[:, 0:STX * E].rearrange("a (t e) -> a t e", e=E)
        jrow = m.sb("tile_row", [P, STX])
        exp_s = m.sb("tile_expert_s", [1, STX])
        QC = TC * TOPK
        tile_is = running[:].rearrange("p a e s -> p (a e s)")[:, 0:QC * STX].rearrange("p (q s) -> p q s", q=QC)
        place = [att[:, u].rearrange("p t (a n) -> p (t a) n", n=P) for u in range(2)]
        in_tile = [flat[:, 0:QC * 2 * STX].rearrange("p (q s) -> p q s", q=QC)
                   for flat in (xin[:].rearrange("p u t d -> p (u t d)"), xT[:].rearrange("p u t n -> p (u t n)"))]
        t_ps, l_ps, r_ps = m.ps("t2_ps", [P, 2, 512]), m.ps("l_ps", [P, 2, 512]), m.ps("r_ps", [P, 4, 512])

        small_in, w_in, x_in, x_used = m.sem("small_in"), M["weights_in"], m.sems("x2_in", 2), m.sem("x_used")
        dch, x1_done, x1_out, made = m.sem("dve_t"), m.sem("x1_done"), m.sem("x1_out"), m.sem("made")
        st_done, var_ready, std_ready, ach = m.sem("st_done"), m.sem("var2"), m.sem("std2"), m.sem("att_ch")
        xn_out, xt_done, xt_cp = m.sems("xn2_out", 2), m.sem("xt2_done"), m.sem("xt2_cp")
        l_done, l_free, ex_in, ex_out = m.sem("l_done"), m.sem("l_free"), m.sem("ex_in"), m.sem("ex_out")
        oh_done, r_done, tile_oh = m.sem("oh_done"), m.sem("r_done"), m.sem("tile_one_hots")
        ids_built, w_built, sel_used = m.sem("ids_built"), m.sem("w_built"), m.sem("sel_used")
        ln_ready, ln1_done, ln2_done = m.sem("ln_ready"), m.sem("ln1_done"), m.sem("ln2_done")
        gb, norm_c = m.sem("gb"), m.sem("norm_c")
        block = ctx.enter_context(nc.Block())

        TWOS = -(-TC // 2)

        def tile(t):
            return acc[:, bass.ds(t, 1), 0:D].rearrange("p a f -> p (a f)")

        def twos(m):
            return range(2 * m, min(2 * m + 2, TC))

        @block.sync
        def _(sp):
            for u in range(2):
                sp.dma_start(xin[:, u], x[u * TC * P:(u + 1) * TC * P, :].rearrange("(t p) d -> p t d", p=P)
                             ).then_inc(x_in[u], 16)
            for o, a in ((gam, gamma), (bet, beta), (br_b, br)):
                sp.dma_start(o[:], a.rearrange("(o d) -> o d", o=1).broadcast_to([P, a.shape[0]])
                             ).then_inc(small_in, 16)
            sp.dma_start(wr[:], Wr.rearrange("(k p) e -> p k e", p=P)).then_inc(small_in, 16)
            def store_x1(c):
                sp.dma_start(out[c * TC * P:(c + 1) * TC * P, :].rearrange("(t p) d -> p t d", p=P),
                             acc[:, c * TC:(c + 1) * TC, 0:D]).then_inc(x1_out, 16)

            for c in range(2, CHUNKS):
                sp.wait_ge(x_used, c - 1)
                sp.dma_start(xin[:, c % 2], x[c * TC * P:(c + 1) * TC * P, :].rearrange("(t p) d -> p t d", p=P)
                             ).then_inc(x_in[c % 2], 16)
                store_x1(c - 2)
            for c in range(CHUNKS - 2, CHUNKS):
                sp.wait_ge(x_used, c + 1)
                store_x1(c)
            with sp.Fori(0, CHUNKS // 2) as i:
                for u in range(2):
                    sp.wait_ge(norm_c, i * 2 + (u + 1))
                    sp.dma_start(dram["xn"][bass.ds((i * 2 + u) * (TC * P), TC * P), :]
                                 .rearrange("(t p) d -> p t d", p=P), xin[:, u]).then_inc(xn_out[u], 16)
            for u in range(2):
                sp.wait_ge(xn_out[u], 16 * (CHUNKS // 2))
            sp.wait_ge(x1_out, 16 * CHUNKS)

        @block.gpsimd
        def _(pool):
            g = nc.gpsimd
            link = Chain(pool, gb)
            kw = dict(allow_small_or_imprecise_dtypes=True)
            link(g.iota(iota_e[:], pattern=[[1, E]], base=0, channel_multiplier=0, **kw))
            link(g.iota(tok_f[:], pattern=[[P, NT]], base=0, channel_multiplier=1, **kw))
            link(g.iota(jt[:], pattern=[[P, ST_]], base=0, channel_multiplier=0, **kw))
            link(g.iota(jrow[:], pattern=[[1, STX]], base=0, channel_multiplier=0, **kw))
            link(g.memset(keep, 1.0))
            link(g.memset(keep[:, :, 0:1], 0.0))
            link(g.affine_select(out=before[:], in_=K["ones"][:], compare_op=ALU.is_gt, fill=0.0, base=0,
                                 pattern=[[1, P]], channel_multiplier=-1))
            pool.sem_inc(made, 1)

        @block.tensor
        def _(pe):
            pe.wait_ge(small_in, 64)
            with pe.Fori(0, CHUNKS // 2) as i:
                for u in range(2):
                    c = i * 2 + u
                    pe.wait_ge(norm_c, c + 1)
                    for n in range(TWOS):
                        pe.wait_ge(xt_cp, c * TWOS + (n + 1))
                        for q, t in enumerate(twos(n)):
                            for k in range(2):
                                mm = nc.tensor.transpose(
                                    t_ps[:, (u * TWOS + n) % 2, (2 * q + k) * P:(2 * q + k + 1) * P],
                                    xin[:, u, t, k * P:(k + 1) * P], K["ident"][:])
                        mm.then_inc(xt_done, 1)
                    pe.wait_ge(xt_cp, c * TWOS + (TWOS + 2))
                    pe.wait_ge(l_free, c + 1)
                    for t in range(TC):
                        for k in range(2):
                            mm = nc.tensor.matmul(l_ps[:, u, t * E:(t + 1) * E], xT[:, u, t, k * P:(k + 1) * P],
                                                  wr[:, k, :], start=(k == 0), stop=(k == 1))
                    mm.then_inc(l_done, 1)
            pe.wait_ge(oh_done, 1)
            pe.wait_ge(made, 1)
            for k in range(TOPK):
                rhs = oh[:, k].rearrange("p t e -> p (t e)")
                nc.tensor.matmul(r_ps[:, k, 0:NR], before[:], rhs, start=True, stop=True)
                mm = nc.tensor.matmul(r_ps[:, 2 + k, 0:NR], K["ones"][:], rhs, start=True, stop=True)
            mm.then_inc(r_done, 1)

            def slot_tables(i, start):
                for u in range(2):
                    pe.wait_ge(ids_built, i * 2 + (u + 1))
                    pe.wait_ge(w_built, i * 2 + (u + 1))
                    for q in range(QC):
                        mm = nc.tensor.matmul(l_ps[:, 0, 0:2 * STX], place[u][:, q, :], in_tile[u][:, q, :],
                                              start=(start and u == 0 and q == 0), stop=True, skip_group_check=True)
                    mm.then_inc(sel_used, 1)

            slot_tables(0, True)
            with pe.Fori(1, CHUNKS // 2) as i:
                slot_tables(i, False)

        @block.scalar
        def _(act):
            act.sem_inc(xt_cp, 2)
            for n in range(2):
                act.wait_ge(var_ready, n + 1)
                nc.scalar.activation(rstd[:], rstd[:], ACT.Sqrt, bias=K["eps"][:, 0:1]).then_inc(std_ready, 1)
                act.wait_ge(ln_ready, n + 1)
                if n == 0:
                    act.wait_ge(x1_out, 16 * CHUNKS)
                    for k in range(2):
                        act.dma_start(M["w1"][:, k].rearrange("p (e h) -> p e h", e=E),
                                      W1[:, k * P:(k + 1) * P, :].rearrange("e p h -> p e h")).then_inc(w_in, 16)
                    for k in range(4):
                        act.dma_start(M["w2"][:, k].rearrange("p (e h) -> p e h", e=E),
                                      W2[:, k * P:(k + 1) * P, :].rearrange("e p h -> p e h")).then_inc(w_in, 16)
                    act.dma_start(M["b1"][:], b1.rearrange("(o e) h -> o (e h)", o=1).broadcast_to([P, E * HID])
                                  ).then_inc(w_in, 16)
                    act.dma_start(M["b2"][:], b2.rearrange("(o e) h -> o (e h)", o=1).broadcast_to([P, E * D])
                                  ).then_inc(w_in, 16)
                    with act.Fori(0, CHUNKS) as c:
                        for q in range(TC):
                            t = c * TC + q
                            nc.scalar.activation(tile(t), tile(t), ACT.Identity, bias=shift[:, bass.ds(t, 1)],
                                                 scale=rstd[:, bass.ds(t, 1)]).then_inc(ln1_done, 1)

            def normalise(c, u):
                act.wait_ge(ach, c + (CHUNKS - 1))
                for q in range(TC):
                    t = c * TC + q
                    nc.scalar.activation(att[:, u, q], tile(t), ACT.Identity, bias=shift[:, bass.ds(t, 1)],
                                         scale=rstd[:, bass.ds(t, 1)]).then_inc(ln2_done, 1)

            def copy_turned(c, u):
                act.wait_ge(l_free, c + 1)
                for n in range(TWOS):
                    act.wait_ge(xt_done, c * TWOS + (n + 1))
                    ts = twos(n)
                    nc.scalar.copy(xT[:, u, ts[0]:ts[-1] + 1].rearrange("p t n -> p (t n)"),
                                   t_ps[:, (u * TWOS + n) % 2, 0:len(ts) * 2 * P]).then_inc(xt_cp, 1)

            normalise(0, 0)
            normalise(1, 1)
            copy_turned(0, 0)
            with act.Fori(1, CHUNKS // 2) as i:
                normalise(i * 2, 0)
                copy_turned(i * 2 - 1, 1)
                normalise(i * 2 + 1, 1)
                copy_turned(i * 2, 0)
            copy_turned(CHUNKS - 1, 1)
            act.wait_ge(ex_in, 1)
            nc.scalar.activation(wgt[:, 1, :], wgt[:, 1, :], ACT.Exp).then_inc(ex_out, 1)

            def weights_in_tile(i):
                for u in range(2):
                    act.wait_ge(tile_oh, i * 2 + (u + 1))
                    if not isinstance(i, int):
                        act.wait_ge(sel_used, i * 2 + (u - 1))
                    for t in range(TC):
                        for k in range(TOPK):
                            at = i * (2 * TC) + (u * TC + t)
                            ins = nc.scalar.activation(in_tile[u][:, t * TOPK + k, STX:2 * STX],
                                                       tile_is[:, t * TOPK + k, :], ACT.Identity,
                                                       bias=K["zero"][:, 0:1], scale=w_of[:, bass.ds(at, 1), k])
                    ins.then_inc(w_built, 1)

            weights_in_tile(0)
            with act.Fori(1, CHUNKS // 2) as i:
                weights_in_tile(i)
            act.wait_ge(w_in, 16 * 8)

        @block.vector
        def _(dve):
            v = nc.vector
            link = Chain(dve, dch)
            dve.sem_inc(l_free, 2)
            d_in = acc[:].rearrange("p t (h f) -> p t h f", h=HEADS)[:, :, :, HD]
            link(v.tensor_scalar(den2[:], d_in, 0.0, None, ALU.is_le))
            link(v.tensor_tensor(den[:], d_in, den2[:], ALU.add))
            link(v.reciprocal(den[:], den[:]))
            def stats_of(t):
                v.bn_stats(stats[:, bass.ds(t, 1), :].rearrange("p a c -> p (a c)"), tile(t)).then_inc(st_done, 1)

            def rows_of(c):
                return acc[:, bass.ds(c * TC, TC)]

            def layer_norm(n):
                dve.wait_ge(st_done, n * NT)
                mean_and_rstd(nc, dve, link, stats[:], mean[:], rstd[:], tmp[:], var_ready, std_ready, n)
                v.scalar_tensor_tensor(out=shift[:], in0=mean[:], scalar=-1.0, in1=rstd[:], op0=ALU.mult, op1=ALU.mult
                                       ).then_inc(ln_ready, 1)

            with dve.Fori(0, CHUNKS // 2) as i:
                for u in range(2):
                    c = i * 2 + u
                    v.tensor_tensor(att[:, u].rearrange("p t (h f) -> p (t h) f", h=HEADS),
                                    rows_of(c).rearrange("p t (h f) -> p (t h) f", h=HEADS)[:, :, 0:HD],
                                    den[:, bass.ds(c * TC, TC), :].rearrange("p t h -> p (t h)").unsqueeze(2)
                                    .broadcast_to([P, TC * HEADS, HD]), ALU.mult).then_inc(ach, 1)
                    dve.wait_ge(ach, c + 1)
                    dve.wait_ge(x_in[u], i * 16 + 16)
                    v.tensor_tensor(rows_of(c)[:, :, 0:D], att[:, u], xin[:, u], ALU.add).then_inc(x_used, 1)
                    dve.wait_ge(x_used, c + 1)
                    for q in range(TC):
                        stats_of(c * TC + q)
            layer_norm(1)
            with dve.Fori(0, CHUNKS) as c:
                for q in range(TC):
                    dve.wait_ge(ln1_done, c * TC + (q + 1))
                    stats_of(c * TC + q)
            layer_norm(2)
            dve.wait_ge(small_in, 64)

            def scale_and_shift(c, u):
                dve.wait_ge(ln2_done, c * TC + TC)
                if not isinstance(c, int):
                    dve.wait_ge(xt_done, (c - 1) * TWOS)
                    dve.wait_ge(xn_out[u], (c - u) * 8)
                v.tensor_tensor(xin[:, u], att[:, u], gam[:].unsqueeze(1).broadcast_to([P, TC, D]), ALU.mult
                                ).then_inc(ach, 1)
                dve.wait_ge(ach, c + (CHUNKS + 1))
                v.tensor_tensor(xin[:, u], xin[:, u], bet[:].unsqueeze(1).broadcast_to([P, TC, D]), ALU.add
                                ).then_inc(norm_c, 1)

            def take_logits(c, u):
                dve.wait_ge(l_done, c + 1)
                v.tensor_tensor(lg[:, bass.ds(c * TC, TC), :], l_ps[:, u, 0:TC * E].rearrange("p (t e) -> p t e", e=E),
                                br_b[:].unsqueeze(1).broadcast_to([P, TC, E]), ALU.add).then_inc(l_free, 1)

            scale_and_shift(0, 0)
            scale_and_shift(1, 1)
            with dve.Fori(1, CHUNKS // 2) as i:
                for u in range(2):
                    scale_and_shift(i * 2 + u, u)
                    take_logits(i * 2 + (u - 2), u)
            for u in range(2):
                take_logits(CHUNKS - 2 + u, u)
            dve.wait_ge(l_free, CHUNKS + 2)
            dve.wait_ge(made, 1)
            ie = iota_e[:].unsqueeze(1).broadcast_to([P, NT, E])
            link(v.tensor_scalar(valid[:], tok_f[:], float(N_NODES), None, ALU.is_lt))
            for k in range(TOPK):
                src_l = (lg, lg2)[k]
                bk, wk = best[:, k].unsqueeze(2), which[:, k].unsqueeze(2)
                link(v.tensor_reduce(best[:, k], src_l[:], AX_X, ALU.max))
                link(v.tensor_tensor(cand[:], src_l[:], bk.broadcast_to([P, NT, E]), ALU.is_equal))
                link(v.tensor_scalar(cand[:], cand[:], 1.0, -float(E), ALU.subtract, ALU.mult))
                link(v.tensor_tensor(cand[:], cand[:], ie, ALU.add))
                link(v.tensor_reduce(which[:, k], cand[:], AX_X, ALU.min))
                link(v.tensor_tensor(oh[:, k], ie, wk.broadcast_to([P, NT, E]), ALU.is_equal))
                if k == 0:
                    link(v.tensor_scalar(cand[:], oh[:, 0], -BIG, None, ALU.mult))
                    link(v.tensor_tensor(lg2[:], lg[:], cand[:], ALU.add))
                link(v.tensor_tensor(oh[:, k], oh[:, k], valid[:].unsqueeze(2).broadcast_to([P, NT, E]), ALU.mult))
            dve.sem_inc(oh_done, 1)
            v.tensor_tensor(wgt[:, 1, :], best[:, 1, :], best[:, 0, :], ALU.subtract).then_inc(ex_in, 1)
            dve.wait_ge(ex_out, 1)
            link(v.tensor_scalar(wgt[:, 0, :], wgt[:, 1, :], 1.0, None, ALU.add))
            link(v.reciprocal(wgt[:, 0, :], wgt[:, 0, :]))
            link(v.tensor_tensor(wgt[:, 1, :], wgt[:, 1, :], wgt[:, 0, :], ALU.mult))
            dve.wait_ge(r_done, 1)
            for k in range(TOPK):
                link(v.tensor_copy(tot[:, :, k * NT:(k + 1) * NT],
                                   r_ps[:, 2 + k, 0:NR].rearrange("p (t e) -> p e t", e=E)))
            fl = "p e s -> p (e s)"
            link(v.tensor_tensor_scan(inc.rearrange(fl), keep.rearrange(fl), tot[:].rearrange(fl), 0.0,
                                      ALU.mult, ALU.add))
            link(v.tensor_tensor(gt[:], inc[:, :, KT - 1:KT].broadcast_to([P, E, ST_]),
                                 jt[:].unsqueeze(1).broadcast_to([P, E, ST_]), ALU.is_gt))
            link(v.tensor_reduce(ntl[:], gt[:], AX_X, ALU.add))
            link(v.tensor_tensor_scan(ctl[:], K["ones"][:, 0:E], ntl[:], 0.0, ALU.mult, ALU.add))
            link(v.tensor_tensor(base[:], ctl[:], ntl[:], ALU.subtract))
            link(v.tensor_scalar(base[:], base[:], float(P), None, ALU.mult))
            link(v.tensor_tensor(inc, inc, tot[:], ALU.subtract))
            link(v.tensor_tensor(inc, inc, base[:].unsqueeze(2).broadcast_to([P, E, KT]), ALU.add))
            for k in range(TOPK):
                link(v.tensor_tensor(rank[:, k], r_ps[:, k, 0:NR].rearrange("p (t e) -> p t e", e=E),
                                     inc[:, :, k * NT:(k + 1) * NT].rearrange("p e t -> p t e"), ALU.add))
            link(v.tensor_tensor(rank[:], rank[:], oh[:], ALU.mult))
            link(v.tensor_reduce(pos[:], rank[:], AX_X, ALU.add))
            link(v.tensor_tensor(exp_f, ctl[0:1].unsqueeze(1).broadcast_to([1, STX, E]),
                                 jrow[0:1].unsqueeze(2).broadcast_to([1, STX, E]), ALU.is_le))
            link(v.tensor_reduce(exp_s[:], exp_f, AX_X, ALU.add))
            link(v.tensor_scalar(M["tile_expert"][:], exp_s[:], float(E - 1), None, ALU.min))
            link(v.tensor_scalar(tmp[:], valid[:], 0.0, float(STX * P), ALU.is_equal, ALU.mult))
            link(v.tensor_tensor(pos[:], pos[:], tmp[:].unsqueeze(1).broadcast_to([P, TOPK, NT]), ALU.add))
            link(v.tensor_copy(pos_i[:], pos[:]))
            link(v.tensor_scalar(pos_i[:], pos_i[:], 7, None, ALU.arith_shift_right))
            link(v.tensor_copy(hi[:].rearrange("p t k -> p k t"), pos_i[:]))
            link(v.scalar_tensor_tensor(out=lo[:].rearrange("p t k -> p k t"), in0=hi[:].rearrange("p t k -> p k t"),
                                        scalar=-float(P), in1=pos[:], op0=ALU.mult, op1=ALU.add))
            link(v.tensor_copy(w_of[:].rearrange("p t k -> p k t"), wgt[:]))
            link(v.tensor_scalar(id1[:], tok_f[:].unsqueeze(2).broadcast_to([P, NT, TOPK]), 1.0, None, ALU.add))
            link(v.tensor_scalar(pad1[:], K["iota_col"][:, 0:1], float(PAD_ROW + 1), None, ALU.add))
            for u in range(2):
                dve.wait_ge(xn_out[u], 16 * (CHUNKS // 2))

            def tokens_in_tile(i):
                for u in range(2):
                    if not isinstance(i, int):
                        dve.wait_ge(sel_used, i * 2 + (u - 1))
                    at = i * (2 * TC) + u * TC

                    def each(a, width):
                        return a.unsqueeze(2).broadcast_to([P, QC, width])

                    v.tensor_tensor(place[u], each(lo[:, bass.ds(at, TC), :].rearrange("p t k -> p (t k)"), P),
                                    K["iota_row"][:].unsqueeze(1).broadcast_to([P, QC, P]), ALU.is_equal)
                    if u or not isinstance(i, int):
                        dve.wait_ge(ids_built, i * 2 + u)
                        dve.wait_ge(w_built, i * 2 + u)
                    v.tensor_tensor(tile_is, each(hi[:, bass.ds(at, TC), :].rearrange("p t k -> p (t k)"), STX),
                                    jrow[:].unsqueeze(1).broadcast_to([P, QC, STX]), ALU.is_equal
                                    ).then_inc(tile_oh, 1)
                    dve.wait_ge(tile_oh, i * 2 + (u + 1))
                    v.tensor_tensor(in_tile[u][:, :, 0:STX], tile_is,
                                    each(id1[:, bass.ds(at, TC), :].rearrange("p t k -> p (t k)"), STX), ALU.mult
                                    ).then_inc(ids_built, 1)

            tokens_in_tile(0)
            with dve.Fori(1, CHUNKS // 2) as i:
                tokens_in_tile(i)
            dve.wait_ge(sel_used, CHUNKS)
            link(v.tensor_scalar(free[:], l_ps[:, 0, 0:STX], 0.0, pad1[:, 0:1], ALU.is_equal, ALU.mult))
            link(v.scalar_tensor_tensor(out=free[:], in0=l_ps[:, 0, 0:STX], scalar=-1.0, in1=free[:], op0=ALU.add,
                                        op1=ALU.add))
            link(v.tensor_copy(M["slot_token"][:], free[:]))
            link(v.tensor_copy(M["slot_weight"][:], l_ps[:, 0, STX:2 * STX]))


def expert_phase(nc, K, M, dram, out):
    tok, wgt = M["slot_token"], M["slot_weight"]
    with ExitStack() as ctx:
        m = Mem(nc, ctx)
        g_idx, s_idx = m.sb("gather_idx", [P, XB], I32), m.sb("scatter_idx", [P, XB], I32)
        xg, xT = m.sb("xg", [P, XB, D]), m.sb("xgT", [P, 2, 2, P])
        hb, hg, hT = m.sb("h_biased", [P, 2, HID]), m.sb("h_gelu", [P, 2, HID]), m.sb("hT", [P, 2, 4, P])
        ysb = m.sb("y_out", [P, XB, D])
        x_ps, h_ps, t_ps, y_ps = (m.ps("x_ps", [P, 1, 512]), m.ps("h_ps", [P, 2, 512]), m.ps("ht_ps", [P, 2, 512]),
                                  m.ps("y_ps", [P, 2, 512]))
        ic, gath, scat = m.sem("idx_c"), m.sems("xg_in", XB), m.sem("y_added")
        xt_done, xt_cp, h_done, hb_done, hg_done = (m.sem("xt3"), m.sem("xt3_cp"), m.sem("h_done"),
                                                    m.sem("hb_done"), m.sem("hg_done"))
        ht_done, ht_cp, y_done, yb_done, ysb_done, y_ps_free = (m.sem("ht_done"), m.sem("ht_cp"), m.sem("y_done"),
                                                                m.sem("yb_done"), m.sem("ysb_done"), m.sem("y_ps_free"))
        y_free, issuing = m.sem("y_free"), m.sem("indirect_issuing")
        block = ctx.enter_context(nc.Block())

        @block.gpsimd
        def _(pool):
            g = nc.gpsimd

            def gather(t, u, n):
                g.tensor_copy(g_idx[:, u:u + 1], tok[:, bass.ds(t, 1)]).then_inc(ic, 1)
                pool.wait_ge(ic, n + 1)
                pool.sem_inc(issuing, 1)
                g.indirect_dma_start(out=xg[:, u], out_offset=None, in_=dram["xn"],
                                     in_offset=bass.IndirectOffsetOnAxis(ap=g_idx[:, u:u + 1], axis=0)
                                     ).then_inc(gath[u], 16)

            for u in range(XB):
                gather(u, u, u)

            def tiles(i):
                for u in range(XB):
                    pool.wait_ge(xt_done, i * XB + (u + 1))
                    gather(i * XB + (u + XB), u, i * (2 * XB) + (2 * u + XB))
                    pool.wait_ge(ysb_done, i * XB + (u + 1))
                    if u or not isinstance(i, int):
                        pool.wait_ge(scat, i * (16 * XB) + 16 * u)
                    pool.sem_inc(y_free, 1)
                    g.tensor_copy(s_idx[:, u:u + 1], tok[:, bass.ds(i * XB + u, 1)]).then_inc(ic, 1)
                    pool.wait_ge(ic, i * (2 * XB) + (2 * u + XB + 2))
                    pool.sem_inc(issuing, 1)
                    g.indirect_dma_start(out=out, in_=ysb[:, u], in_offset=None, compute_op=ALU.add,
                                         out_offset=bass.IndirectOffsetOnAxis(ap=s_idx[:, u:u + 1], axis=0)
                                         ).then_inc(scat, 16)

            tiles(0)
            with pool.Fori(1, ST_ // XB) as i:
                tiles(i)
            pool.wait_ge(scat, 16 * ST_)
            for u in range(XB):
                pool.wait_ge(gath[u], 16 * (ST_ // XB + 1))

        @block.tensor
        def _(pe):
            ident = K["ident"][:]
            def turn_x(u, i, t):
                pe.wait_ge(gath[u], i * 16 + 16)
                if not isinstance(t, int) or t:
                    pe.wait_ge(xt_cp, t)
                for k in range(2):
                    mm = nc.tensor.transpose(x_ps[:, 0, k * P:(k + 1) * P], xg[:, u, k * P:(k + 1) * P], ident)
                mm.then_inc(xt_done, 1)

            def up(u, t, e):
                pe.wait_ge(xt_cp, t + 1)
                for k in range(2):
                    mm = nc.tensor.matmul(h_ps[:, u, :], xT[:, u, k, :],
                                          M["w1"][:, k, bass.ds(e * HID, HID)], start=(k == 0), stop=(k == 1))
                mm.then_inc(h_done, 1)

            def turn_h(u, t):
                pe.wait_ge(hg_done, t + 1)
                for k in range(4):
                    mm = nc.tensor.transpose(t_ps[:, u, k * P:(k + 1) * P], hg[:, u, k * P:(k + 1) * P], ident)
                mm.then_inc(ht_done, 1)

            def down(u, t, e):
                pe.wait_ge(ht_cp, t + 1)
                for k in range(4):
                    mm = nc.tensor.matmul(y_ps[:, u, 0:D], hT[:, u, k, :], M["w2"][:, k, bass.ds(e * D, D)],
                                          start=(k == 0), stop=(k == 3))
                mm.then_inc(y_done, 1)

            def experts(t, n):
                return nc.values_load_multi_w_load_instructions(
                    M["tile_expert"][0:1, bass.ds(t, n)], engines=PE_ONLY, min_val=0, max_val=E - 1,
                    skip_runtime_bounds_check_because=WHY_IN_RANGE)[1]

            turn_x(0, 0, 0)
            up(0, 0, experts(0, 1)[0])
            turn_x(1, 0, 1)
            with pe.Fori(0, ST_ // XB) as i:
                ex = experts(i * XB, XB + 1)
                for u in range(XB):
                    t = i * XB + u
                    h, n = u % 2, (u + 2) % XB
                    turn_h(h, t)
                    pe.wait_ge(hb_done, t + 1)
                    up(1 - h, t + 1, ex[u + 1])
                    turn_x(n, i + (u + 2) // XB, t + 2)
                    pe.wait_ge(y_ps_free, t + 1)
                    down(h, t, ex[u])

        @block.scalar
        def _(act):
            with act.Fori(0, ST_ // XB) as i:
                for u in range(XB):
                    act.wait_ge(hb_done, i * XB + (u + 2))
                    nc.scalar.activation(hg[:, u % 2], hb[:, u % 2], ACT.Gelu).then_inc(hg_done, 1)

        @block.vector
        def _(dve):
            v = nc.vector
            dve.sem_inc(y_free, XB - 1)
            dve.sem_inc(y_ps_free, 2)
            dve.sem_inc(hb_done, 1)
            dve.wait_ge(M["weights_in"], 16 * 8)

            def experts(t, n):
                return nc.values_load_multi_w_load_instructions(
                    M["tile_expert"][0:1, bass.ds(t, n)], engines=DVE_ONLY, min_val=0, max_val=E - 1,
                    skip_runtime_bounds_check_because=WHY_IN_RANGE)[1]

            def bias_h(u, t, e):
                dve.wait_ge(h_done, t + 1)
                v.tensor_tensor(hb[:, u], h_ps[:, u, :], M["b1"][:, bass.ds(e * HID, HID)], ALU.add
                                ).then_inc(hb_done, 1)

            def copy_x(u, t):
                dve.wait_ge(xt_done, t + 1)
                v.tensor_copy(xT[:, u].rearrange("p k n -> p (k n)"), x_ps[:, 0, 0:2 * P]).then_inc(xt_cp, 1)

            copy_x(0, 0)
            bias_h(0, 0, experts(0, 1)[0])
            copy_x(1, 1)
            with dve.Fori(0, ST_ // XB) as i:
                ex = experts(i * XB, XB + 1)
                for u in range(XB):
                    t = i * XB + u
                    h = u % 2
                    dve.wait_ge(ht_done, t + 1)
                    v.tensor_copy(hT[:, h].rearrange("p k n -> p (k n)"), t_ps[:, h, :]).then_inc(ht_cp, 1)
                    bias_h(1 - h, t + 1, ex[u + 1])
                    copy_x(h, t + 2)
                    dve.wait_ge(y_done, t + 1)
                    dve.wait_ge(y_free, t + 1)
                    v.tensor_tensor(ysb[:, u], y_ps[:, h, 0:D], M["b2"][:, bass.ds(ex[u] * D, D)], ALU.add
                                    ).then_inc(y_ps_free, 1)
                    dve.wait_ge(y_ps_free, t + 3)
                    v.tensor_scalar(ysb[:, u], ysb[:, u], wgt[:, bass.ds(t, 1)], None, ALU.mult).then_inc(ysb_done, 1)


def build(nc, x, edges, W, att, gamma, beta, Wr, br, W1, b1, W2, b2, out):
    def scratch(name, shape, dt):
        return nc.dram_tensor(name, shape, dt, kind="Internal").ap()

    dram = {
        "z_table": scratch("z_table", (NP, ROW), F32), "xn": scratch("xn_rows", (NP, D), F32),
        "step_node_tile": scratch("step_node_tile", (SP,), I32), "flags": scratch("step_flags", (2, SP, P), F32),
    }
    with ExitStack() as ctx:
        K = lasting(nc, ctx)
        constants_phase(nc, K)
        with ExitStack() as graph:
            K.update(graph_tables(nc, graph))
            step_table_phase(nc, K, dram, edges)
            chain_table_phase(nc, K)
            node_phase(nc, K, dram, x, W, att)
            edge_phase(nc, K, dram)
        M = expert_buffers(nc, ctx)
        token_phase(nc, K, M, dram, x, gamma, beta, Wr, br, W1, b1, W2, b2, out)
        expert_phase(nc, K, M, dram, out)


def kernel(x, src, dst, L0_gnn_W, L0_gnn_att, L0_ffn_gamma, L0_ffn_beta, L0_ffn_Wr, L0_ffn_br, L0_ffn_W1,
           L0_ffn_b1, L0_ffn_W2, L0_ffn_b2):
    import numpy as np
    import concourse.bacc as bacc
    from concourse.bass_utils import run_bass_kernel_spmd

    def padded(a, shape, fill):
        a = np.asarray(a)
        out = np.full(shape, fill, a.dtype)
        out[:a.shape[0]] = a
        return out

    dst = padded(dst, (ET * P,), PAD_DST).reshape(ET, P)
    edges = np.full((ET, EROW), -1, dst.dtype)
    edges[1:, 0] = dst[:-1, -1]
    edges[:, 1:P + 1] = dst
    edges[:-1, P + 1] = dst[1:, 0]
    edges[:, P + 2:] = padded(src, (ET * P,), 0).reshape(ET, P)
    arrays = {
        "x": padded(x, (NP, D), 0), "edges": edges, "W": L0_gnn_W, "att": L0_gnn_att,
        "gamma": L0_ffn_gamma, "beta": L0_ffn_beta, "Wr": L0_ffn_Wr, "br": L0_ffn_br, "W1": L0_ffn_W1,
        "b1": L0_ffn_b1, "W2": L0_ffn_W2, "b2": L0_ffn_b2,
    }
    arrays = {name: np.ascontiguousarray(a) for name, a in arrays.items()}
    nc = bacc.Bacc("TRN2", target_bir_lowering=False, num_devices=1)
    args = [nc.dram_tensor(name, a.shape, mybir.dt.from_np(a.dtype), kind="ExternalInput").ap()
            for name, a in arrays.items()]
    out = nc.dram_tensor("out", (NP, D), F32, kind="ExternalOutput").ap()
    build(nc, *args, out)
    r = run_bass_kernel_spmd(nc, [arrays], core_ids=[0])
    return r.results[0]["out"][:N_NODES]
```
